# Optimizing a Trainium2 kernel written in Bass

```python
import numpy as np
import jax
import jax.numpy as jnp

def _softmax(x, axis=-1):
    return jax.nn.softmax(x, axis=axis)

def _gelu(x):
    return jax.nn.gelu(x, approximate=True)

def _silu(x):
    return jax.nn.silu(x)

def _sigmoid(x):
    return jax.nn.sigmoid(x)

def _layernorm(x, axis=-1, eps=1e-05):
    m = jnp.mean(x, axis=axis, keepdims=True)
    v = jnp.var(x, axis=axis, keepdims=True)
    return (x - m) / jnp.sqrt(v + eps)

def _scatter_add(tgt, idx, src, axis=0):
    return tgt.at[idx].add(src)

def _segment_sum(src, seg, n):
    return jax.ops.segment_sum(src, seg, n)
kernel_name = 'mk_prb_d2_jaxref_r8_b3da35'

def setup_inputs(seed: int=0):
    np.random.seed(seed)
    _w = jnp.asarray

    def _L0_attn_setup():
        import jax, jax.numpy as jnp
        import numpy as np
        B, T, C = (2, 256, 128)
        H, L = (16, 36)
        D_HEAD = C // H
        key = jax.random.key(seed)
        ks = jax.random.split(key, 7)
        s = 0.02
        return {'x': jax.random.normal(ks[0], (B, T, C), dtype=jnp.float32), 'latent_w': jax.random.normal(ks[1], (C, L), dtype=jnp.float32) * s, 'latent_b': jax.random.normal(ks[2], (L,), dtype=jnp.float32) * s, 'Wd_w': jax.random.normal(ks[3], (H, C, L), dtype=jnp.float32) * s, 'Wd_b': jax.random.normal(ks[4], (H, L), dtype=jnp.float32) * s, 'out_w': jax.random.normal(ks[5], (H * L, C), dtype=jnp.float32) * s, 'out_b': jax.random.normal(ks[6], (C,), dtype=jnp.float32) * s}
    _L0_attn_in = _L0_attn_setup()

    def _L0_ffn_setup():
        import jax, jax.numpy as jnp
        import numpy as np
        H, E, DFF = (128, 8, 512)
        key = jax.random.key(seed)
        ks = jax.random.split(key, 7)
        s = lambda *shape: 1.0 / np.sqrt(shape[-2] if len(shape) > 1 else shape[-1])
        x = jax.random.normal(ks[0], (2, 256, H), dtype=jnp.float32)
        Wr = jax.random.normal(ks[1], (H, E), dtype=jnp.float32) * (1.0 / np.sqrt(H))
        br = jnp.zeros((E,), dtype=jnp.float32)
        W1 = jax.random.normal(ks[2], (E, H, DFF), dtype=jnp.float32) * (1.0 / np.sqrt(H))
        b1 = jnp.zeros((E, DFF), dtype=jnp.float32)
        W2 = jax.random.normal(ks[3], (E, DFF, H), dtype=jnp.float32) * (1.0 / np.sqrt(DFF))
        b2 = jnp.zeros((E, H), dtype=jnp.float32)
        return {'x': x, 'Wr': Wr, 'br': br, 'W1': W1, 'b1': b1, 'W2': W2, 'b2': b2}
    _L0_ffn_in = _L0_ffn_setup()

    def _L1_attn_setup():
        import jax, jax.numpy as jnp
        import numpy as np
        D_MODEL = 128
        N_HEADS = 16
        LATENT_HEADS = 8
        LATENT_DIM = 64
        N_LATENTS = 64
        WINDOW = 32
        HEAD_DIM = D_MODEL // N_HEADS
        LAT_HD = LATENT_DIM // LATENT_HEADS
        B, S = (2, 512)

        def _pool_to_latents(x):
            Bx, Sx, C = x.shape
            chunk = max(1, Sx // N_LATENTS)
            return x.reshape(Bx, N_LATENTS, chunk, C).mean(axis=2)

        def _local_window_attn(Q, K, V):
            Bx, H, Sx, D = Q.shape
            W = WINDOW
            nb = Sx // W
            Qb = Q.reshape(Bx, H, nb, W, D)
            Kp = jnp.pad(K, ((0, 0), (0, 0), (W, 0), (0, 0))).reshape(Bx, H, nb + 1, W, D)
            Vp = jnp.pad(V, ((0, 0), (0, 0), (W, 0), (0, 0))).reshape(Bx, H, nb + 1, W, D)
            Kw = jnp.concatenate([Kp[:, :, :-1], Kp[:, :, 1:]], axis=3)
            Vw = jnp.concatenate([Vp[:, :, :-1], Vp[:, :, 1:]], axis=3)
            i = jnp.arange(W)[:, None]
            j = jnp.arange(2 * W)[None, :]
            base = (j > i) & (j <= i + W)
            blk0 = (jnp.arange(nb) > 0)[:, None, None] | (j >= W)[None, :, :]
            mask = base[None, :, :] & blk0
            sc = jnp.einsum('bhnid,bhnjd->bhnij', Qb, Kw) / np.sqrt(D).astype(np.float32)
            sc = jnp.where(mask[None, None], sc, -jnp.inf)
            p = jax.nn.softmax(sc, axis=-1)
            out = jnp.einsum('bhnij,bhnjd->bhnid', p, Vw)
            return out.reshape(Bx, H, Sx, D)
        key = jax.random.key(seed)
        ks = jax.random.split(key, 11)
        std = 0.02
        w = lambda k, shp: jax.random.normal(k, shp, jnp.float32) * std
        return {'x': jax.random.normal(ks[0], (B, S, D_MODEL), jnp.float32), 'wq': w(ks[1], (D_MODEL, D_MODEL)), 'wk': w(ks[2], (D_MODEL, D_MODEL)), 'wv': w(ks[3], (D_MODEL, D_MODEL)), 'wgq': w(ks[4], (D_MODEL, LATENT_DIM)), 'wgk': w(ks[5], (D_MODEL, LATENT_DIM)), 'wgv': w(ks[6], (D_MODEL, LATENT_DIM)), 'r_out_w': w(ks[7], (LATENT_DIM, D_MODEL)), 'gate_local_w': w(ks[8], (N_HEADS, HEAD_DIM)), 'gate_remote_w': w(ks[9], (N_HEADS, HEAD_DIM)), 'w_out': w(ks[10], (D_MODEL, D_MODEL))}
    _L1_attn_in = _L1_attn_setup()

    def _L1_ffn_setup():
        import jax, jax.numpy as jnp
        import numpy as np
        TOP_K = 8
        CAPACITY = 64

        def _silu(x):
            return x * jax.nn.sigmoid(x)
        key = jax.random.key(seed)
        ks = jax.random.split(key, 7)
        B, S, H, E, I, Is = (2, 128, 128, 64, 64, 256)
        s = 0.05
        return {'hidden_states': jax.random.normal(ks[0], (B, S, H), jnp.float32), 'gate_w': jax.random.normal(ks[1], (H, E), jnp.float32) * s, 'shared_gate_w': jax.random.normal(ks[2], (H, 1), jnp.float32) * s, 'shared_gate_up_w': jax.random.normal(ks[3], (H, 2 * Is), jnp.float32) * s, 'shared_down_w': jax.random.normal(ks[4], (Is, H), jnp.float32) * s, 'expert_gate_up_w': jax.random.normal(ks[5], (E, H, 2 * I), jnp.float32) * s, 'expert_down_w': jax.random.normal(ks[6], (E, I, H), jnp.float32) * s}
    _L1_ffn_in = _L1_ffn_setup()
    _d = {'L0_attn_x': _L0_attn_in['x'], 'L0_attn_latent_w': _L0_attn_in['latent_w'], 'L0_attn_latent_b': _L0_attn_in['latent_b'], 'L0_attn_Wd_w': _L0_attn_in['Wd_w'], 'L0_attn_Wd_b': _L0_attn_in['Wd_b'], 'L0_attn_out_w': _L0_attn_in['out_w'], 'L0_attn_out_b': _L0_attn_in['out_b'], 'L0_ffn_Wr': _L0_ffn_in['Wr'], 'L0_ffn_br': _L0_ffn_in['br'], 'L0_ffn_W1': _L0_ffn_in['W1'], 'L0_ffn_b1': _L0_ffn_in['b1'], 'L0_ffn_W2': _L0_ffn_in['W2'], 'L0_ffn_b2': _L0_ffn_in['b2'], 'L1_attn_wq': _L1_attn_in['wq'], 'L1_attn_wk': _L1_attn_in['wk'], 'L1_attn_wv': _L1_attn_in['wv'], 'L1_attn_wgq': _L1_attn_in['wgq'], 'L1_attn_wgk': _L1_attn_in['wgk'], 'L1_attn_wgv': _L1_attn_in['wgv'], 'L1_attn_r_out_w': _L1_attn_in['r_out_w'], 'L1_attn_gate_local_w': _L1_attn_in['gate_local_w'], 'L1_attn_gate_remote_w': _L1_attn_in['gate_remote_w'], 'L1_attn_w_out': _L1_attn_in['w_out'], 'L1_ffn_gate_w': _L1_ffn_in['gate_w'], 'L1_ffn_shared_gate_w': _L1_ffn_in['shared_gate_w'], 'L1_ffn_shared_gate_up_w': _L1_ffn_in['shared_gate_up_w'], 'L1_ffn_shared_down_w': _L1_ffn_in['shared_down_w'], 'L1_ffn_expert_gate_up_w': _L1_ffn_in['expert_gate_up_w'], 'L1_ffn_expert_down_w': _L1_ffn_in['expert_down_w']}
    _x0 = _d['L0_attn_x']
    _d['L0_attn_x'] = jax.random.normal(jax.random.fold_in(jax.random.key(seed), 1), (32, 256, 128), dtype=_x0.dtype)
    del _x0
    return _d

def reference(L0_attn_x, L0_attn_latent_w, L0_attn_latent_b, L0_attn_Wd_w, L0_attn_Wd_b, L0_attn_out_w, L0_attn_out_b, L0_ffn_Wr, L0_ffn_br, L0_ffn_W1, L0_ffn_b1, L0_ffn_W2, L0_ffn_b2, L1_attn_wq, L1_attn_wk, L1_attn_wv, L1_attn_wgq, L1_attn_wgk, L1_attn_wgv, L1_attn_r_out_w, L1_attn_gate_local_w, L1_attn_gate_remote_w, L1_attn_w_out, L1_ffn_gate_w, L1_ffn_shared_gate_w, L1_ffn_shared_gate_up_w, L1_ffn_shared_down_w, L1_ffn_expert_gate_up_w, L1_ffn_expert_down_w):

    def _L0_attn_ref(x, latent_w, latent_b, Wd_w, Wd_b, out_w, out_b):
        import jax, jax.numpy as jnp
        import numpy as np
        B, T, C = (2, 256, 128)
        H, L = (16, 36)
        D_HEAD = C // H
        b, t, c = x.shape
        h = Wd_w.shape[0]
        d_head = c // h
        Wdkv = x @ latent_w + latent_b
        q = jnp.einsum('btc,hcl->bhtl', x, Wd_w) + Wd_b[None, :, None, :]
        scores = jnp.einsum('bhtl,bsl->bhts', q, Wdkv) / jnp.asarray(np.sqrt(d_head), dtype=x.dtype)
        causal = jnp.tril(jnp.ones((t, t), dtype=bool))
        scores = jnp.where(causal[None, None, :, :], scores, -jnp.inf)
        attn = jax.nn.softmax(scores, axis=-1)
        y = jnp.einsum('bhts,bsl->bhtl', attn, Wdkv)
        z = jnp.transpose(y, (0, 2, 1, 3)).reshape(b, t, h * Wdkv.shape[-1])
        return z @ out_w + out_b

    def _L0_ffn_ref(x, Wr, br, W1, b1, W2, b2):
        import jax, jax.numpy as jnp
        import numpy as np
        H, E, DFF = (128, 8, 512)
        B, S, Hd = x.shape
        n_exp = W1.shape[0]
        xt = x.reshape(-1, Hd)
        logits = xt @ Wr + br
        probs = jax.nn.softmax(logits, axis=-1)
        gate = jnp.max(probs, axis=-1)
        idx = jnp.argmax(probs, axis=-1)
        h1 = jnp.maximum(jnp.einsum('th,ehf->etf', xt, W1) + b1[:, None, :], 0.0)
        ye = jnp.einsum('etf,efh->eth', h1, W2) + b2[:, None, :]
        onehot = jax.nn.one_hot(idx, n_exp, dtype=xt.dtype)
        y = jnp.einsum('te,eth->th', onehot, ye) * gate[:, None]
        return y.reshape(B, S, Hd)

    def _L1_attn_ref(x, wq, wk, wv, wgq, wgk, wgv, r_out_w, gate_local_w, gate_remote_w, w_out):
        import jax, jax.numpy as jnp
        import numpy as np
        D_MODEL = 128
        N_HEADS = 16
        LATENT_HEADS = 8
        LATENT_DIM = 64
        N_LATENTS = 64
        WINDOW = 32
        HEAD_DIM = D_MODEL // N_HEADS
        LAT_HD = LATENT_DIM // LATENT_HEADS
        B, S = (2, 512)

        def _pool_to_latents(x):
            Bx, Sx, C = x.shape
            chunk = max(1, Sx // N_LATENTS)
            return x.reshape(Bx, N_LATENTS, chunk, C).mean(axis=2)

        def _local_window_attn(Q, K, V):
            Bx, H, Sx, D = Q.shape
            W = WINDOW
            nb = Sx // W
            Qb = Q.reshape(Bx, H, nb, W, D)
            Kp = jnp.pad(K, ((0, 0), (0, 0), (W, 0), (0, 0))).reshape(Bx, H, nb + 1, W, D)
            Vp = jnp.pad(V, ((0, 0), (0, 0), (W, 0), (0, 0))).reshape(Bx, H, nb + 1, W, D)
            Kw = jnp.concatenate([Kp[:, :, :-1], Kp[:, :, 1:]], axis=3)
            Vw = jnp.concatenate([Vp[:, :, :-1], Vp[:, :, 1:]], axis=3)
            i = jnp.arange(W)[:, None]
            j = jnp.arange(2 * W)[None, :]
            base = (j > i) & (j <= i + W)
            blk0 = (jnp.arange(nb) > 0)[:, None, None] | (j >= W)[None, :, :]
            mask = base[None, :, :] & blk0
            sc = jnp.einsum('bhnid,bhnjd->bhnij', Qb, Kw) / np.sqrt(D).astype(np.float32)
            sc = jnp.where(mask[None, None], sc, -jnp.inf)
            p = jax.nn.softmax(sc, axis=-1)
            out = jnp.einsum('bhnij,bhnjd->bhnid', p, Vw)
            return out.reshape(Bx, H, Sx, D)
        Bx, Sx, _ = x.shape
        chunk = max(1, Sx // N_LATENTS)
        Q = (x @ wq).reshape(Bx, Sx, N_HEADS, HEAD_DIM).transpose(0, 2, 1, 3)
        K = (x @ wk).reshape(Bx, Sx, N_HEADS, HEAD_DIM).transpose(0, 2, 1, 3)
        V = (x @ wv).reshape(Bx, Sx, N_HEADS, HEAD_DIM).transpose(0, 2, 1, 3)
        local = _local_window_attn(Q, K, V)
        GQ = (x @ wgq).reshape(Bx, Sx, LATENT_HEADS, LAT_HD).transpose(0, 2, 1, 3)
        GK = _pool_to_latents(x @ wgk).reshape(Bx, N_LATENTS, LATENT_HEADS, LAT_HD).transpose(0, 2, 1, 3)
        GV = _pool_to_latents(x @ wgv).reshape(Bx, N_LATENTS, LATENT_HEADS, LAT_HD).transpose(0, 2, 1, 3)
        lsc = jnp.einsum('bhsd,bhnd->bhsn', GQ, GK) / np.sqrt(LAT_HD).astype(np.float32)
        lmask = jnp.arange(N_LATENTS)[None, :] <= (jnp.arange(Sx) // chunk)[:, None]
        lsc = jnp.where(lmask[None, None], lsc, -jnp.inf)
        lp = jax.nn.softmax(lsc, axis=-1)
        rem = jnp.einsum('bhsn,bhnd->bhsd', lp, GV)
        rem = rem.transpose(0, 2, 1, 3).reshape(Bx, Sx, LATENT_DIM) @ r_out_w
        rem = rem.reshape(Bx, Sx, N_HEADS, HEAD_DIM).transpose(0, 2, 1, 3)
        gl = jax.nn.sigmoid(jnp.einsum('bhsd,hd->bhs', Q, gate_local_w))[..., None]
        gr = jax.nn.sigmoid(jnp.einsum('bhsd,hd->bhs', Q, gate_remote_w))[..., None]
        out = gl * local + gr * rem
        out = out.transpose(0, 2, 1, 3).reshape(Bx, Sx, D_MODEL)
        return out @ w_out

    def _L1_ffn_ref(hidden_states, gate_w, shared_gate_w, shared_gate_up_w, shared_down_w, expert_gate_up_w, expert_down_w):
        import jax, jax.numpy as jnp
        import numpy as np
        TOP_K = 8
        CAPACITY = 64

        def _silu(x):
            return x * jax.nn.sigmoid(x)
        B, S, H = hidden_states.shape
        x = hidden_states.reshape(-1, H)
        T = x.shape[0]
        E = gate_w.shape[1]
        Is = shared_gate_up_w.shape[1] // 2
        I = expert_gate_up_w.shape[2] // 2
        gu = x @ shared_gate_up_w
        shared = _silu(gu[:, :Is]) * gu[:, Is:] @ shared_down_w
        shared = shared * jax.nn.sigmoid(x @ shared_gate_w)
        logits = x @ gate_w
        probs = jax.nn.softmax(logits.astype(jnp.float32), axis=-1)
        w, idx = jax.lax.top_k(probs, TOP_K)
        w = (w / jnp.sum(w, axis=-1, keepdims=True)).astype(x.dtype)
        e_flat = idx.reshape(-1)
        w_flat = w.reshape(-1)
        A = e_flat.shape[0]
        tok = jnp.arange(A) // TOP_K
        onehot = jax.nn.one_hot(e_flat, E, dtype=jnp.int32)
        pos = jnp.take_along_axis(jnp.cumsum(onehot, axis=0) - 1, e_flat[:, None], axis=1)[:, 0]
        slot = jnp.minimum(pos, CAPACITY)
        buf = jnp.zeros((E, CAPACITY + 1, H), x.dtype).at[e_flat, slot].set(x[tok])
        gu_e = jnp.einsum('ech,ehf->ecf', buf, expert_gate_up_w)
        act = _silu(gu_e[..., :I]) * gu_e[..., I:]
        out_e = jnp.einsum('eci,eih->ech', act, expert_down_w)
        y = out_e[e_flat, slot] * w_flat[:, None]
        y = jnp.where((pos < CAPACITY)[:, None], y, jnp.zeros_like(y))
        y = y.reshape(T, TOP_K, H).sum(axis=1)
        return (y + shared).reshape(B, S, H)
    x = L0_attn_x
    xn = _layernorm(x, axis=-1)
    x = x + _L0_attn_ref(xn, L0_attn_latent_w, L0_attn_latent_b, L0_attn_Wd_w, L0_attn_Wd_b, L0_attn_out_w, L0_attn_out_b) + _L0_ffn_ref(xn, L0_ffn_Wr, L0_ffn_br, L0_ffn_W1, L0_ffn_b1, L0_ffn_W2, L0_ffn_b2)
    xn = _layernorm(x, axis=-1)
    x = x + _L1_attn_ref(xn, L1_attn_wq, L1_attn_wk, L1_attn_wv, L1_attn_wgq, L1_attn_wgk, L1_attn_wgv, L1_attn_r_out_w, L1_attn_gate_local_w, L1_attn_gate_remote_w, L1_attn_w_out) + _L1_ffn_ref(xn, L1_ffn_gate_w, L1_ffn_shared_gate_w, L1_ffn_shared_gate_up_w, L1_ffn_shared_down_w, L1_ffn_expert_gate_up_w, L1_ffn_expert_down_w)
    return x

_drawn_inputs = setup_inputs


def setup_inputs(seed=0):
    import zlib

    import numpy as np

    out = dict(_drawn_inputs(seed))
    spreads = {'L0_ffn_br': (0.0, 0.1), 'L0_ffn_b1': (0.0, 0.3), 'L0_ffn_b2': (0.0, 0.1)}
    factors = {'L0_attn_latent_w': 3.334,
     'L0_attn_latent_b': 7.322,
     'L0_attn_Wd_w': 8.0,
     'L0_attn_Wd_b': 8.0,
     'L0_attn_out_w': 2.917,
     'L0_attn_out_b': 2.749,
     'L1_attn_wq': 8.0,
     'L1_attn_wk': 8.0,
     'L1_attn_wv': 8.0,
     'L1_attn_wgq': 28.393,
     'L1_attn_wgk': 28.275,
     'L1_attn_wgv': 8.0,
     'L1_attn_r_out_w': 8.0,
     'L1_attn_gate_local_w': 30.244,
     'L1_attn_gate_remote_w': 49.388,
     'L1_attn_w_out': 8.0,
     'L1_ffn_gate_w': 8.0,
     'L1_ffn_shared_gate_w': 25.52,
     'L1_ffn_expert_gate_up_w': 8.0,
     'L1_ffn_expert_down_w': 8.0,
     'L1_ffn_shared_gate_up_w': 6.207,
     'L1_ffn_shared_down_w': 6.257}
    for name, (base, spread) in spreads.items():
        noise = np.random.default_rng([zlib.crc32(name.encode()), seed]).standard_normal(out[name].shape)
        drawn = base * np.exp(spread * noise) if base else spread * noise
        out[name] = jnp.asarray(drawn.astype(out[name].dtype))
    for name, factor in factors.items():
        out[name] = (out[name] * factor).astype(out[name].dtype)
    return out
```

```python
from contextlib import ExitStack

import concourse.bass as bass
from concourse import mybir

F32 = mybir.dt.float32
BF16 = mybir.dt.bfloat16
U32 = mybir.dt.uint32
I32 = mybir.dt.int32
ALU = mybir.AluOpType
ACT = mybir.ActivationFunctionType
AX = mybir.AxisListType
P = 128
NEG = -1e30
EPS = 1e-5


class Batch:

    def __init__(self, pair, half):
        self.pair, self.half, self.b = pair, half, pair * 2 + half

    def next(self):
        return Batch(self.pair, 1) if self.half == 0 else Batch(self.pair + 1, 0)


def program(nc, a, out):
    x = a["L0_attn_x"]
    B, T, C = x.shape
    H, _, L = a["L0_attn_Wd_w"].shape
    E0 = a["L0_ffn_Wr"].shape[1]
    NT = B * T // P
    TILES = NT + E0
    E1 = a["L1_ffn_gate_w"].shape[1]
    IS = a["L1_ffn_shared_down_w"].shape[0]
    DL = a["L1_attn_wgq"].shape[1]
    W = 32
    NL = 64
    CHUNK = T // NL
    PAIRS = H // 2
    SCALE0 = float((C // H) ** -0.5)
    LP = 64
    HY = 4
    NC = 5

    ctx = ExitStack()
    with ctx:
        ctx.enter_context(nc.allow_non_contiguous_dma(reason="small weight columns, once"))

        early = ExitStack()
        scope = [ctx]

        def sb(name, shape, dt=F32):
            return scope[0].enter_context(nc.sbuf_tensor(name, shape, dt))

        def sem(name):
            return ctx.enter_context(nc.semaphore(name))

        bank = [ctx.enter_context(nc.psum_tensor(f"bank{i}", [P, 512], F32)) for i in range(4)]
        bankA, bankB = bank[0], bank[1]
        bankY = bank[2:4]
        bankS = ctx.enter_context(nc.psum_tensor("bankS", [P, 2, 512], F32))
        bankT = ctx.enter_context(nc.psum_tensor("bankT", [P, 2, 512], F32))

        ident = sb("ident", [P, P])
        identb = sb("identb", [P, P], BF16)
        ones = sb("ones", [1, P])
        halfneg = sb("halfneg", [P, 2])
        zeros = sb("zeros", [P, C])
        iota_i = sb("iota_i", [P, TILES], I32)
        iota_f = sb("iota_f", [P, TILES])
        gate_all = sb("gate_all", [P, NT])
        pos_all = sb("pos_all", [P, NT], I32)
        mv = sb("mv", [P, 2, 2])
        stats = sb("stats", [P, 2, 6])
        rstd = sb("rstd", [P, 2, 2])
        xa_all = sb("xa_all", [P, NT, C])
        NB = T // W
        wqk = sb("wqk", [P, 2, C])
        wv = sb("wv", [P, C])
        wgqk = sb("wgqk", [P, 2, P])
        wgv = sb("wgv", [P, DL])
        wro = sb("wro", [DL, C])
        wo1 = sb("wo1", [P, C])
        gw = sb("gw", [P, E1 + 1])
        sgu = sb("sgu", [P, 2 * IS])
        sdw = sb("sdw", [P, IS // P, C])
        gcol = sb("gcol", [P, 2])
        gates = sb("gates", [P, 2, P])
        block16 = sb("block16", [P, P])
        maskl = sb("maskl", [P, 2, 2 * W], BF16)
        maskr = sb("maskr", [P, NB, NL], BF16)
        headcol = sb("headcol", [P, 4])
        quadcol = sb("quadcol", [P, P])
        upto = sb("upto", [P, 2, P], BF16)
        scope[0] = early
        maskq = sb("maskq", [P, P], BF16)
        maskk = sb("maskk", [P, P], BF16)
        headrow = sb("headrow", [H, H, P], BF16)
        wd = sb("wd", [P, PAIRS, 2, LP])
        bd = sb("bd", [P, PAIRS])
        lw = sb("lw", [P, 2, LP])
        lb = sb("lb", [P, 1])
        lbrow = sb("lbrow", [1, L])
        wr = sb("wr", [P, E0])
        brow = sb("brow", [1, E0])
        ow = sb("ow", [P, NC, P])
        ob = sb("ob", [1, P])

        xt = sb("xt", [P, 2, 2, C])
        xn = sb("xn", [P, 2, 2, C])
        xnT = sb("xnT", [P, 2, T])
        kT = sb("kT", [P, 2, T])
        vaug = sb("vaug", [P, 2, 2, L + 1])
        qT = sb("qT", [P, 2, PAIRS, T])
        mneg = sb("mneg", [P, 2, 2, H])
        mT = sb("mT", [H, 2, T], BF16)
        pT = sb("pT", [P, 4, 384])
        rz = sb("rz", [P, 2, 2, HY])
        z = sb("z", [P, 2, H * L])
        zT = sb("zT", [P, NC, T])
        xn_all = sb("xn_all", [P, NT, C])
        lg_all = sb("lg_all", [P, NT, E0])

        F0 = a["L0_ffn_W1"].shape[2]
        KF = F0 // P
        TILES = NT + E0
        WC = 2 * F0 + KF
        wall = sb("wall", [P, E0, WC])
        b2row = sb("b2row", [1, E0, C])
        strict = sb("strict", [P, P], BF16)
        onesb = sb("onesb", [P, P], BF16)
        mx0 = sb("mx0", [P, NT])
        lgs0 = sb("lgs0", [P, NT, E0])
        eq0 = sb("eq0", [P, NT, E0])
        oh0 = sb("oh0", [P, NT, E0], BF16)
        tot0 = sb("tot0", [P, NT, E0])
        cs0 = sb("cs0", [P, NT, E0])
        cnt_i = sb("cnt_i", [P, 2, E0], I32)
        ptile = sb("ptile", [P, E0])
        pend = sb("pend", [P, E0])
        pbase = sb("pbase", [P, E0])
        posf = sb("posf", [P, NT])
        tsel = sb("tsel", [P, TILES, E0])
        tef = sb("tef", [P, TILES])
        te_i = sb("te_i", [P, TILES], I32)
        stage_x = sb("stage_x", [P, 2, C])
        stage_p = sb("stage_p", [P, 2, 1], I32)
        xsb = sb("xsb", [P, 2, C])
        xsT = sb("xsT", [P, 2, P])
        w1b = sb("w1b", [P, 2, F0 + KF])
        hT = sb("hT", [P, 2, KF, P])
        ysb = sb("ysb", [P, 2, C])
        xs_d = nc.dram_tensor("xs_sorted", [TILES * P, C], F32).ap()
        ys_d = nc.dram_tensor("ys_sorted", [TILES * P, C], F32).ap()

        early.close()
        scope[0] = ctx
        cnt_all = sb("cnt_all", [E1, B * T])
        mid = ExitStack()
        scope[0] = mid
        yg = sb("yg", [P, 2, 2, C])
        idx_g = sb("idx_g", [P, 2, 2], I32)
        gate_g = sb("gate_g", [P, 2, 2])
        x1 = sb("x1", [P, 2, 2, C])
        tab = sb("tab", [P, 2, 2, C + E1])
        xT1 = sb("xT1", [P, 2, T])
        xp = sb("xp", [P, 2, NL])
        xr = sb("xr", [P, 2, NB, 4, W])
        xpr = sb("xpr", [P, 2, 2, 4, W])
        qx = sb("qx", [P, 2, NB, 4, W])
        qs = sb("qs", [P, 2, T])
        km = sb("km", [P, 2, 4, W + T])
        gqx = sb("gqx", [P, 2, NB, 4, W])
        gkm = sb("gkm", [P, 2, 2, NL])
        vx = sb("vx", [P, 2, NB, C])
        gvx = sb("gvx", [P, 2, 2, DL])
        lg1 = sb("lg1", [P, 2, E1 + 1])
        mx8 = sb("mx8", [P, 2, 8])
        lgr = sb("lgr", [P, 2, E1])
        mb = sb("mb", [P, 2, 2, E1], BF16)
        shl = sb("shl", [P, 2, E1])
        exl = sb("exl", [P, 2, E1])
        tsg = sb("tsg", [P, 2])
        sgc = sb("sgc", [P, 2, 2])
        wsum = sb("wsum", [P, 2, 2])
        carry = sb("carry", [E1, 2, 1])
        mxs = sb("mxs", [P, 2, 12])
        pr = sb("pr", [P, 2, 12 * NL])
        pt = sb("pt", [P, NB, 6, 2, W])
        tsh = sb("tsh", [P, 2 * T])
        shT = sb("shT", [P, IS // P, T])
        rdr = sb("rdr", [DL, T])
        remn = sb("remn", [DL, T])
        rdl = sb("rdl", [P, T])
        tg = sb("tg", [P, 2, T])
        at1 = sb("at1", [P, T])
        at2 = sb("at2", [P, T])
        aT = sb("aT", [P, T])
        res = sb("res", [P, 2, 2, C])
        mid.close()
        scope[0] = ctx
        CAP = 64
        IE = a["L1_ffn_expert_down_w"].shape[1]
        GE = 8
        NG = E1 // GE
        RW = C + E1
        slot_i = sb("slot_i", [CAP, 1], I32)
        slot_f = sb("slot_f", [CAP, 2])
        full_tiles = sb("full_tiles", [E1, CAP, NT])
        tile_row = sb("tile_row", [E1, 2, CAP])
        tile_at = sb("tile_at", [CAP, E1])
        row_at = sb("row_at", [CAP, E1], I32)
        ridx = sb("ridx", [CAP, 2, GE], I32)
        cg = sb("cg", [CAP, 2, GE, P])
        below = sb("below", [CAP, GE, P])
        tok = sb("tok", [CAP, 2, GE])
        dump = sb("dump", [CAP, GE])
        sidx = sb("sidx", [CAP, 2, GE], I32)
        xg = sb("xg", [CAP, 2, GE, RW])
        xgT = sb("xgT", [P, 2, GE * CAP])
        wge = sb("wge", [P, 2, GE, 2 * IE])
        wde = sb("wde", [IE, 2, GE, C])
        the = sb("the", [IE, GE * CAP])
        ae = sb("ae", [IE, GE * CAP])
        wblk = sb("wblk", [CAP, 2, GE * GE])
        yo = sb("yo", [CAP, 2, GE, C])
        cnt_d = nc.dram_tensor("counts", [E1 * NT, P], F32).ap()
        PAD = P
        xtab_d = nc.dram_tensor("xtab", [B * T + PAD, C + E1], F32).ap()
        acc_d = nc.dram_tensor("acc", [B * T + PAD, C], F32).ap()

        names = """consts zeroed w_in x_in0 x_in1 bn stats_done var rstd_done xn_done xn_kept xnT_ps xnT_sb kv_ps kv_sb
        q_ps q_sb s_ps red_done mT_ps mT_sb st_ps exp_done av_done rz_done y_sb zt_ps zt_sb out_ps xa_done cst dumped passed xs_zero rt ex0 rk_ps staged scat0 scat1 te_done xs_in0 xs_in1 w1_sb xsT_ps xsT_sb h_ps h_act h_dve
        yt_ps yt_sb ys_out0 ys_out1 yg_t x1_all te_go w1_in pads
        yg0 yg1 gidx x1_done bn1 stats1 var1 rstd1 xn1_done tT_ps tT_sb xp_done qk_ps rt_ps rt_sb qx_done kt_sb g_ps g_sb gk_sb
        rstep M_done ex_in ex_done tab_done cnt_ps cnt_sb v_ps v_sb s2_ps red2 sub_done exp2 tr_done shg_ps shu_ps tanh_sh
        sh1_done sh_sb shd_ps av_ps rd_done remn_done rem2_ps gate_ps gate_sb comb aT_done ao_ps r1_done res_done
        tab_out0 tab_out1 res_out0 res_out1 l1_consts wprep xpr_sb slots cnt_out f4 cg_in0 cg_in1 sel sidx_done xg_in0 xg_in1 xgT_ps xgT_sb gu_ps
        the_sb ae1 ae_sb oe_ps wblk_sb yo_sb rix added we_in0 we_in1 tr4""".split()
        S = {n: sem(n) for n in names}
        x_in = [S["x_in0"], S["x_in1"]]
        block = ctx.enter_context(nc.Block())

        def passed(eng):
            eng.sem_inc(S["passed"], 1)

        NW = 14 + 2 + 2 * KF + 1
        hbank = [bankS, bankT]
        xv = x.rearrange("b (t p) c -> b p t c", p=P)
        LOOP = B // 2 - 1

        @block.sync
        def _(sp):
            sp.wait_ge(S["zeroed"], 4)
            for e in range(2):
                sp.dma_start(wd[:, :, e, 0:L], a["L0_attn_Wd_w"].rearrange("(j e) c l -> e c j l", e=2)[e]).then_inc(S["w_in"], 16)
                sp.dma_start(bd[LP * e:LP * e + L, :], a["L0_attn_Wd_b"].rearrange("(j e) l -> e l j", e=2)[e]).then_inc(S["w_in"], 16)
                sp.dma_start(lw[:, e, 0:L], a["L0_attn_latent_w"]).then_inc(S["w_in"], 16)
                sp.dma_start(lb[LP * e:LP * e + L, :], a["L0_attn_latent_b"].rearrange("(l o) -> l o", o=1)).then_inc(S["w_in"], 16)
            sp.dma_start(lbrow[:, :], a["L0_attn_latent_b"].rearrange("(o l) -> o l", o=1)).then_inc(S["w_in"], 16)
            sp.dma_start(wr[:, :], a["L0_ffn_Wr"]).then_inc(S["w_in"], 16)
            sp.dma_start(brow[:, :], a["L0_ffn_br"].rearrange("(o l) -> o l", o=1)).then_inc(S["w_in"], 16)
            sp.dma_start(ow[:, 0:4, :], a["L0_attn_out_w"][0:4 * P, :].rearrange("(k p) c -> p k c", p=P)).then_inc(S["w_in"], 16)
            sp.dma_start(ow[0:LP, 4, :], a["L0_attn_out_w"][4 * P:H * L, :]).then_inc(S["w_in"], 16)
            sp.dma_start(ob[:, :], a["L0_attn_out_b"].rearrange("(o l) -> o l", o=1)).then_inc(S["w_in"], 16)
            for e in range(2):
                lo, hi = e * E0 // 2, (e + 1) * E0 // 2
                sp.dma_start(wall[:, lo:hi, 0:F0], a["L0_ffn_W1"][lo:hi].rearrange("e c f -> c e f")).then_inc(S["w_in"], 16)
            for k in range(KF):
                sp.dma_start(wall[:, :, F0 + KF + k * C:F0 + KF + (k + 1) * C],
                             a["L0_ffn_W2"].rearrange("e (k p) c -> k p e c", p=P)[k]).then_inc(S["w_in"], 16)
                sp.dma_start(wall[:, :, F0 + k:F0 + k + 1], a["L0_ffn_b1"].rearrange("e (k p o) -> k p e o", p=P, o=1)[k]).then_inc(S["w_in"], 16)
            sp.dma_start(b2row[:, :, :], a["L0_ffn_b2"].rearrange("(o e) c -> o e c", o=1)).then_inc(S["w_in"], 16)
            sp.dma_start(xs_d.rearrange("(j p) c -> p j c", p=P), zeros[:, :].unsqueeze(1).to_broadcast([P, TILES, C])).then_inc(S["xs_zero"], 16)
            for u in range(2):
                sp.dma_start(xt[:, u], xv[u]).then_inc(x_in[u], 16)
            for k, w in enumerate(("wq", "wk")):
                sp.dma_start(wqk[:, k, :], a["L1_attn_" + w]).then_inc(S["w1_in"], 16)
                sp.dma_start(wgqk[:, k, 0:DL], a["L1_attn_" + ("wgq", "wgk")[k]]).then_inc(S["w1_in"], 16)
                sp.dma_start(gcol[:, k:k + 1], a["L1_attn_gate_" + ("local_w", "remote_w")[k]].rearrange("h (d o) -> (h d) o", o=1)).then_inc(S["w1_in"], 16)
            sp.dma_start(wv[:, :], a["L1_attn_wv"]).then_inc(S["w1_in"], 16)
            sp.dma_start(wgv[:, :], a["L1_attn_wgv"]).then_inc(S["w1_in"], 16)
            sp.dma_start(wro[:, :], a["L1_attn_r_out_w"]).then_inc(S["w1_in"], 16)
            sp.dma_start(wo1[:, :], a["L1_attn_w_out"]).then_inc(S["w1_in"], 16)
            sp.dma_start(gw[:, 0:E1], a["L1_ffn_gate_w"]).then_inc(S["w1_in"], 16)
            sp.dma_start(gw[:, E1:E1 + 1], a["L1_ffn_shared_gate_w"]).then_inc(S["w1_in"], 16)
            sp.dma_start(sgu[:, :], a["L1_ffn_shared_gate_up_w"]).then_inc(S["w1_in"], 16)
            sp.dma_start(sdw[:, :, :], a["L1_ffn_shared_down_w"].rearrange("(k p) c -> p k c", p=P)).then_inc(S["w1_in"], 16)
            sp.dma_start(acc_d[B * T:B * T + PAD, :], zeros[:, :]).then_inc(S["pads"], 16)
            sp.dma_start(xtab_d[B * T:B * T + PAD, 0:C], zeros[:, :]).then_inc(S["pads"], 16)
            sp.dma_start(xtab_d[B * T:B * T + PAD, C:C + E1], zeros[:, 0:E1]).then_inc(S["pads"], 16)

            def step(b):
                sp.wait_ge(S["xa_done"], b.b + 2)
                sp.dma_start(xt[:, b.half], xv[b.b + 2]).then_inc(x_in[b.half], 16)

            with sp.Fori(0, LOOP) as i:
                step(Batch(i, 0))
                step(Batch(i, 1))

            def load(i, u):
                if u is not None:
                    sp.dma_start(xsb[:, u], xs_d[bass.ds((i * 2 + u) * P, P), :]).then_inc(S[f"xs_in{u}"], 16)

            def store(i, u):
                sp.wait_ge(S["yt_sb"], i * 2 + (u + 1))
                sp.dma_start(ys_d[bass.ds((i * 2 + u) * P, P), :], ysb[:, u]).then_inc(S[f"ys_out{u}"], 16)

            sp.wait_ge(S["scat0"], 16 * (NT // 2))
            sp.wait_ge(S["scat1"], 16 * (NT // 2))
            load(0, 0)
            load(0, 1)
            with sp.Fori(0, TILES // 2 - 1) as i:
                for u in range(2):
                    sp.wait_ge(S["xsT_ps"], i * 2 + (u + 1))
                    load(i + 1, u)
                    store(i, u)
            for u in range(2):
                store(TILES // 2 - 1, u)
            sp.wait_ge(S["ys_out0"], 16 * (TILES // 2))
            sp.wait_ge(S["ys_out1"], 16 * (TILES // 2))

            def save_table(n):
                sp.wait_ge(S["tab_done"], n.b + 1)
                sp.dma_start(xtab_d[bass.ds(n.b * T, T), :].rearrange("(t p) c -> p t c", p=P), tab[:, n.half]).then_inc(S[f"tab_out{n.half}"], 16)

            def save_stream(b):
                sp.wait_ge(S["res_done"], b.b + 2)
                sp.dma_start(acc_d[bass.ds(b.b * T, T), :].rearrange("(t p) c -> p t c", p=P), res[:, b.half]).then_inc(S[f"res_out{b.half}"], 16)

            save_table(Batch(0, 0))
            with sp.Fori(0, LOOP) as i:
                for b in (Batch(i, 0), Batch(i, 1)):
                    save_table(b.next())
                    save_stream(b)
            save_table(Batch(LOOP, 1))
            save_stream(Batch(LOOP, 0))
            save_stream(Batch(LOOP, 1))
            for u in range(2):
                sp.wait_ge(S[f"res_out{u}"], 16 * (B // 2) + 16)
                sp.wait_ge(S[f"tab_out{u}"], 16 * (B // 2) + 16)
            sp.wait_ge(S["cnt_sb"], B + 1)
            sp.dma_start(cnt_d.rearrange("(e n) p -> e (n p)", e=E1), cnt_all[:, :]).then_inc(S["cnt_out"], 16)

            def weights(g):
                u = g.half
                sp.dma_start(wge[:, u], a["L1_ffn_expert_gate_up_w"][bass.ds(g.b * GE, GE)].rearrange("e h f -> h e f")).then_inc(S[f"we_in{u}"], 16)
                sp.dma_start(wde[:, u], a["L1_ffn_expert_down_w"][bass.ds(g.b * GE, GE)].rearrange("e i h -> i e h")).then_inc(S[f"we_in{u}"], 16)

            weights(Batch(0, 0))
            weights(Batch(0, 1))
            with sp.Fori(0, NG // 2 - 1) as i:
                for g in (Batch(i, 0), Batch(i, 1)):
                    sp.wait_ge(S["oe_ps"], g.b + 1)
                    weights(g.next().next())
            sp.wait_ge(S["added"], 16 * E1)
            sp.dma_start(out.rearrange("b t c -> (b t) c"), acc_d[0:B * T, :]).then_inc(S["dumped"], 16)
            sp.wait_ge(S["dumped"], 16)

        @block.gpsimd
        def _(pool):
            pool.memset(zeros[:, :], 0.0)
            pool.memset(wd[:, :, :, :], 0.0).then_inc(S["zeroed"], 1)
            pool.memset(lw[:, :, :], 0.0).then_inc(S["zeroed"], 1)
            pool.memset(lb[:, :], 0.0)
            pool.memset(bd[:, :], 0.0).then_inc(S["zeroed"], 1)
            pool.memset(ones[:, :], 1.0)
            pool.memset(halfneg[:, :], -0.5)
            pool.memset(vaug[:, :, :, L:L + 1], 1.0)
            pool.memset(onesb[:, :], 1.0)
            pool.memset(strict[:, :], 1.0)
            pool.iota(iota_i[:, :], pattern=[[1, TILES]], base=0, channel_multiplier=0)
            pool.memset(ident[:, :], 0.0)
            pool.memset(identb[:, :], 0.0)
            pool.memset(maskq[:, :], 0.0)
            pool.memset(maskk[:, :], 0.0)
            pool.memset(headrow[:, :, :], 0.0).then_inc(S["cst"], 1)
            pool.wait_ge(S["cst"], 1)
            for m in (ident, identb):
                pool.affine_select(out=m[:, :], in_=m[:, :], compare_op=ALU.not_equal, fill=1.0, base=0,
                                   pattern=[[-1, P]], channel_multiplier=1)
            pool.affine_select(out=maskq[:, :], in_=maskq[:, :], compare_op=ALU.is_ge, fill=NEG, base=0,
                               pattern=[[-1, P]], channel_multiplier=1)
            pool.affine_select(out=strict[:, :], in_=strict[:, :], compare_op=ALU.is_gt, fill=0.0, base=0,
                               pattern=[[1, P]], channel_multiplier=-1)
            pool.affine_select(out=maskk[:, :], in_=maskk[:, :], compare_op=ALU.is_ge, fill=NEG, base=0,
                               pattern=[[1, P]], channel_multiplier=-1)
            pool.affine_select(out=headrow[:, :, :], in_=headrow[:, :, :], compare_op=ALU.not_equal, fill=1.0, base=0,
                               pattern=[[1, H], [0, P]], channel_multiplier=-1).then_inc(S["consts"], 1)

            made = 1

            def chain(ins):
                nonlocal made
                made += 1
                ins.then_inc(S["cst"], 1)
                pool.wait_ge(S["cst"], made)

            def keep(v, op, fill, base, pattern, step):
                chain(pool.affine_select(out=v, in_=v, compare_op=op, fill=fill, base=base, pattern=pattern, channel_multiplier=step))

            pool.memset(wgqk[:, :, :], 0.0).then_inc(S["zeroed"], 1)
            pool.memset(maskl[:, :, :], 0.0)
            pool.memset(maskr[:, :, :], 0.0)
            pool.memset(headcol[:, :], 1.0)
            pool.memset(quadcol[:, :], 0.0)
            pool.memset(upto[:, :, :], 1.0)
            chain(pool.memset(block16[:, :], 1.0))
            keep(block16[:, :], ALU.is_ge, 0.0, 0, [[-8, 16], [0, 8]], 1)
            keep(block16[:, :], ALU.is_ge, 0.0, 7, [[8, 16], [0, 8]], -1)
            keep(upto[:, 0, :], ALU.is_ge, 0.0, 0, [[1, P]], -1)
            for g in range(4):
                q = slice(W * g, W * g + W)
                keep(maskl[q], ALU.is_gt, NEG, 0, [[0, 2], [1, 2 * W]], -1)
                keep(maskl[q], ALU.is_ge, NEG, W, [[0, 2], [-1, 2 * W]], 1)
                keep(maskr[q], ALU.is_ge, NEG, 0, [[W, NB], [-CHUNK, NL]], 1)
                keep(headcol[q, :], ALU.is_ge, 0.0, 0, [[-8, 4]], 1)
                keep(headcol[q, :], ALU.is_ge, 0.0, 7, [[8, 4]], -1)
                chain(pool.memset(quadcol[q, :].rearrange("p (a h d) -> p a h d", h=4, d=8)[:, :, g, :], 1.0))
            pool.memset(maskl[:, 0, 0:W], NEG).then_inc(S["l1_consts"], 1)
            pool.wait_ge(S["l1_consts"], 1)

            def stage_a(n):
                pool.wait_ge(S["stats_done"], n.b + 1)
                passed(pool)
                pool.tensor_scalar(rstd[:, 0], mv[:, :, 1], EPS, None, ALU.add).then_inc(S["var"], 1)
                pool.wait_ge(S["var"], n.b + 1)
                pool.tensor_tensor(rstd[:, 1], rstd[:, 0], halfneg[:, :], ALU.pow).then_inc(S["rstd_done"], 1)
                pool.wait_ge(S["xn_done"], n.b + 1)
                pool.tensor_copy(xn_all[:, bass.ds(n.b * 2, 2), :], xn[:, n.half]).then_inc(S["xn_kept"], 1)

            stage_a(Batch(0, 0))
            with pool.Fori(0, LOOP) as i:
                stage_a(Batch(i, 1))
                stage_a(Batch(i + 1, 0))
            stage_a(Batch(LOOP, 1))

            pool.wait_ge(S["te_done"], 1)
            pool.wait_ge(S["xs_zero"], 16)

            def scatter(i, u, first):
                n = i * 2 + u
                if not first:
                    pool.wait_ge(S[f"scat{u}"], i * 16)
                pool.tensor_copy(stage_x[:, u, :], xn_all[:, bass.ds(n, 1), :].rearrange("p a c -> p (a c)"))
                pool.tensor_copy(stage_p[:, u, :], pos_all[:, bass.ds(n, 1)]).then_inc(S["staged"], 1)
                pool.wait_ge(S["staged"], n + 1)
                passed(pool)
                pool.indirect_dma_start(out=xs_d, out_offset=bass.IndirectOffsetOnAxis(ap=stage_p[:, u, :], axis=0),
                                        in_=stage_x[:, u, :], in_offset=None).then_inc(S[f"scat{u}"], 16)

            for u in range(2):
                scatter(0, u, True)
            with pool.Fori(1, NT // 2) as i:
                for u in range(2):
                    scatter(i, u, False)

            pool.wait_ge(S["ys_out0"], 16 * (TILES // 2))
            pool.wait_ge(S["ys_out1"], 16 * (TILES // 2))
            pool.wait_ge(S["scat0"], 16 * (NT // 2))
            pool.wait_ge(S["scat1"], 16 * (NT // 2))

            pool.memset(km[:, :, :, :], 0.0)
            pool.memset(gkm[:, :, :, :], 0.0)
            pool.memset(carry[:, :, :], 0.0).then_inc(S["pads"], 16)

            def gather(m):
                u = m.half
                pool.tensor_copy(idx_g[:, u, :], pos_all[:, bass.ds(m.b * 2, 2)])
                pool.tensor_copy(gate_g[:, u, :], gate_all[:, bass.ds(m.b * 2, 2)]).then_inc(S["gidx"], 1)
                pool.wait_ge(S["gidx"], m.b + 1)
                passed(pool)
                for t in range(2):
                    pool.indirect_dma_start(out=yg[:, u, t, :], out_offset=None, in_=ys_d,
                                            in_offset=bass.IndirectOffsetOnAxis(ap=idx_g[:, u, t:t + 1], axis=0)).then_inc(S[f"yg{u}"], 16)

            def deviation(n):
                pool.wait_ge(S["stats1"], n.b + 1)
                passed(pool)
                pool.tensor_scalar(rstd[:, 0], mv[:, :, 1], EPS, None, ALU.add).then_inc(S["var1"], 1)
                pool.wait_ge(S["var1"], n.b + 1)
                pool.tensor_tensor(rstd[:, 1], rstd[:, 0], halfneg[:, :], ALU.pow).then_inc(S["rstd1"], 1)

            gather(Batch(0, 0))
            gather(Batch(0, 1))
            deviation(Batch(0, 0))
            with pool.Fori(0, LOOP) as i:
                for b in (Batch(i, 0), Batch(i, 1)):
                    deviation(b.next())
                    gather(b.next().next())
            deviation(Batch(LOOP, 1))
            pool.iota(slot_i[:, :], pattern=[[0, 1]], base=0, channel_multiplier=1).then_inc(S["slots"], 1)
            for u in range(2):
                pool.wait_ge(S[f"res_out{u}"], 16 * (B // 2) + 16)
                pool.wait_ge(S[f"tab_out{u}"], 16 * (B // 2) + 16)
            pool.wait_ge(S["cnt_out"], 16)
            pool.wait_ge(S["f4"], 1)

            def count_rows(g):
                u = g.half
                pool.tensor_copy(ridx[:, u, :], row_at[:, bass.ds(g.b * GE, GE)]).then_inc(S["rix"], 1)
                pool.wait_ge(S["rix"], g.b + 1)
                passed(pool)
                for e in range(GE):
                    pool.indirect_dma_start(out=cg[:, u, e, :], out_offset=None, in_=cnt_d,
                                            in_offset=bass.IndirectOffsetOnAxis(ap=ridx[:, u, e:e + 1], axis=0)).then_inc(S[f"cg_in{u}"], 16)

            def token_rows(g):
                u = g.half
                pool.wait_ge(S["sidx_done"], g.b + 1)
                passed(pool)
                for e in range(GE):
                    pool.indirect_dma_start(out=xg[:, u, e, :], out_offset=None, in_=xtab_d,
                                            in_offset=bass.IndirectOffsetOnAxis(ap=sidx[:, u, e:e + 1], axis=0)).then_inc(S[f"xg_in{u}"], 16)

            def add_rows(g):
                u = g.half
                pool.wait_ge(S["yo_sb"], g.b + 1)
                passed(pool)
                for e in range(GE):
                    pool.indirect_dma_start(out=acc_d, out_offset=bass.IndirectOffsetOnAxis(ap=sidx[:, u, e:e + 1], axis=0),
                                            in_=yo[:, u, e, :], in_offset=None, compute_op=ALU.add).then_inc(S["added"], 16)
                    pool.wait_ge(S["added"], (g.b * GE + (e + 1)) * 16)
                    passed(pool)

            def step4(g, n):
                if n:
                    count_rows(n)
                    token_rows(n)
                if g:
                    add_rows(g)

            step4(None, Batch(0, 0))
            with pool.Fori(0, NG // 2 - 1) as i:
                step4(Batch(i, 0), Batch(i, 1))
                step4(Batch(i, 1), Batch(i + 1, 0))
            step4(Batch(NG // 2 - 1, 0), Batch(NG // 2 - 1, 1))
            step4(Batch(NG // 2 - 1, 1), None)

        @block.vector
        def _(dve):
            def norm(n):
                u = n.half
                dve.wait_ge(x_in[u], n.pair * 16 + 16)
                for t in range(2):
                    ins = dve.bn_stats(stats[:, t, :], xt[:, u, t, :])
                ins.then_inc(S["bn"], 1)
                dve.wait_ge(S["bn"], n.b + 1)
                passed(dve)
                for t in range(2):
                    ins = dve.bn_aggr(mv[:, t, :], stats[:, t, :])
                ins.then_inc(S["stats_done"], 1)
                dve.wait_ge(S["rstd_done"], n.b + 1)
                dve.wait_ge(S["stats_done"], n.b + 1)
                for t in range(2):
                    ins = dve.tensor_scalar(xn[:, u, t, :], xt[:, u, t, :], mv[:, t, 0:1], rstd[:, 1, t:t + 1],
                                            ALU.subtract, ALU.mult)
                ins.then_inc(S["xn_done"], 1)

            def kv(n):
                u = n.half
                dve.wait_ge(S["kv_ps"], n.b + 1)
                dve.tensor_scalar(kT[:, u, :], bankB[:, 0:T], lb[:, 0:1], None, ALU.add)
                dve.tensor_copy(vaug[:, u, :, 0:L], bankB[:, 256:256 + 2 * L].rearrange("p (t l) -> p t l", t=2))
                dve.tensor_copy(lg_all[:, bass.ds(n.b * 2, 2), :],
                                bankB[:, 384:384 + 2 * E0].rearrange("p (t l) -> p t l", t=2)).then_inc(S["kv_sb"], 1)

            def red(n, g):
                dve.wait_ge(S["s_ps"], n.b * PAIRS + (g + 1))
                dve.tensor_reduce(mneg[:, n.half, 0, 2 * g:2 * g + 2], bankS[:, :, 0:128], AX.X, ALU.max, negate=True)
                dve.tensor_reduce(mneg[:, n.half, 1, 2 * g:2 * g + 2], bankS[:, :, 128:384], AX.X, ALU.max,
                                  negate=True).then_inc(S["red_done"], 1)

            def yevac(b, q):
                dve.wait_ge(S["av_done"], b.b * H + HY * (q + 1))
                y = bankY[q % 2][:, 0:2 * HY * (L + 1)].rearrange("p (t h l) -> p t h l", t=2, h=HY)
                dve.reciprocal(rz[:, q % 2], y[:, :, :, L]).then_inc(S["rz_done"], 1)
                dve.wait_ge(S["rz_done"], b.b * 4 + (q + 1))
                zq = z[:, :, q * HY * L:(q + 1) * HY * L].rearrange("p t (h l) -> p t h l", h=HY)
                dve.tensor_tensor(zq, y[:, :, :, 0:L], rz[:, q % 2].unsqueeze(3).to_broadcast([P, 2, HY, L]),
                                  ALU.mult).then_inc(S["y_sb"], 1)

            def resid(b):
                dve.wait_ge(S["out_ps"], b.b + 2)
                dve.tensor_tensor(xa_all[:, bass.ds(b.b * 2, 2), :], bankB[:, 0:2 * C].rearrange("p (t c) -> p t c", t=2),
                                  xt[:, b.half], ALU.add).then_inc(S["xa_done"], 1)

            def step(b, n):
                if n:
                    norm(n)
                    kv(n)
                yevac(b, 0)
                if n:
                    red(n, 0)
                    red(n, 1)
                yevac(b, 1)
                if n:
                    for g in range(2, 6):
                        red(n, g)
                yevac(b, 2)
                if n:
                    red(n, 6)
                    red(n, 7)
                yevac(b, 3)
                resid(b)

            dve.sem_inc(S["xa_done"], 1)
            dve.sem_inc(S["red_done"], 1)
            dve.wait_ge(S["w_in"], 16 * NW)
            dve.wait_ge(S["consts"], 1)
            first = Batch(0, 0)
            norm(first)
            kv(first)
            for g in range(PAIRS):
                red(first, g)
            with dve.Fori(0, LOOP) as i:
                step(Batch(i, 0), Batch(i, 1))
                step(Batch(i, 1), Batch(i + 1, 0))
            step(Batch(LOOP, 0), Batch(LOOP, 1))
            step(Batch(LOOP, 1), None)

            done = 0

            def link(ins):
                nonlocal done
                done += 1
                ins.then_inc(S["rt"], 1)
                dve.wait_ge(S["rt"], done)

            def cast(v, shape):
                return v.to_broadcast(shape)

            full = [P, NT, E0]
            dve.wait_ge(S["kv_sb"], B)
            link(dve.tensor_copy(iota_f[:, :], iota_i[:, :]))
            link(dve.tensor_reduce(mx0[:, :], lg_all[:, :, :], AX.X, ALU.max))
            link(dve.tensor_tensor(lgs0[:, :, :], lg_all[:, :, :], cast(mx0[:, :].unsqueeze(2), full), ALU.subtract))
            link(dve.tensor_tensor(eq0[:, :, :], lg_all[:, :, :], cast(mx0[:, :].unsqueeze(2), full), ALU.is_equal))
            link(dve.tensor_scalar(pbase[:, :], iota_f[:, 0:E0], -1.0, float(E0), ALU.mult, ALU.add))
            link(dve.tensor_tensor(eq0[:, :, :], eq0[:, :, :], cast(pbase[:, :].unsqueeze(1), full), ALU.mult))
            link(dve.tensor_reduce(mx0[:, :], eq0[:, :, :], AX.X, ALU.max))
            link(dve.tensor_tensor(oh0[:, :, :], eq0[:, :, :], cast(mx0[:, :].unsqueeze(2), full), ALU.is_equal))
            dve.sem_inc(S["te_go"], 1)
            dve.wait_ge(S["ex0"], 1)
            link(dve.tensor_reduce(posf[:, :], lgs0[:, :, :], AX.X, ALU.add))
            link(dve.reciprocal(gate_all[:, :], posf[:, :]))
            dve.wait_ge(S["rk_ps"], 1)
            link(dve.tensor_copy(tot0[:, :, :], bankB[:, :].rearrange("p (n e) -> p n e", e=E0)))
            for e in range(E0):
                ins = dve.tensor_tensor_scan(cs0[:, :, e], cast(iota_f[:, 1:2], [P, NT]), tot0[:, :, e], 0.0, ALU.mult, ALU.add)
            link(ins)
            link(dve.tensor_scalar(cnt_i[:, 0, :], cs0[:, NT - 1, :], float(P - 1), None, ALU.add))
            link(dve.tensor_scalar(cnt_i[:, 1, :], cnt_i[:, 0, :], P.bit_length() - 1, None, ALU.arith_shift_right))
            link(dve.tensor_copy(ptile[:, :], cnt_i[:, 1, :]))
            link(dve.tensor_tensor_scan(pend[:, :], cast(iota_f[:, 1:2], [P, E0]), ptile[:, :], 0.0, ALU.mult, ALU.add))
            link(dve.tensor_tensor(pbase[:, :], pend[:, :], ptile[:, :], ALU.subtract))
            link(dve.tensor_scalar(pbase[:, :], pbase[:, :], float(P), None, ALU.mult))
            link(dve.tensor_tensor(cs0[:, :, :], cs0[:, :, :], tot0[:, :, :], ALU.subtract))
            link(dve.tensor_tensor(cs0[:, :, :], cs0[:, :, :], cast(pbase[:, :].unsqueeze(1), full), ALU.add))
            link(dve.tensor_tensor(cs0[:, :, :], bankA[:, :].rearrange("p (n e) -> p n e", e=E0), cs0[:, :, :], ALU.add))
            link(dve.tensor_tensor(cs0[:, :, :], cs0[:, :, :], oh0[:, :, :], ALU.mult))
            link(dve.tensor_reduce(posf[:, :], cs0[:, :, :], AX.X, ALU.add))
            link(dve.tensor_copy(pos_all[:, :], posf[:, :]))
            tiles = [P, TILES, E0]
            link(dve.tensor_tensor(tsel[:, :, :], cast(pend[:, :].unsqueeze(1), tiles), cast(iota_f[:, :].unsqueeze(2), tiles), ALU.is_le))
            link(dve.tensor_reduce(tef[:, :], tsel[:, :, :], AX.X, ALU.add))
            dve.tensor_scalar(te_i[:, :], tef[:, :], float(E0 - 1), None, ALU.min).then_inc(S["te_done"], 1)
            dve.wait_ge(S["te_done"], 1)

            def expert_tile(i, u, first):
                j = i * 2 + u
                e = dve.value_load(te_i[0:1, bass.ds(j, 1)], min_val=0, max_val=E0 - 1)
                if not first:
                    dve.wait_ge(S["h_dve"], j - 1)
                dve.tensor_copy(w1b[:, u, :], wall[:, bass.ds(e, 1), 0:F0 + KF].rearrange("p a c -> p (a c)")).then_inc(S["w1_sb"], 1)
                dve.wait_ge(S["w1_sb"], j + 1)
                dve.wait_ge(S["h_ps"], j + 1)
                for k in range(KF // 2, KF):
                    ins = dve.tensor_scalar(hT[:, u, k, :], hbank[u][:, 1, (k - KF // 2) * P:(k - KF // 2 + 1) * P],
                                            w1b[:, u, F0 + k:F0 + k + 1], 0.0, ALU.add, ALU.max)
                ins.then_inc(S["h_dve"], 1)
                if not first:
                    dve.wait_ge(S[f"ys_out{u}"], i * 16)
                dve.wait_ge(S["yt_ps"], j + 1)
                dve.tensor_copy(ysb[:, u], bankY[u][:, 0:C]).then_inc(S["yt_sb"], 1)

            for u in range(2):
                expert_tile(0, u, True)
            with dve.Fori(1, TILES // 2) as i:
                for u in range(2):
                    expert_tile(i, u, False)

            dve.sem_inc(S["res_done"], 1)
            dve.sem_inc(S["cnt_sb"], 1)
            for u in range(2):
                dve.sem_inc(S[f"res_out{u}"], 16)
                dve.sem_inc(S[f"tab_out{u}"], 16)
            dve.wait_ge(S["w1_in"], 16 * 14)
            dve.wait_ge(S["l1_consts"], 1)
            dve.wait_ge(S["pads"], 64)
            for k in range(2):
                dve.tensor_scalar(gates[:, k, :], block16[:, :], gcol[:, k:k + 1], None, ALU.mult)
            dve.tensor_scalar(wgqk[:, 1, :], wgqk[:, 1, :], 1.0 / CHUNK, None, ALU.mult)
            dve.tensor_scalar(wgv[:, :], wgv[:, :], 1.0 / CHUNK, None, ALU.mult)
            dve.tensor_scalar(wo1[:, :], wo1[:, :], 0.5, None, ALU.mult)
            dve.tensor_scalar(sdw[:, :, :], sdw[:, :, :], 0.5, None, ALU.mult).then_inc(S["wprep"], 1)

            def norm1(n, prior):
                u = n.half
                dve.wait_ge(S[f"yg{u}"], n.pair * 32 + 32)
                if prior:
                    dve.wait_ge(S["res_done"], n.b)
                for t in range(2):
                    ins = dve.scalar_tensor_tensor(x1[:, u, t, :], yg[:, u, t, :], gate_g[:, u, t:t + 1],
                                                   xa_all[:, bass.ds(n.b * 2 + t, 1), :].rearrange("p a c -> p (a c)"),
                                                   ALU.mult, ALU.add)
                ins.then_inc(S["x1_done"], 1)
                dve.wait_ge(S["x1_done"], n.b + 1)
                passed(dve)
                for t in range(2):
                    ins = dve.bn_stats(stats[:, t, :], x1[:, u, t, :])
                ins.then_inc(S["bn1"], 1)
                dve.wait_ge(S["bn1"], n.b + 1)
                passed(dve)
                for t in range(2):
                    ins = dve.bn_aggr(mv[:, t, :], stats[:, t, :])
                ins.then_inc(S["stats1"], 1)
                dve.wait_ge(S["rstd1"], n.b + 1)
                dve.wait_ge(S["stats1"], n.b + 1)
                dve.wait_ge(S[f"tab_out{u}"], n.pair * 16 + 16)
                for t in range(2):
                    ins = dve.tensor_scalar(tab[:, u, t, 0:C], x1[:, u, t, :], mv[:, t, 0:1], rstd[:, 1, t:t + 1],
                                            ALU.subtract, ALU.mult)
                ins.then_inc(S["xn1_done"], 1)

            def pool_latents(n):
                dve.wait_ge(S["tT_sb"], n.b * 2 + 1)
                dve.tensor_reduce(xp[:, n.half, :], xT1[:, n.half, :].rearrange("p (n k) -> p n k", k=CHUNK), AX.X,
                                  ALU.add).then_inc(S["xp_done"], 1)

            def spread(dst, src):
                return dve.tensor_tensor(dst, src.rearrange("p (n q) -> p n q", q=W).unsqueeze(2).to_broadcast([P, NB, 4, W]),
                                         headcol[:, :].unsqueeze(1).unsqueeze(3).to_broadcast([P, NB, 4, W]), ALU.mult)

            def queries(n):
                dve.wait_ge(S["qk_ps"], n.b + 1)
                spread(qx[:, n.half], bank[1][:, 0:T]).then_inc(S["qx_done"], 1)

            RSTEPS = 4

            def route(n):
                u = n.half
                dve.wait_ge(S["rt_ps"], n.b + 1)
                dve.tensor_copy(lg1[:, :, :], bank[0][:, 256:256 + 2 * (E1 + 1)].rearrange("p (t e) -> p t e", t=2)).then_inc(S["rt_sb"], 1)
                dve.wait_ge(S["rt_sb"], n.b + 1)
                passed(dve)
                for t in range(2):
                    ins = dve.max(mx8[:, t, :], lg1[:, t, 0:E1])
                ins.then_inc(S["rstep"], 1)
                dve.wait_ge(S["rstep"], n.b * RSTEPS + 1)
                passed(dve)
                for t in range(2):
                    ins = dve.match_replace(lgr[:, t, :], mx8[:, t, :], lg1[:, t, 0:E1], NEG)
                dve.tensor_tensor(shl[:, :, :], lg1[:, :, 0:E1], mx8[:, :, 0:1].to_broadcast([P, 2, E1]), ALU.subtract).then_inc(S["ex_in"], 1)
                dve.wait_ge(S["ex_in"], n.b + 1)
                dve.tensor_tensor(mb[:, u], lg1[:, :, 0:E1], lgr[:, :, :], ALU.not_equal).then_inc(S["M_done"], 1)

            def weigh(n):
                u = n.half
                dve.wait_ge(S["ex_done"], n.b + 1)
                dve.wait_ge(S["M_done"], n.b + 1)
                dve.tensor_tensor(exl[:, :, :], exl[:, :, :], mb[:, u], ALU.mult).then_inc(S["rstep"], 1)
                dve.wait_ge(S["rstep"], n.b * RSTEPS + 2)
                dve.tensor_reduce(wsum[:, 0, :], exl[:, :, :], AX.X, ALU.add).then_inc(S["rstep"], 1)
                dve.wait_ge(S["rstep"], n.b * RSTEPS + 3)
                dve.reciprocal(wsum[:, 1, :], wsum[:, 0, :]).then_inc(S["rstep"], 1)
                dve.wait_ge(S["rstep"], n.b * RSTEPS + 4)
                dve.tensor_scalar(sgc[:, u, :], tsg[:, :], 0.5, 0.5, ALU.mult, ALU.add)
                dve.tensor_tensor(tab[:, u, :, C:C + E1], exl[:, :, :], wsum[:, 1, :].unsqueeze(2).to_broadcast([P, 2, E1]),
                                  ALU.mult).then_inc(S["tab_done"], 1)

            def latents(n):
                u = n.half
                dve.wait_ge(S["g_ps"], n.b + 1)
                spread(gqx[:, u], bank[2][:, 0:T])
                dve.tensor_tensor(gvx[:, u], bank[2][:, 320:320 + 2 * DL].rearrange("p (k c) -> p k c", k=2),
                                  quadcol[:, 0:DL].unsqueeze(1).to_broadcast([P, 2, DL]), ALU.mult).then_inc(S["g_sb"], 1)

            def count(n):
                u = n.half
                dve.wait_ge(S["cnt_sb"], n.b + 1)
                dve.wait_ge(S["cnt_ps"], n.b + 1)
                dve.tensor_scalar(carry[:, u, :], bank[3][0:E1, T - 1:T], carry[:, 1 - u, :], None, ALU.add)
                dve.tensor_scalar(cnt_all[:, bass.ds(n.b * T, T)], bank[3][0:E1, 0:T], carry[:, 1 - u, :], None, ALU.add).then_inc(S["cnt_sb"], 1)

            def values(n):
                for k in range(2):
                    dve.wait_ge(S["v_ps"], n.b * 2 + (k + 1))
                    dve.tensor_tensor(vx[:, n.half, 4 * k:4 * k + 4, :], bank[k][:, :].rearrange("p (n c) -> p n c", c=C),
                                      quadcol[:, :].unsqueeze(1).to_broadcast([P, 4, C]), ALU.mult).then_inc(S["v_sb"], 1)

            def shift(b, g):
                k = g % 2
                s = (bankS, bankT)[k][:, :, 0:6 * NL].rearrange("p b (g k) -> p b g k", k=NL)
                dve.wait_ge(S["s2_ps"], b.b * 4 + (g + 1))
                dve.tensor_reduce(mxs[:, k, :].rearrange("p (b g) -> p b g", b=2), s, AX.X, ALU.max).then_inc(S["red2"], 1)
                dve.wait_ge(S["red2"], b.b * 4 + (g + 1))
                if g >= 2:
                    dve.wait_ge(S["tr_done"], b.b * 4 + (g - 1))
                dve.tensor_tensor(pr[:, k, :].rearrange("p (b g k) -> p b g k", b=2, k=NL), s,
                                  mxs[:, k, :].rearrange("p (b g) -> p b g", b=2).unsqueeze(3).to_broadcast([P, 2, 6, NL]),
                                  ALU.subtract).then_inc(S["sub_done"], 1)

            def turn(b, g):
                dve.wait_ge(S["exp2"], b.b * 4 + (g + 1))
                dve.transpose(pt[:, 2 * g:2 * g + 2].rearrange("p b g k q -> p (b g k q)"), pr[:, g % 2, :]).then_inc(S["tr_done"], 1)

            def shared(b):
                dve.wait_ge(S["tanh_sh"], b.b + 1)
                h = shT[:, :, :].rearrange("p k t -> p (k t)")
                dve.scalar_tensor_tensor(h, tsh[:, :], 1.0, bank[0][:, :], ALU.add, ALU.mult).then_inc(S["sh1_done"], 1)
                dve.wait_ge(S["sh1_done"], b.b + 1)
                dve.wait_ge(S["shu_ps"], b.b + 1)
                dve.tensor_tensor(h, h, bank[1][:, :], ALU.mult).then_inc(S["sh_sb"], 1)

            def finish(b):
                u = b.half
                dve.wait_ge(S["av_ps"], b.b + 1)
                dve.reciprocal(rdr[:, :], bank[3][0:DL, T:2 * T]).then_inc(S["rd_done"], 1)
                dve.wait_ge(S["rd_done"], b.b + 1)
                dve.tensor_tensor(remn[:, :], bank[3][0:DL, 0:T], rdr[:, :], ALU.mult).then_inc(S["remn_done"], 1)
                dve.reciprocal(rdl[:, :], bank[2][:, T:2 * T])
                dve.wait_ge(S["gate_sb"], b.b + 1)
                dve.scalar_tensor_tensor(at1[:, :], tg[:, 0, :], 1.0, bank[2][:, 0:T], ALU.add, ALU.mult).then_inc(S["comb"], 1)
                dve.wait_ge(S["comb"], b.b * 3 + 1)
                dve.tensor_tensor(at1[:, :], at1[:, :], rdl[:, :], ALU.mult).then_inc(S["comb"], 1)
                dve.wait_ge(S["rem2_ps"], b.b + 1)
                dve.scalar_tensor_tensor(at2[:, :], tg[:, 1, :], 1.0, bank[3][:, 0:T], ALU.add, ALU.mult).then_inc(S["comb"], 1)
                dve.wait_ge(S["comb"], b.b * 3 + 3)
                dve.tensor_tensor(aT[:, :], at1[:, :], at2[:, :], ALU.add).then_inc(S["aT_done"], 1)
                dve.wait_ge(S["shd_ps"], b.b + 1)
                dve.wait_ge(S[f"res_out{u}"], b.pair * 16 + 16)
                for t in range(2):
                    ins = dve.scalar_tensor_tensor(res[:, u, t, :], bank[1][:, t * C:(t + 1) * C], sgc[:, u, t:t + 1],
                                                   x1[:, u, t, :], ALU.mult, ALU.add)
                ins.then_inc(S["r1_done"], 1)
                dve.wait_ge(S["r1_done"], b.b + 1)
                dve.wait_ge(S["ao_ps"], b.b + 1)
                dve.tensor_tensor(res[:, u], bank[2][:, 0:2 * C].rearrange("p (t c) -> p t c", t=2), res[:, u],
                                  ALU.add).then_inc(S["res_done"], 1)

            def step1(b, n):
                if b:
                    shift(b, 0)
                if n:
                    norm1(n, b is not None)
                if b:
                    shift(b, 1)
                    turn(b, 0)
                if n:
                    pool_latents(n)
                    queries(n)
                    route(n)
                if b:
                    shift(b, 2)
                    turn(b, 1)
                if n:
                    latents(n)
                    count(n)
                    weigh(n)
                if b:
                    shift(b, 3)
                    turn(b, 2)
                if n:
                    values(n)
                if b:
                    turn(b, 3)
                    shared(b)
                    finish(b)

            step1(None, Batch(0, 0))
            with dve.Fori(0, LOOP) as i:
                step1(Batch(i, 0), Batch(i, 1))
                step1(Batch(i, 1), Batch(i + 1, 0))
            step1(Batch(LOOP, 0), Batch(LOOP, 1))
            step1(Batch(LOOP, 1), None)
            steps4 = 0

            def link4(ins):
                nonlocal steps4
                steps4 += 1
                ins.then_inc(S["sel"], 1)
                dve.wait_ge(S["sel"], steps4)

            for u in range(2):
                dve.wait_ge(S[f"res_out{u}"], 16 * (B // 2) + 16)
                dve.wait_ge(S[f"tab_out{u}"], 16 * (B // 2) + 16)
            dve.wait_ge(S["cnt_sb"], B + 1)
            dve.wait_ge(S["slots"], 1)
            dve.tensor_copy(slot_f[:, 0:1], slot_i[:, :])
            link4(dve.tensor_scalar(slot_f[:, 1:2], slot_i[:, :], float(NT), None, ALU.mult))
            link4(dve.tensor_tensor(full_tiles[:, :, :],
                                    cnt_all[:, :].rearrange("e (n p) -> e n p", p=P)[:, :, P - 1].unsqueeze(1).to_broadcast([E1, CAP, NT]),
                                    iota_f[0:E1, 0:CAP].unsqueeze(2).to_broadcast([E1, CAP, NT]), ALU.is_le))
            link4(dve.tensor_reduce(tile_row[:, 0, :], full_tiles[:, :, :], AX.X, ALU.add))
            link4(dve.tensor_scalar(tile_row[:, 0, :], tile_row[:, 0, :], float(NT - 1), None, ALU.min))
            dve.tensor_scalar(tile_row[:, 1, :], tile_row[:, 0, :], slot_f[:, 1:2], None, ALU.add).then_inc(S["tr4"], 1)
            dve.wait_ge(S["tr4"], 2)
            dve.tensor_scalar(tile_at[:, :], bank[0][0:CAP, 0:E1], float(P), None, ALU.mult)
            dve.tensor_copy(row_at[:, :], bank[0][0:CAP, E1:2 * E1]).then_inc(S["f4"], 1)
            dve.wait_ge(S["f4"], 1)

            def slots(g):
                u = g.half
                at = steps4
                dve.wait_ge(S[f"cg_in{u}"], g.pair * (16 * GE) + 16 * GE)
                dve.tensor_scalar(below[:, :, :], cg[:, u], slot_f[:, 0:1], None, ALU.is_le).then_inc(S["sel"], 1)
                dve.wait_ge(S["sel"], g.b * 4 + (at + 1))
                dve.tensor_reduce(tok[:, 0, :], below[:, :, :], AX.X, ALU.add).then_inc(S["sel"], 1)
                dve.wait_ge(S["sel"], g.b * 4 + (at + 2))
                dve.tensor_tensor(tok[:, 1, :], tok[:, 0, :], tile_at[:, bass.ds(g.b * GE, GE)], ALU.add).then_inc(S["sel"], 1)
                dve.wait_ge(S["sel"], g.b * 4 + (at + 3))
                dve.tensor_scalar(dump[:, :], tok[:, 1, :], float(B * T), slot_f[:, 0:1], ALU.is_ge, ALU.mult).then_inc(S["sel"], 1)
                dve.wait_ge(S["sel"], g.b * 4 + (at + 4))
                dve.tensor_tensor(sidx[:, u, :], tok[:, 1, :], dump[:, :], ALU.add).then_inc(S["sidx_done"], 1)

            def experts(g):
                u = g.half
                dve.wait_ge(S[f"xg_in{u}"], g.pair * (16 * GE) + 16 * GE)
                dve.tensor_copy(wblk[:, u, :].rearrange("p (e k) -> p e k", k=GE), xg[:, u, :, bass.ds(g.b * GE + C, GE)]).then_inc(S["wblk_sb"], 1)
                dve.wait_ge(S["the_sb"], g.b + 1)
                dve.scalar_tensor_tensor(ae[:, :], the[:, :], 1.0, bank[2][0:IE, :], ALU.add, ALU.mult).then_inc(S["ae1"], 1)
                dve.wait_ge(S["ae1"], g.b + 1)
                dve.tensor_tensor(ae[:, :], ae[:, :], bank[3][0:IE, :], ALU.mult).then_inc(S["ae_sb"], 1)
                dve.wait_ge(S["oe_ps"], g.b + 1)
                dve.wait_ge(S["wblk_sb"], g.b + 1)
                for k in range(2):
                    diag = wblk[:, u, 4 * k * (GE + 1):4 * k * (GE + 1) + 3 * (GE + 1) + 1:GE + 1]
                    ins = dve.scalar_tensor_tensor(yo[:, u, 4 * k:4 * k + 4, :], bankS[0:CAP, k, :].rearrange("p (e c) -> p e c", c=C), 0.5,
                                                   diag.unsqueeze(2).to_broadcast([CAP, 4, C]), ALU.mult, ALU.mult)
                ins.then_inc(S["yo_sb"], 1)

            def step4(g, n):
                if n:
                    slots(n)
                if g:
                    experts(g)

            step4(None, Batch(0, 0))
            with dve.Fori(0, NG // 2 - 1) as i:
                step4(Batch(i, 0), Batch(i, 1))
                step4(Batch(i, 1), Batch(i + 1, 0))
            step4(Batch(NG // 2 - 1, 0), Batch(NG // 2 - 1, 1))
            step4(Batch(NG // 2 - 1, 1), None)

        @block.scalar
        def _(act):
            def xnt(n):
                act.wait_ge(S["xnT_ps"], n.b + 1)
                act.copy(xnT[:, n.half, :], bankA[:, 0:T]).then_inc(S["xnT_sb"], 1)

            def qevac(n, r):
                act.wait_ge(S["q_ps"], n.b * 4 + (r + 1))
                for k in range(2):
                    j = 2 * r + k
                    act.activation(qT[:, n.half, j, :], bankA[:, k * T:(k + 1) * T], ACT.Identity,
                                   bias=bd[:, j:j + 1]).then_inc(S["q_sb"], 1)

            def mt(n):
                act.wait_ge(S["mT_ps"], n.b + 1)
                act.copy(mT[:, n.half, :], bankB[0:H, 0:T]).then_inc(S["mT_sb"], 1)

            def probs(b, g):
                for e in range(2):
                    h = 2 * g + e
                    act.wait_ge(S["st_ps"], b.b * H + (h + 1))
                    if h >= 4:
                        act.wait_ge(S["av_done"], b.b * H + (h - 3))
                    act.activation(pT[:, h % 4, :], bankT[:, e, 0:384], ACT.Exp, scale=SCALE0).then_inc(S["exp_done"], 1)

            def zt(b):
                act.wait_ge(S["out_ps"], b.b + 1)
                for r, (src, n, rows) in enumerate(((bankA, 2, P), (bankB, 2, P), (bankA, 1, LP))):
                    act.wait_ge(S["zt_ps"], b.b * 3 + (r + 1))
                    act.copy(zT[0:rows, 2 * r:2 * r + n, :], src[0:rows, 0:n * T].rearrange("p (k t) -> p k t", k=n)).then_inc(S["zt_sb"], 1)

            def step(b, n):
                for g in range(PAIRS):
                    probs(b, g)
                    if n and g == 0:
                        xnt(n)
                    if n and 1 <= g <= 4:
                        qevac(n, g - 1)
                if n:
                    mt(n)
                zt(b)

            act.wait_ge(S["w_in"], 16 * NW)
            first = Batch(0, 0)
            xnt(first)
            for r in range(4):
                qevac(first, r)
            mt(first)
            with act.Fori(0, LOOP) as i:
                step(Batch(i, 0), Batch(i, 1))
                step(Batch(i, 1), Batch(i + 1, 0))
            step(Batch(LOOP, 0), Batch(LOOP, 1))
            step(Batch(LOOP, 1), None)

            act.wait_ge(S["te_go"], 1)
            act.activation(lgs0[:, :, :], lgs0[:, :, :], ACT.Exp).then_inc(S["ex0"], 1)

            def expert_tile(i, u):
                j = i * 2 + u
                act.wait_ge(S["xsT_ps"], j + 1)
                act.copy(xsT[:, u, :], bank[u][:, 0:P]).then_inc(S["xsT_sb"], 1)
                act.wait_ge(S["h_ps"], j + 1)
                for k in range(KF // 2):
                    ins = act.activation(hT[:, u, k, :], hbank[u][:, 0, k * P:(k + 1) * P], ACT.Relu,
                                         bias=w1b[:, u, F0 + k:F0 + k + 1])
                ins.then_inc(S["h_act"], 1)

            with act.Fori(0, TILES // 2) as i:
                for u in range(2):
                    expert_tile(i, u)

            SCALE1 = float((C // H) ** -0.5)

            def soft(b, g):
                act.wait_ge(S["sub_done"], b.b * 4 + (g + 1))
                act.activation(pr[:, g % 2, :], pr[:, g % 2, :], ACT.Exp, scale=SCALE1).then_inc(S["exp2"], 1)

            def xt1(n):
                act.wait_ge(S["tT_ps"], n.b + 1)
                act.copy(xT1[:, n.half, :], bank[0][:, 0:T]).then_inc(S["tT_sb"], 1)
                act.copy(xr[:, n.half], bank[0][:, 0:T].rearrange("p (n q) -> p n q", q=W).unsqueeze(2).to_broadcast([P, NB, 4, W])).then_inc(S["tT_sb"], 1)
                act.wait_ge(S["xp_done"], n.b + 1)
                act.copy(xpr[:, n.half], xp[:, n.half, :].rearrange("p (n q) -> p n q", q=W).unsqueeze(2).to_broadcast([P, 2, 4, W])).then_inc(S["xpr_sb"], 1)

            def keys(n):
                u = n.half
                act.wait_ge(S["qx_done"], n.b + 1)
                act.copy(qs[:, u, :], bank[1][:, 0:T])
                for g in range(4):
                    q = slice(W * g, W * g + W)
                    ins = act.copy(km[q, u, g, W:W + T], bank[1][q, T:2 * T])
                ins.then_inc(S["kt_sb"], 1)

            def latent_keys(n):
                act.wait_ge(S["g_sb"], n.b + 1)
                for g in range(2):
                    q = slice(W * g, W * g + W)
                    ins = act.copy(gkm[q, n.half, g, :], bank[2][q, 256:256 + NL])
                ins.then_inc(S["gk_sb"], 1)

            def route(n):
                act.wait_ge(S["ex_in"], n.b + 1)
                act.activation(exl[:, :, :], shl[:, :, :], ACT.Exp)
                act.activation(tsg[:, :], lg1[:, :, E1], ACT.Tanh, scale=0.5).then_inc(S["ex_done"], 1)

            def shared(b):
                act.wait_ge(S["shg_ps"], b.b + 1)
                act.activation(tsh[:, :], bank[0][:, :], ACT.Tanh, scale=0.5).then_inc(S["tanh_sh"], 1)

            def gate(b):
                act.wait_ge(S["gate_ps"], b.b + 1)
                act.activation(tg[:, :, :].rearrange("p k t -> p (k t)"), bank[0][:, :], ACT.Tanh, scale=0.5).then_inc(S["gate_sb"], 1)

            def step1(b, n):
                if b:
                    soft(b, 0)
                if n:
                    xt1(n)
                if b:
                    soft(b, 1)
                if n:
                    keys(n)
                    route(n)
                if b:
                    soft(b, 2)
                if n:
                    latent_keys(n)
                if b:
                    soft(b, 3)
                    shared(b)
                    gate(b)

            act.wait_ge(S["wprep"], 1)
            step1(None, Batch(0, 0))
            with act.Fori(0, LOOP) as i:
                step1(Batch(i, 0), Batch(i, 1))
                step1(Batch(i, 1), Batch(i + 1, 0))
            step1(Batch(LOOP, 0), Batch(LOOP, 1))
            step1(Batch(LOOP, 1), None)
            def experts(g):
                u = g.half
                act.wait_ge(S["xgT_ps"], g.b + 1)
                act.copy(xgT[:, u, :], bank[1][:, :]).then_inc(S["xgT_sb"], 1)
                act.wait_ge(S["gu_ps"], g.b + 1)
                act.activation(the[:, :], bank[2][0:IE, :], ACT.Tanh, scale=0.5).then_inc(S["the_sb"], 1)

            with act.Fori(0, NG // 2) as i:
                experts(Batch(i, 0))
                experts(Batch(i, 1))

        @block.tensor
        def _(pe):
            def xnt(n):
                pe.wait_ge(S["xn_done"], n.b + 1)
                for t in range(2):
                    ins = pe.transpose(bankA[:, t * P:(t + 1) * P], xn[:, n.half, t, :], ident[:, :])
                ins.then_inc(S["xnT_ps"], 1)

            def kv(n, prior):
                u = n.half
                pe.wait_ge(S["xnT_sb"], n.b + 1)
                if prior:
                    pe.wait_ge(S["xa_done"], n.b)
                pe.matmul(bankB[:, 0:T], lw[:, :, :].rearrange("p e l -> p (e l)"), xnT[:, u, :], start=True, stop=True)
                for t in range(2):
                    tok = xnT[:, u, t * P:(t + 1) * P]
                    pe.matmul(bankB[:, 256 + t * L:256 + (t + 1) * L], tok, lw[:, 0, 0:L], start=True, stop=False)
                    pe.matmul(bankB[:, 256 + t * L:256 + (t + 1) * L], ones[:, :], lbrow[:, :], start=False, stop=True)
                    pe.matmul(bankB[:, 384 + t * E0:384 + (t + 1) * E0], tok, wr[:, :], start=True, stop=False)
                    ins = pe.matmul(bankB[:, 384 + t * E0:384 + (t + 1) * E0], ones[:, :], brow[:, :], start=False, stop=True)
                ins.then_inc(S["kv_ps"], 1)

            def qproj(n, r):
                if r >= 1:
                    pe.wait_ge(S["q_sb"], n.b * PAIRS + 2 * r)
                for k in range(2):
                    ins = pe.matmul(bankA[:, k * T:(k + 1) * T], wd[:, 2 * r + k, :, :].rearrange("p e l -> p (e l)"),
                                    xnT[:, n.half, :], start=True, stop=True)
                ins.then_inc(S["q_ps"], 1)

            def smax(n, g):
                u = n.half
                pe.wait_ge(S["q_sb"], n.b * PAIRS + (g + 1))
                if g == 0:
                    pe.wait_ge(S["kv_sb"], n.b + 1)
                pe.wait_ge(S["red_done"], n.b * PAIRS + (g + 1))
                for e in range(2):
                    r = slice(LP * e, LP * e + L)
                    s = bankS[:, e, :]
                    pe.matmul(s[:, 0:128], qT[r, u, g, 0:P], kT[r, u, 0:P], start=True, stop=False)
                    pe.matmul(s[:, 0:128], identb[:, :], maskq[:, :], start=False, stop=True)
                    pe.matmul(s[:, 128:384], qT[r, u, g, P:T], kT[r, u, :], start=True, stop=False)
                    ins = pe.matmul(s[:, 256:384], identb[:, :], maskq[:, :], start=False, stop=True)
                ins.then_inc(S["s_ps"], 1)

            def mt(n):
                pe.wait_ge(S["red_done"], n.b * PAIRS + (PAIRS + 1))
                for t in range(2):
                    ins = pe.transpose(bankB[0:H, t * P:(t + 1) * P], mneg[:, n.half, t, :], ident[:, :])
                ins.then_inc(S["mT_ps"], 1)

            def st(b, g):
                u = b.half
                if g == 0:
                    pe.wait_ge(S["mT_sb"], b.b + 1)
                for e in range(2):
                    h = 2 * g + e
                    if h >= 2:
                        pe.wait_ge(S["exp_done"], b.b * H + (h - 1))
                    r = slice(LP * e, LP * e + L)
                    s = bankT[:, e, :]
                    for k, cols in ((0, slice(0, 256)), (1, slice(256, 384))):
                        qs = slice(k * P, T)
                        pe.matmul(s[:, cols], kT[r, u, k * P:(k + 1) * P], qT[r, u, g, qs], start=True, stop=False)
                        pe.matmul(s[:, cols], headrow[:, h, :], mT[:, u, qs], start=False, stop=False)
                        ins = pe.matmul(s[:, cols.start:cols.start + P], identb[:, :], maskk[:, :], start=False, stop=True)
                    ins.then_inc(S["st_ps"], 1)

            def av(b, g):
                u = b.half
                q = g // 2
                if g in (4, 6):
                    pe.wait_ge(S["y_sb"], b.b * 4 + (q - 1))
                y = bankY[q % 2][:, 0:2 * HY * (L + 1)].rearrange("p (t h l) -> p t h l", t=2, h=HY)
                for e in range(2):
                    h = 2 * g + e
                    pe.wait_ge(S["exp_done"], b.b * H + (h + 1))
                    p = pT[:, h % 4, :]
                    pe.matmul(y[:, 0, h % HY, :], p[:, 0:128], vaug[:, u, 0, :], start=True, stop=True)
                    pe.matmul(y[:, 1, h % HY, :], p[:, 128:256], vaug[:, u, 0, :], start=True, stop=False)
                    pe.matmul(y[:, 1, h % HY, :], p[:, 256:384], vaug[:, u, 1, :], start=False, stop=True).then_inc(S["av_done"], 1)

            def zt(b, n):
                pe.wait_ge(S["y_sb"], b.b * 4 + 4)
                if n:
                    pe.wait_ge(S["mT_sb"], n.b + 1)
                for r, (dst, k0, rows) in enumerate(((bankA, 0, P), (bankB, 2, P), (bankA, 4, LP))):
                    if r == 2:
                        pe.wait_ge(S["zt_sb"], b.b * 3 + 1)
                        passed(pe)
                    for k in range(k0, min(k0 + 2, NC)):
                        for t in range(2):
                            ins = pe.transpose(dst[0:rows, (k - k0) * T + t * P:(k - k0) * T + (t + 1) * P],
                                               z[:, t, k * P:k * P + rows], ident[:, :])
                    ins.then_inc(S["zt_ps"], 1)
                pe.wait_ge(S["zt_sb"], b.b * 3 + 3)
                for t in range(2):
                    o = bankB[:, t * C:(t + 1) * C]
                    for k in range(NC):
                        rows = P if k < 4 else LP
                        pe.matmul(o, zT[0:rows, k, t * P:(t + 1) * P], ow[0:rows, k, :], start=(k == 0), stop=False)
                    ins = pe.matmul(o, ones[:, :], ob[:, :], start=False, stop=True)
                ins.then_inc(S["out_ps"], 1)

            def step(b, n):
                for g in range(PAIRS):
                    st(b, g)
                    if g >= 1:
                        av(b, g - 1)
                    if n and g == 0:
                        xnt(n)
                    if n and g == 1:
                        kv(n, True)
                    if n and 1 <= g <= 4:
                        qproj(n, g - 1)
                    if n and g >= 3:
                        for s in ((0, 1), (2, 3), (4, 5), (6,), (7,))[g - 3]:
                            smax(n, s)
                av(b, PAIRS - 1)
                if n:
                    mt(n)
                zt(b, n)

            pe.sem_inc(S["out_ps"], 1)
            pe.wait_ge(S["w_in"], 16 * NW)
            pe.wait_ge(S["consts"], 1)
            first = Batch(0, 0)
            xnt(first)
            kv(first, False)
            for r in range(4):
                qproj(first, r)
            for g in range(PAIRS):
                smax(first, g)
            mt(first)
            with pe.Fori(0, LOOP) as i:
                step(Batch(i, 0), Batch(i, 1))
                step(Batch(i, 1), Batch(i + 1, 0))
            step(Batch(LOOP, 0), Batch(LOOP, 1))
            step(Batch(LOOP, 1), None)

            pe.wait_ge(S["te_go"], 1)
            pe.wait_ge(S["xa_done"], B + 1)
            flat = oh0[:, :, :].rearrange("p n e -> p (n e)")
            pe.matmul(bankA[:, :], strict[:, :], flat, start=True, stop=True)
            pe.matmul(bankB[:, :], onesb[:, :], flat, start=True, stop=True).then_inc(S["rk_ps"], 1)
            pe.wait_ge(S["te_done"], 1)

            def expert_tile(i, u, first):
                j = i * 2 + u
                e = pe.value_load(te_i[0:1, bass.ds(j, 1)], min_val=0, max_val=E0 - 1)
                pe.wait_ge(S[f"xs_in{u}"], i * 16 + 16)
                pe.transpose(bank[u][:, 0:P], xsb[:, u, :], ident[:, :]).then_inc(S["xsT_ps"], 1)
                pe.wait_ge(S["w1_sb"], j + 1)
                pe.wait_ge(S["xsT_sb"], j + 1)
                for k in range(KF):
                    c = (k % 2) * P
                    ins = pe.matmul(hbank[u][:, k // 2, c:c + P], w1b[:, u, k * P:(k + 1) * P], xsT[:, u, :], start=True, stop=True)
                ins.then_inc(S["h_ps"], 1)
                pe.wait_ge(S["h_act"], j + 1)
                pe.wait_ge(S["h_dve"], j + 1)
                if not first:
                    pe.wait_ge(S["yt_sb"], j - 1)
                for k in range(KF):
                    pe.matmul(bankY[u][:, 0:C], hT[:, u, k, :],
                              wall[:, bass.ds(e, 1), F0 + KF + k * C:F0 + KF + (k + 1) * C].rearrange("p a c -> p (a c)"),
                              start=(k == 0), stop=False)
                pe.matmul(bankY[u][:, 0:C], ones[:, :], b2row[:, bass.ds(e, 1), :].rearrange("p a c -> p (a c)"),
                          start=False, stop=True).then_inc(S["yt_ps"], 1)

            for u in range(2):
                expert_tile(0, u, True)
            with pe.Fori(1, TILES // 2) as i:
                for u in range(2):
                    expert_tile(i, u, False)

            def scores(b, g):
                u = b.half
                if g == 0:
                    pe.wait_ge(S["kt_sb"], b.b + 1)
                    pe.wait_ge(S["gk_sb"], b.b + 1)
                else:
                    pe.wait_ge(S["s2_ps"], b.b * 4 + g)
                if g >= 2:
                    pe.wait_ge(S["sub_done"], b.b * 4 + (g - 1))
                for k in range(2):
                    n = 2 * g + k
                    s = (bankS, bankT)[g % 2][:, k, :]
                    pe.matmul(s[:, 0:4 * NL], identb[:, :], maskl[:, min(n, 1), :].unsqueeze(1).to_broadcast([P, 4, NL]), start=True, stop=False)
                    for h in range(4):
                        pe.matmul(s[:, h * NL:(h + 1) * NL], qx[:, u, n].rearrange("p h q -> p (h q)"),
                                  km[:, u, h, n * W:n * W + 2 * W], start=False, stop=(h == 3))
                    pe.matmul(s[:, 4 * NL:6 * NL], identb[:, :], maskr[:, n, :].unsqueeze(1).to_broadcast([P, 2, NL]), start=True, stop=False)
                    for h in range(2):
                        ins = pe.matmul(s[:, (4 + h) * NL:(5 + h) * NL], gqx[:, u, n].rearrange("p h q -> p (h q)"),
                                        gkm[:, u, h, :], start=False, stop=(h == 1))
                ins.then_inc(S["s2_ps"], 1)

            def xt1(n):
                pe.wait_ge(S["xn1_done"], n.b + 1)
                for t in range(2):
                    ins = pe.transpose(bank[0][:, t * P:(t + 1) * P], tab[:, n.half, t, 0:C], ident[:, :])
                ins.then_inc(S["tT_ps"], 1)

            def qk(n, prior):
                u = n.half
                pe.wait_ge(S["tT_sb"], n.b * 2 + 2)
                if prior:
                    pe.wait_ge(S["res_done"], n.b)
                for k in range(2):
                    ins = pe.matmul(bank[1][:, k * T:(k + 1) * T], wqk[:, k, :], xT1[:, u, :], start=True, stop=True)
                ins.then_inc(S["qk_ps"], 1)
                for t in range(2):
                    c = 256 + t * (E1 + 1)
                    ins = pe.matmul(bank[0][:, c:c + E1 + 1], xT1[:, u, t * P:(t + 1) * P], gw[:, :], start=True, stop=True)
                ins.then_inc(S["rt_ps"], 1)

            def latents(n):
                u = n.half
                pe.wait_ge(S["xpr_sb"], n.b + 1)
                pe.matmul(bank[2][:, 0:T], wgqk[:, 0, :], xT1[:, u, :], start=True, stop=True)
                pe.matmul(bank[2][:, T:T + NL], wgqk[:, 1, :], xp[:, u, :], start=True, stop=True)
                for k in range(2):
                    ins = pe.matmul(bank[2][:, 320 + k * DL:320 + (k + 1) * DL], xpr[:, u, k].rearrange("p r q -> p (r q)"), wgv[:, :], start=True, stop=True)
                ins.then_inc(S["g_ps"], 1)

            def count(n):
                pe.wait_ge(S["M_done"], n.b + 1)
                pe.matmul(bank[3][0:E1, 0:T], mb[:, n.half, 0, :], upto[:, :, :].rearrange("p k t -> p (k t)"), start=True, stop=False)
                pe.matmul(bank[3][0:E1, P:T], mb[:, n.half, 1, :], upto[:, 0, :], start=False, stop=True).then_inc(S["cnt_ps"], 1)

            def values(n):
                u = n.half
                pe.wait_ge(S["kt_sb"], n.b + 1)
                pe.wait_ge(S["rt_sb"], n.b + 1)
                for k in range(2):
                    for j in range(4):
                        ins = pe.matmul(bank[k][:, j * C:(j + 1) * C], xr[:, u, 4 * k + j].rearrange("p r q -> p (r q)"), wv[:, :], start=True, stop=True)
                    ins.then_inc(S["v_ps"], 1)

            def shared_up(b, last):
                u = b.half
                pe.wait_ge(S["v_sb"], b.b * 2 + (2 if last else 4))
                for k in range(2):
                    for j in range(2):
                        c = (2 * k + j) * P
                        ins = pe.matmul(bank[k][:, j * T:(j + 1) * T], sgu[:, c:c + P], xT1[:, u, :], start=True, stop=True)
                    ins.then_inc(S[("shg_ps", "shu_ps")[k]], 1)

            def attend(b, last):
                u = b.half
                pe.wait_ge(S["tr_done"], b.b * 4 + 4)
                pe.wait_ge(S["gk_sb"], b.b + (1 if last else 2))
                pe.wait_ge(S["cnt_sb"], b.b + (2 if last else 3))
                for h in range(4):
                    q = slice(W * h, W * h + W)
                    if h < 2:
                        for k in range(2):
                            pe.matmul(bank[3][q, 0:T], gvx[:, u, k, q], pt[:, :, 4 + h, k, :], start=(k == 0), stop=(k == 1))
                        for k in range(2):
                            pe.matmul(bank[3][q, T:2 * T], quadcol[:, 0:W], pt[:, :, 4 + h, k, :], start=(k == 0), stop=(k == 1))
                    for n in range(NB):
                        o = bank[2][q, n * W:(n + 1) * W]
                        if n:
                            pe.matmul(o, vx[:, u, n - 1, q], pt[:, n, h, 0, :], start=True, stop=False)
                        pe.matmul(o, vx[:, u, n, q], pt[:, n, h, 1, :], start=(n == 0), stop=True)
                    for k in range(2):
                        ins = pe.matmul(bank[2][q, T:2 * T], quadcol[:, 0:W], pt[:, :, h, k, :], start=(k == 0), stop=(k == 1))
                ins.then_inc(S["av_ps"], 1)

            def finish(b):
                u = b.half
                pe.wait_ge(S["sh1_done"], b.b + 1)
                for k in range(2):
                    ins = pe.matmul(bank[0][:, k * T:(k + 1) * T], gates[:, k, :], qs[:, u, :], start=True, stop=True)
                ins.then_inc(S["gate_ps"], 1)
                pe.wait_ge(S["remn_done"], b.b + 1)
                pe.matmul(bank[3][:, 0:T], wro[:, :], remn[:, :], start=True, stop=True).then_inc(S["rem2_ps"], 1)
                pe.wait_ge(S["sh_sb"], b.b + 1)
                for t in range(2):
                    for k in range(2):
                        ins = pe.matmul(bank[1][:, t * C:(t + 1) * C], shT[:, k, t * P:(t + 1) * P], sdw[:, k, :], start=(k == 0), stop=(k == 1))
                ins.then_inc(S["shd_ps"], 1)
                pe.wait_ge(S["aT_done"], b.b + 1)
                for t in range(2):
                    ins = pe.matmul(bank[2][:, t * C:(t + 1) * C], aT[:, t * P:(t + 1) * P], wo1[:, :], start=True, stop=True)
                ins.then_inc(S["ao_ps"], 1)

            def step1(b, n):
                if b:
                    scores(b, 0)
                if n:
                    xt1(n)
                if b:
                    scores(b, 1)
                if n:
                    qk(n, b is not None)
                if b:
                    scores(b, 2)
                if n:
                    latents(n)
                    count(n)
                if b:
                    scores(b, 3)
                if n:
                    values(n)
                if b:
                    shared_up(b, n is None)
                    attend(b, n is None)
                    finish(b)

            pe.wait_ge(S["wprep"], 1)
            step1(None, Batch(0, 0))
            with pe.Fori(0, LOOP) as i:
                step1(Batch(i, 0), Batch(i, 1))
                step1(Batch(i, 1), Batch(i + 1, 0))
            step1(Batch(LOOP, 0), Batch(LOOP, 1))
            step1(Batch(LOOP, 1), None)
            pe.wait_ge(S["tr4"], 1)
            pe.transpose(bank[0][0:CAP, 0:E1], tile_row[:, 0, :], ident[0:E1, 0:E1])
            pe.transpose(bank[0][0:CAP, E1:2 * E1], tile_row[:, 1, :], ident[0:E1, 0:E1]).then_inc(S["tr4"], 1)

            def experts(g):
                u = g.half
                pe.wait_ge(S[f"xg_in{u}"], g.pair * (16 * GE) + 16 * GE)
                passed(pe)
                for e in range(GE):
                    ins = pe.transpose(bank[1][:, e * CAP:(e + 1) * CAP], xg[:, u, e, 0:C], ident[0:CAP, 0:CAP])
                ins.then_inc(S["xgT_ps"], 1)
                pe.wait_ge(S["xgT_sb"], g.b + 1)
                pe.wait_ge(S[f"we_in{u}"], g.pair * 32 + 32)
                for k in range(2):
                    for e in range(GE):
                        ins = pe.matmul(bank[2 + k][0:IE, e * CAP:(e + 1) * CAP], wge[:, u, e, k * IE:(k + 1) * IE],
                                        xgT[:, u, e * CAP:(e + 1) * CAP], start=True, stop=True)
                ins.then_inc(S["gu_ps"], 1)
                pe.wait_ge(S["ae_sb"], g.b + 1)
                passed(pe)
                for e in range(GE):
                    ins = pe.matmul(bankS[0:CAP, e // 4, (e % 4) * C:(e % 4 + 1) * C], ae[:, e * CAP:(e + 1) * CAP],
                                    wde[:, u, e, :], start=True, stop=True)
                ins.then_inc(S["oe_ps"], 1)

            with pe.Fori(0, NG // 2) as i:
                experts(Batch(i, 0))
                experts(Batch(i, 1))


_INS = ['L0_attn_x', 'L0_attn_latent_w', 'L0_attn_latent_b', 'L0_attn_Wd_w', 'L0_attn_Wd_b', 'L0_attn_out_w',
        'L0_attn_out_b', 'L0_ffn_Wr', 'L0_ffn_br', 'L0_ffn_W1', 'L0_ffn_b1', 'L0_ffn_W2', 'L0_ffn_b2', 'L1_attn_wq',
        'L1_attn_wk', 'L1_attn_wv', 'L1_attn_wgq', 'L1_attn_wgk', 'L1_attn_wgv', 'L1_attn_r_out_w',
        'L1_attn_gate_local_w', 'L1_attn_gate_remote_w', 'L1_attn_w_out', 'L1_ffn_gate_w', 'L1_ffn_shared_gate_w',
        'L1_ffn_shared_gate_up_w', 'L1_ffn_shared_down_w', 'L1_ffn_expert_gate_up_w', 'L1_ffn_expert_down_w']


def kernel(**inputs):
    import numpy as _np
    import concourse.bacc as _bacc
    from concourse import mybir as _mybir
    from concourse.bass_utils import run_bass_kernel_spmd as _run

    nc = _bacc.Bacc("TRN2", target_bir_lowering=False, num_devices=1)
    arrays, aps = {}, {}
    for name in _INS:
        v = _np.ascontiguousarray(inputs[name])
        arrays[f"in_{name}"] = v
        aps[name] = nc.dram_tensor(f"in_{name}", v.shape, _mybir.dt.from_np(v.dtype), kind="ExternalInput").ap()
    shape = inputs["L0_attn_x"].shape
    out = nc.dram_tensor("out_x", shape, _mybir.dt.float32, kind="ExternalOutput").ap()
    program(nc, aps, out)
    r = _run(nc, [arrays], core_ids=[0])
    return r.results[0]["out_x"]
```

```python
from contextlib import ExitStack

import concourse.bass as bass
from concourse import mybir

F32 = mybir.dt.float32
BF16 = mybir.dt.bfloat16
U32 = mybir.dt.uint32
I32 = mybir.dt.int32
ALU = mybir.AluOpType
ACT = mybir.ActivationFunctionType
AX = mybir.AxisListType
P = 128
NEG = -1e30
EPS = 1e-5


class Batch:

    def __init__(self, pair, half):
        self.pair, self.half, self.b = pair, half, pair * 2 + half

    def next(self):
        return Batch(self.pair, 1) if self.half == 0 else Batch(self.pair + 1, 0)


def program(nc, a, out):
    x = a["L0_attn_x"]
    B, T, C = x.shape
    H, _, L = a["L0_attn_Wd_w"].shape
    E0 = a["L0_ffn_Wr"].shape[1]
    NT = B * T // P
    TILES = NT + E0
    E1 = a["L1_ffn_gate_w"].shape[1]
    IS = a["L1_ffn_shared_down_w"].shape[0]
    DL = a["L1_attn_wgq"].shape[1]
    W = 32
    NL = 64
    CHUNK = T // NL
    PAIRS = H // 2
    SCALE0 = float((C // H) ** -0.5)
    LP = 64
    XCH = 4
    TRIPLES = -(-H // 3)
    DEN = 96
    THIRD = DEN - 2 * L
    ROWS = 3 * L + 3
    LR = L + E0
    PARTS = ((0, 0, 0, L), (1, 0, L, L), (2, 0, 2 * L, THIRD), (2, THIRD, DEN + 3, L - THIRD))

    ctx = ExitStack()
    with ctx:
        ctx.enter_context(nc.allow_non_contiguous_dma(reason="small weight columns, once"))

        early = ExitStack()
        scope = [ctx]

        def sb(name, shape, dt=F32):
            return scope[0].enter_context(nc.sbuf_tensor(name, shape, dt))

        def sem(name):
            return ctx.enter_context(nc.semaphore(name))

        bank = [ctx.enter_context(nc.psum_tensor(f"bank{i}", [P, 512], F32)) for i in range(4)]
        bankA, bankB = bank[0], bank[1]
        bankY = bank[2:4]
        bankS = ctx.enter_context(nc.psum_tensor("bankS", [P, 2, 512], F32))
        bankT = ctx.enter_context(nc.psum_tensor("bankT", [P, 2, 512], F32))

        ident = sb("ident", [P, P])
        identb = sb("identb", [P, P], BF16)
        ones = sb("ones", [1, P])
        halfneg = sb("halfneg", [P, 2])
        zeros = sb("zeros", [P, C])
        iota_i = sb("iota_i", [P, TILES], I32)
        iota_f = sb("iota_f", [P, TILES])
        gate_all = sb("gate_all", [P, NT])
        pos_all = sb("pos_all", [P, NT], I32)
        mv = sb("mv", [P, 2, 2])
        stats = sb("stats", [P, 2, 6])
        rstd = sb("rstd", [P, 2, 2])
        xa_all = sb("xa_all", [P, NT, C])
        NB = T // W
        wqk = sb("wqk", [P, 2, C])
        wv = sb("wv", [P, C])
        wgqk = sb("wgqk", [P, 2, P])
        wgv = sb("wgv", [P, DL])
        wro = sb("wro", [DL, C])
        wo1 = sb("wo1", [P, C])
        gw = sb("gw", [P, E1 + 1])
        sgu = sb("sgu", [P, 2 * IS])
        sdw = sb("sdw", [P, IS // P, C])
        gcol = sb("gcol", [P, 2])
        gates = sb("gates", [P, 2, P])
        block16 = sb("block16", [P, P])
        maskl = sb("maskl", [P, 2, 2 * W], BF16)
        maskr = sb("maskr", [P, NB, NL], BF16)
        headcol = sb("headcol", [P, 4])
        quadcol = sb("quadcol", [P, P])
        upto = sb("upto", [P, 2, P], BF16)
        scope[0] = early
        maskq = sb("maskq", [P, P], BF16)
        maskk = sb("maskk", [P, P], BF16)
        wd = sb("wd", [P, PAIRS, 2, LP])
        bd = sb("bd", [P, PAIRS])
        lw = sb("lw", [P, 2, LP])
        lb = sb("lb", [P, 1])
        lbrow = sb("lbrow", [1, LR])
        lwr = sb("lwr", [P, LR])
        ow = sb("ow", [P, TRIPLES, C])
        headsel = sb("headsel", [P, P])
        ob = sb("ob", [1, P])

        xn = sb("xn", [P, 2, 2, C])
        xnT = sb("xnT", [P, 2, T])
        kT = sb("kT", [P, 2, 2, T])
        vaug = sb("vaug", [P, 2, 2, 3, P])
        qT = sb("qT", [P, 2, PAIRS, T])
        mneg = sb("mneg", [P, 2, 2, 2, PAIRS])
        mT = sb("mT", [H, 2, T])
        pT = sb("pT", [P, 4, 384])
        rz = sb("rz", [P, 2, T])
        rzb = sb("rzb", [P, 2, T])
        zT = sb("zT", [P, 2, TRIPLES, T])
        xn_all = sb("xn_all", [P, NT, C])
        lg_all = sb("lg_all", [P, NT, E0])

        F0 = a["L0_ffn_W1"].shape[2]
        KF = F0 // P
        TILES = NT + E0
        WC = 2 * F0 + KF
        wall = sb("wall", [P, E0, WC])
        b2row = sb("b2row", [1, E0, C])
        strict = sb("strict", [P, P], BF16)
        onesb = sb("onesb", [P, P], BF16)
        mx0 = sb("mx0", [P, NT])
        lgs0 = sb("lgs0", [P, NT, E0])
        eq0 = sb("eq0", [P, NT, E0])
        oh0 = sb("oh0", [P, NT, E0], BF16)
        tot0 = sb("tot0", [P, NT, E0])
        cs0 = sb("cs0", [P, NT, E0])
        cnt_i = sb("cnt_i", [P, 2, E0], I32)
        ptile = sb("ptile", [P, E0])
        pend = sb("pend", [P, E0])
        pbase = sb("pbase", [P, E0])
        posf = sb("posf", [P, NT])
        tsel = sb("tsel", [P, TILES, E0])
        tef = sb("tef", [P, TILES])
        te_i = sb("te_i", [P, TILES], I32)
        stage_x = sb("stage_x", [P, 2, C])
        stage_p = sb("stage_p", [P, 2, 1], I32)
        xsb = sb("xsb", [P, 2, C])
        xsT = sb("xsT", [P, 2, P])
        w1b = sb("w1b", [P, 2, F0 + KF])
        hT = sb("hT", [P, 2, KF, P])
        ysb = sb("ysb", [P, 2, C])
        xs_d = nc.dram_tensor("xs_sorted", [TILES * P, C], F32).ap()
        ys_d = nc.dram_tensor("ys_sorted", [TILES * P, C], F32).ap()

        early.close()
        scope[0] = ctx
        cnt_all = sb("cnt_all", [E1, B * T])
        mid = ExitStack()
        scope[0] = mid
        yg = sb("yg", [P, 2, 2, C])
        idx_g = sb("idx_g", [P, 2, 2], I32)
        gate_g = sb("gate_g", [P, 2, 2])
        x1 = sb("x1", [P, 2, 2, C])
        tab = sb("tab", [P, 2, 2, C + E1])
        xT1 = sb("xT1", [P, 2, T])
        xp = sb("xp", [P, 2, NL])
        xr = sb("xr", [P, 2, NB, 4, W])
        xpr = sb("xpr", [P, 2, 2, 4, W])
        qx = sb("qx", [P, 2, NB, 4, W])
        qs = sb("qs", [P, 2, T])
        km = sb("km", [P, 2, 4, W + T])
        gqx = sb("gqx", [P, 2, NB, 4, W])
        gkm = sb("gkm", [P, 2, 2, NL])
        vx = sb("vx", [P, 2, NB, C])
        gvx = sb("gvx", [P, 2, 2, DL])
        lg1 = sb("lg1", [P, 2, E1 + 1])
        mx8 = sb("mx8", [P, 2, 8])
        lgr = sb("lgr", [P, 2, E1])
        mb = sb("mb", [P, 2, 2, E1], BF16)
        shl = sb("shl", [P, 2, E1])
        exl = sb("exl", [P, 2, E1])
        tsg = sb("tsg", [P, 2])
        sgc = sb("sgc", [P, 2, 2])
        wsum = sb("wsum", [P, 2, 2])
        carry = sb("carry", [E1, 2, 1])
        mxs = sb("mxs", [P, 2, 12])
        pr = sb("pr", [P, 2, 12 * NL])
        pt = sb("pt", [P, NB, 6, 2, W])
        tsh = sb("tsh", [P, 2 * T])
        shT = sb("shT", [P, IS // P, T])
        rdr = sb("rdr", [DL, T])
        remn = sb("remn", [DL, T])
        rdl = sb("rdl", [P, T])
        tg = sb("tg", [P, 2, T])
        at1 = sb("at1", [P, T])
        at2 = sb("at2", [P, T])
        aT = sb("aT", [P, T])
        res = sb("res", [P, 2, 2, C])
        mid.close()
        scope[0] = ctx
        CAP = 64
        IE = a["L1_ffn_expert_down_w"].shape[1]
        GE = 8
        NG = E1 // GE
        RW = C + E1
        slot_i = sb("slot_i", [CAP, 1], I32)
        slot_f = sb("slot_f", [CAP, 2])
        full_tiles = sb("full_tiles", [E1, CAP, NT])
        tile_row = sb("tile_row", [E1, 2, CAP])
        tile_at = sb("tile_at", [CAP, E1])
        row_at = sb("row_at", [CAP, E1], I32)
        ridx = sb("ridx", [CAP, 2, GE], I32)
        cg = sb("cg", [CAP, 2, GE, P])
        below = sb("below", [CAP, GE, P])
        tok = sb("tok", [CAP, 2, GE])
        dump = sb("dump", [CAP, GE])
        sidx = sb("sidx", [CAP, 2, GE], I32)
        xg = sb("xg", [CAP, 2, GE, RW])
        xgT = sb("xgT", [P, 2, GE * CAP])
        wge = sb("wge", [P, 2, GE, 2 * IE])
        wde = sb("wde", [IE, 2, GE, C])
        the = sb("the", [IE, GE * CAP])
        ae = sb("ae", [IE, GE * CAP])
        wblk = sb("wblk", [CAP, 2, GE * GE])
        yo = sb("yo", [CAP, 2, GE, C])
        cnt_d = nc.dram_tensor("counts", [E1 * NT, P], F32).ap()
        PAD = P
        xtab_d = nc.dram_tensor("xtab", [B * T + PAD, C + E1], F32).ap()
        acc_d = nc.dram_tensor("acc", [B * T + PAD, C], F32).ap()

        names = """consts zeroed zeroed1 w_in x_in0 x_in1 bn stats_done var rstd_done xn_done xn_kept xnT_ps xnT_sb kv_ps kv_sb
        q_ps q_sb s_ps red_done mT_ps mT_sb st_ps exp_done av_done rz_done y_sb zt_ps zt_sb out_ps xa_done cst dumped passed xs_zero rt ex0 rk_ps staged scat0 scat1 te_done xs_in0 xs_in1 w1_sb xsT_ps xsT_sb h_ps h_act h_dve
        yt_ps yt_sb ys_out0 ys_out1 yg_t x1_all te_go w1_in pads
        yg0 yg1 gidx x1_done bn1 stats1 var1 rstd1 xn1_done tT_ps tT_sb xp_done qk_ps rt_ps rt_sb qx_done kt_sb g_ps g_sb gk_sb
        rstep M_done ex_in ex_done tab_done cnt_ps cnt_sb v_ps v_sb s2_ps red2 sub_done exp2 tr_done shg_ps shu_ps tanh_sh
        sh1_done sh_sb shd_ps av_ps rd_done remn_done rem2_ps gate_ps gate_sb comb aT_done ao_ps r1_done res_done
        tab_out0 tab_out1 res_out0 res_out1 l1_consts wprep xpr_sb slots cnt_out f4 cg_in0 cg_in1 sel sidx_done xg_in0 xg_in1 xgT_ps xgT_sb gu_ps
        the_sb ae1 ae_sb oe_ps wblk_sb yo_sb rix added we_in0 we_in1 tr4 m_in0 m_in1 rz_ps rzb_sb""".split()
        S = {n: sem(n) for n in names}
        x_in = [S["x_in0"], S["x_in1"]]
        block = ctx.enter_context(nc.Block())

        def passed(eng):
            eng.sem_inc(S["passed"], 1)

        NW = 15 + 4 + 2 * KF + 1
        hbank = [bankS, bankT]
        xv = x.rearrange("b (t p) c -> p (b t) c", p=P)
        LOOP = B // 2 - 1
        MAX_BEFORE = ((), (), (0,), (1,), (3,), (4,), (6,), (7,), ())
        MAX_AFTER = ((), (), (), (2,), (), (5,), (), (), ())
        DENS = ((), (), (0,), (1,), (), (2,), (3,), (), (4, 5))
        SPREAD = ((), (), (), (0,), (1,), (), (2,), (3,), (4, 5))

        @block.sync
        def _(sp):
            sp.dma_start(xa_all[:, 0:4, :], xv[:, 0:4, :]).then_inc(x_in[0], 16)
            sp.wait_ge(S["zeroed"], 5)
            for e in range(2):
                sp.dma_start(wd[:, :, e, 0:L], a["L0_attn_Wd_w"].rearrange("(j e) c l -> e c j l", e=2)[e]).then_inc(S["w_in"], 16)
                sp.dma_start(bd[LP * e:LP * e + L, :], a["L0_attn_Wd_b"].rearrange("(j e) l -> e l j", e=2)[e]).then_inc(S["w_in"], 16)
                sp.dma_start(lw[:, e, 0:L], a["L0_attn_latent_w"]).then_inc(S["w_in"], 16)
                sp.dma_start(lb[LP * e:LP * e + L, :], a["L0_attn_latent_b"].rearrange("(l o) -> l o", o=1)).then_inc(S["w_in"], 16)
            sp.dma_start(lwr[:, 0:L], a["L0_attn_latent_w"]).then_inc(S["w_in"], 16)
            sp.dma_start(lbrow[:, 0:L], a["L0_attn_latent_b"].rearrange("(o l) -> o l", o=1)).then_inc(S["w_in"], 16)
            sp.dma_start(lwr[:, L:LR], a["L0_ffn_Wr"]).then_inc(S["w_in"], 16)
            sp.dma_start(lbrow[:, L:LR], a["L0_ffn_br"].rearrange("(o l) -> o l", o=1)).then_inc(S["w_in"], 16)
            oh = a["L0_attn_out_w"].rearrange("(h l) c -> l h c", l=L)
            for j, l0, r0, n in PARTS:
                sp.dma_start(ow[r0:r0 + n, 0:len(range(j, H, 3)), :], oh[l0:l0 + n, j:H:3, :]).then_inc(S["w_in"], 16)
            sp.dma_start(ob[:, :], a["L0_attn_out_b"].rearrange("(o l) -> o l", o=1)).then_inc(S["w_in"], 16)
            for k in range(XCH):
                lo, hi = (4 if k == 0 else k * NT // XCH), (k + 1) * NT // XCH
                sp.dma_start(xa_all[:, lo:hi, :], xv[:, lo:hi, :]).then_inc(x_in[1], 16)
            for e in range(2):
                lo, hi = e * E0 // 2, (e + 1) * E0 // 2
                sp.dma_start(wall[:, lo:hi, 0:F0], a["L0_ffn_W1"][lo:hi].rearrange("e c f -> c e f")).then_inc(S["w_in"], 16)
            for k in range(KF):
                sp.dma_start(wall[:, :, F0 + KF + k * C:F0 + KF + (k + 1) * C],
                             a["L0_ffn_W2"].rearrange("e (k p) c -> k p e c", p=P)[k]).then_inc(S["w_in"], 16)
                sp.dma_start(wall[:, :, F0 + k:F0 + k + 1], a["L0_ffn_b1"].rearrange("e (k p o) -> k p e o", p=P, o=1)[k]).then_inc(S["w_in"], 16)
            sp.dma_start(b2row[:, :, :], a["L0_ffn_b2"].rearrange("(o e) c -> o e c", o=1)).then_inc(S["w_in"], 16)
            sp.dma_start(xs_d.rearrange("(j p) c -> p j c", p=P), zeros[:, :].unsqueeze(1).to_broadcast([P, TILES, C])).then_inc(S["xs_zero"], 16)
            sp.wait_ge(S["zeroed1"], 1)
            for k, w in enumerate(("wq", "wk")):
                sp.dma_start(wqk[:, k, :], a["L1_attn_" + w]).then_inc(S["w1_in"], 16)
                sp.dma_start(wgqk[:, k, 0:DL], a["L1_attn_" + ("wgq", "wgk")[k]]).then_inc(S["w1_in"], 16)
                sp.dma_start(gcol[:, k:k + 1], a["L1_attn_gate_" + ("local_w", "remote_w")[k]].rearrange("h (d o) -> (h d) o", o=1)).then_inc(S["w1_in"], 16)
            sp.dma_start(wv[:, :], a["L1_attn_wv"]).then_inc(S["w1_in"], 16)
            sp.dma_start(wgv[:, :], a["L1_attn_wgv"]).then_inc(S["w1_in"], 16)
            sp.dma_start(wro[:, :], a["L1_attn_r_out_w"]).then_inc(S["w1_in"], 16)
            sp.dma_start(wo1[:, :], a["L1_attn_w_out"]).then_inc(S["w1_in"], 16)
            sp.dma_start(gw[:, 0:E1], a["L1_ffn_gate_w"]).then_inc(S["w1_in"], 16)
            sp.dma_start(gw[:, E1:E1 + 1], a["L1_ffn_shared_gate_w"]).then_inc(S["w1_in"], 16)
            sp.dma_start(sgu[:, :], a["L1_ffn_shared_gate_up_w"]).then_inc(S["w1_in"], 16)
            sp.dma_start(sdw[:, :, :], a["L1_ffn_shared_down_w"].rearrange("(k p) c -> p k c", p=P)).then_inc(S["w1_in"], 16)
            sp.dma_start(acc_d[B * T:B * T + PAD, :], zeros[:, :]).then_inc(S["pads"], 16)
            sp.dma_start(xtab_d[B * T:B * T + PAD, 0:C], zeros[:, :]).then_inc(S["pads"], 16)
            sp.dma_start(xtab_d[B * T:B * T + PAD, C:C + E1], zeros[:, 0:E1]).then_inc(S["pads"], 16)

            def maxima(n):
                sp.wait_ge(S["mT_sb"], n.b + 1)
                for e in range(2):
                    r = LP * e + L
                    sp.dma_start(qT[r:r + 1, n.half], mT[PAIRS * e:PAIRS * (e + 1), n.half, :]).then_inc(S[f"m_in{n.half}"], 16)

            with sp.Fori(0, B // 2) as i:
                maxima(Batch(i, 0))
                maxima(Batch(i, 1))

            def load(i, u):
                if u is not None:
                    sp.dma_start(xsb[:, u], xs_d[bass.ds((i * 2 + u) * P, P), :]).then_inc(S[f"xs_in{u}"], 16)

            def store(i, u):
                sp.wait_ge(S["yt_sb"], i * 2 + (u + 1))
                sp.dma_start(ys_d[bass.ds((i * 2 + u) * P, P), :], ysb[:, u]).then_inc(S[f"ys_out{u}"], 16)

            sp.wait_ge(S["scat0"], 16 * (NT // 2))
            sp.wait_ge(S["scat1"], 16 * (NT // 2))
            load(0, 0)
            load(0, 1)
            with sp.Fori(0, TILES // 2 - 1) as i:
                for u in range(2):
                    sp.wait_ge(S["xsT_ps"], i * 2 + (u + 1))
                    load(i + 1, u)
                    store(i, u)
            for u in range(2):
                store(TILES // 2 - 1, u)
            sp.wait_ge(S["ys_out0"], 16 * (TILES // 2))
            sp.wait_ge(S["ys_out1"], 16 * (TILES // 2))

            def save_table(n):
                sp.wait_ge(S["tab_done"], n.b + 1)
                sp.dma_start(xtab_d[bass.ds(n.b * T, T), :].rearrange("(t p) c -> p t c", p=P), tab[:, n.half]).then_inc(S[f"tab_out{n.half}"], 16)

            def save_stream(b):
                sp.wait_ge(S["res_done"], b.b + 2)
                sp.dma_start(acc_d[bass.ds(b.b * T, T), :].rearrange("(t p) c -> p t c", p=P), res[:, b.half]).then_inc(S[f"res_out{b.half}"], 16)

            save_table(Batch(0, 0))
            with sp.Fori(0, LOOP) as i:
                for b in (Batch(i, 0), Batch(i, 1)):
                    save_table(b.next())
                    save_stream(b)
            save_table(Batch(LOOP, 1))
            save_stream(Batch(LOOP, 0))
            save_stream(Batch(LOOP, 1))
            for u in range(2):
                sp.wait_ge(S[f"res_out{u}"], 16 * (B // 2) + 16)
                sp.wait_ge(S[f"tab_out{u}"], 16 * (B // 2) + 16)
            sp.wait_ge(S["cnt_sb"], B + 1)
            sp.dma_start(cnt_d.rearrange("(e n) p -> e (n p)", e=E1), cnt_all[:, :]).then_inc(S["cnt_out"], 16)

            def weights(g):
                u = g.half
                sp.dma_start(wge[:, u], a["L1_ffn_expert_gate_up_w"][bass.ds(g.b * GE, GE)].rearrange("e h f -> h e f")).then_inc(S[f"we_in{u}"], 16)
                sp.dma_start(wde[:, u], a["L1_ffn_expert_down_w"][bass.ds(g.b * GE, GE)].rearrange("e i h -> i e h")).then_inc(S[f"we_in{u}"], 16)

            weights(Batch(0, 0))
            weights(Batch(0, 1))
            with sp.Fori(0, NG // 2 - 1) as i:
                for g in (Batch(i, 0), Batch(i, 1)):
                    sp.wait_ge(S["oe_ps"], g.b + 1)
                    weights(g.next().next())
            sp.wait_ge(S["added"], 16 * E1)
            sp.dma_start(out.rearrange("b t c -> (b t) c"), acc_d[0:B * T, :]).then_inc(S["dumped"], 16)
            sp.wait_ge(S["dumped"], 16)

        @block.gpsimd
        def _(pool):
            pool.memset(zeros[:, :], 0.0)
            pool.memset(wd[:, :, :, :], 0.0).then_inc(S["zeroed"], 1)
            pool.memset(lw[:, :, :], 0.0).then_inc(S["zeroed"], 1)
            pool.memset(bd[:, :], 0.0).then_inc(S["zeroed"], 1)
            pool.memset(lb[:, :], 0.0).then_inc(S["cst"], 1)
            pool.wait_ge(S["cst"], 1)
            pool.affine_select(out=lb[:, :], in_=lb[:, :], compare_op=ALU.not_equal, fill=1.0, base=-L,
                               pattern=[[0, 1]], channel_multiplier=1).then_inc(S["cst"], 1)
            pool.wait_ge(S["cst"], 2)
            pool.affine_select(out=lb[:, :], in_=lb[:, :], compare_op=ALU.not_equal, fill=1.0, base=-(L + LP),
                               pattern=[[0, 1]], channel_multiplier=1).then_inc(S["zeroed"], 1)
            pool.memset(ones[:, :], 1.0)
            pool.memset(halfneg[:, :], -0.5)
            pool.memset(ow[:, :, :], 0.0).then_inc(S["zeroed"], 1)
            pool.memset(headsel[:, :], 0.0)
            pool.memset(vaug[:, :, :, :, :], 0.0)
            pool.memset(kT[:, :, :, :], 0.0)
            pool.memset(onesb[:, :], 1.0)
            pool.memset(strict[:, :], 1.0)
            pool.iota(iota_i[:, :], pattern=[[1, TILES]], base=0, channel_multiplier=0)
            pool.memset(ident[:, :], 0.0)
            pool.memset(identb[:, :], 0.0)
            pool.memset(maskq[:, :], 0.0)
            pool.memset(maskk[:, :], 0.0).then_inc(S["cst"], 1)
            pool.wait_ge(S["cst"], 3)
            for j in range(3):
                pool.memset(vaug[:, :, :, j, DEN + j:DEN + j + 1], 1.0)
            for j, _, r0, n in PARTS:
                pool.affine_select(out=headsel[:, r0:r0 + n], in_=headsel[:, r0:r0 + n], compare_op=ALU.not_equal, fill=1.0,
                                   base=-(DEN + j), pattern=[[0, n]], channel_multiplier=1)
            for m in (ident, identb):
                pool.affine_select(out=m[:, :], in_=m[:, :], compare_op=ALU.not_equal, fill=1.0, base=0,
                                   pattern=[[-1, P]], channel_multiplier=1)
            pool.affine_select(out=maskq[:, :], in_=maskq[:, :], compare_op=ALU.is_ge, fill=NEG, base=0,
                               pattern=[[-1, P]], channel_multiplier=1)
            pool.affine_select(out=strict[:, :], in_=strict[:, :], compare_op=ALU.is_gt, fill=0.0, base=0,
                               pattern=[[1, P]], channel_multiplier=-1)
            pool.affine_select(out=maskk[:, :], in_=maskk[:, :], compare_op=ALU.is_ge, fill=NEG, base=0,
                               pattern=[[1, P]], channel_multiplier=-1).then_inc(S["consts"], 1)

            made = 3

            def chain(ins):
                nonlocal made
                made += 1
                ins.then_inc(S["cst"], 1)
                pool.wait_ge(S["cst"], made)

            def keep(v, op, fill, base, pattern, step):
                chain(pool.affine_select(out=v, in_=v, compare_op=op, fill=fill, base=base, pattern=pattern, channel_multiplier=step))

            pool.memset(wgqk[:, :, :], 0.0).then_inc(S["zeroed1"], 1)
            pool.memset(maskl[:, :, :], 0.0)
            pool.memset(maskr[:, :, :], 0.0)
            pool.memset(headcol[:, :], 1.0)
            pool.memset(quadcol[:, :], 0.0)
            pool.memset(upto[:, :, :], 1.0)
            chain(pool.memset(block16[:, :], 1.0))
            keep(block16[:, :], ALU.is_ge, 0.0, 0, [[-8, 16], [0, 8]], 1)
            keep(block16[:, :], ALU.is_ge, 0.0, 7, [[8, 16], [0, 8]], -1)
            keep(upto[:, 0, :], ALU.is_ge, 0.0, 0, [[1, P]], -1)
            for g in range(4):
                q = slice(W * g, W * g + W)
                keep(maskl[q], ALU.is_gt, NEG, 0, [[0, 2], [1, 2 * W]], -1)
                keep(maskl[q], ALU.is_ge, NEG, W, [[0, 2], [-1, 2 * W]], 1)
                keep(maskr[q], ALU.is_ge, NEG, 0, [[W, NB], [-CHUNK, NL]], 1)
                keep(headcol[q, :], ALU.is_ge, 0.0, 0, [[-8, 4]], 1)
                keep(headcol[q, :], ALU.is_ge, 0.0, 7, [[8, 4]], -1)
                chain(pool.memset(quadcol[q, :].rearrange("p (a h d) -> p a h d", h=4, d=8)[:, :, g, :], 1.0))
            pool.memset(maskl[:, 0, 0:W], NEG).then_inc(S["l1_consts"], 1)
            pool.wait_ge(S["l1_consts"], 1)

            def stage_a(n):
                pool.wait_ge(S["stats_done"], n.b + 1)
                passed(pool)
                pool.tensor_scalar(rstd[:, 0], mv[:, :, 1], EPS, None, ALU.add).then_inc(S["var"], 1)
                pool.wait_ge(S["var"], n.b + 1)
                pool.tensor_tensor(rstd[:, 1], rstd[:, 0], halfneg[:, :], ALU.pow).then_inc(S["rstd_done"], 1)
                pool.wait_ge(S["xn_done"], n.b + 1)
                pool.tensor_copy(xn_all[:, bass.ds(n.b * 2, 2), :], xn[:, n.half]).then_inc(S["xn_kept"], 1)

            stage_a(Batch(0, 0))
            with pool.Fori(0, LOOP) as i:
                stage_a(Batch(i, 1))
                stage_a(Batch(i + 1, 0))
            stage_a(Batch(LOOP, 1))

            pool.wait_ge(S["te_done"], 1)
            pool.wait_ge(S["xs_zero"], 16)

            def scatter(i, u, first):
                n = i * 2 + u
                if not first:
                    pool.wait_ge(S[f"scat{u}"], i * 16)
                pool.tensor_copy(stage_x[:, u, :], xn_all[:, bass.ds(n, 1), :].rearrange("p a c -> p (a c)"))
                pool.tensor_copy(stage_p[:, u, :], pos_all[:, bass.ds(n, 1)]).then_inc(S["staged"], 1)
                pool.wait_ge(S["staged"], n + 1)
                passed(pool)
                pool.indirect_dma_start(out=xs_d, out_offset=bass.IndirectOffsetOnAxis(ap=stage_p[:, u, :], axis=0),
                                        in_=stage_x[:, u, :], in_offset=None).then_inc(S[f"scat{u}"], 16)

            for u in range(2):
                scatter(0, u, True)
            with pool.Fori(1, NT // 2) as i:
                for u in range(2):
                    scatter(i, u, False)

            pool.wait_ge(S["ys_out0"], 16 * (TILES // 2))
            pool.wait_ge(S["ys_out1"], 16 * (TILES // 2))
            pool.wait_ge(S["scat0"], 16 * (NT // 2))
            pool.wait_ge(S["scat1"], 16 * (NT // 2))

            pool.memset(km[:, :, :, :], 0.0)
            pool.memset(gkm[:, :, :, :], 0.0)
            pool.memset(carry[:, :, :], 0.0).then_inc(S["pads"], 16)

            def gather(m):
                u = m.half
                pool.tensor_copy(idx_g[:, u, :], pos_all[:, bass.ds(m.b * 2, 2)])
                pool.tensor_copy(gate_g[:, u, :], gate_all[:, bass.ds(m.b * 2, 2)]).then_inc(S["gidx"], 1)
                pool.wait_ge(S["gidx"], m.b + 1)
                passed(pool)
                for t in range(2):
                    pool.indirect_dma_start(out=yg[:, u, t, :], out_offset=None, in_=ys_d,
                                            in_offset=bass.IndirectOffsetOnAxis(ap=idx_g[:, u, t:t + 1], axis=0)).then_inc(S[f"yg{u}"], 16)

            def deviation(n):
                pool.wait_ge(S["stats1"], n.b + 1)
                passed(pool)
                pool.tensor_scalar(rstd[:, 0], mv[:, :, 1], EPS, None, ALU.add).then_inc(S["var1"], 1)
                pool.wait_ge(S["var1"], n.b + 1)
                pool.tensor_tensor(rstd[:, 1], rstd[:, 0], halfneg[:, :], ALU.pow).then_inc(S["rstd1"], 1)

            gather(Batch(0, 0))
            gather(Batch(0, 1))
            deviation(Batch(0, 0))
            with pool.Fori(0, LOOP) as i:
                for b in (Batch(i, 0), Batch(i, 1)):
                    deviation(b.next())
                    gather(b.next().next())
            deviation(Batch(LOOP, 1))
            pool.iota(slot_i[:, :], pattern=[[0, 1]], base=0, channel_multiplier=1).then_inc(S["slots"], 1)
            for u in range(2):
                pool.wait_ge(S[f"res_out{u}"], 16 * (B // 2) + 16)
                pool.wait_ge(S[f"tab_out{u}"], 16 * (B // 2) + 16)
            pool.wait_ge(S["cnt_out"], 16)
            pool.wait_ge(S["f4"], 1)

            def count_rows(g):
                u = g.half
                pool.tensor_copy(ridx[:, u, :], row_at[:, bass.ds(g.b * GE, GE)]).then_inc(S["rix"], 1)
                pool.wait_ge(S["rix"], g.b + 1)
                passed(pool)
                for e in range(GE):
                    pool.indirect_dma_start(out=cg[:, u, e, :], out_offset=None, in_=cnt_d,
                                            in_offset=bass.IndirectOffsetOnAxis(ap=ridx[:, u, e:e + 1], axis=0)).then_inc(S[f"cg_in{u}"], 16)

            def token_rows(g):
                u = g.half
                pool.wait_ge(S["sidx_done"], g.b + 1)
                passed(pool)
                for e in range(GE):
                    pool.indirect_dma_start(out=xg[:, u, e, :], out_offset=None, in_=xtab_d,
                                            in_offset=bass.IndirectOffsetOnAxis(ap=sidx[:, u, e:e + 1], axis=0)).then_inc(S[f"xg_in{u}"], 16)

            def add_rows(g):
                u = g.half
                pool.wait_ge(S["yo_sb"], g.b + 1)
                passed(pool)
                for e in range(GE):
                    pool.indirect_dma_start(out=acc_d, out_offset=bass.IndirectOffsetOnAxis(ap=sidx[:, u, e:e + 1], axis=0),
                                            in_=yo[:, u, e, :], in_offset=None, compute_op=ALU.add).then_inc(S["added"], 16)
                    pool.wait_ge(S["added"], (g.b * GE + (e + 1)) * 16)
                    passed(pool)

            def step4(g, n):
                if n:
                    count_rows(n)
                    token_rows(n)
                if g:
                    add_rows(g)

            step4(None, Batch(0, 0))
            with pool.Fori(0, NG // 2 - 1) as i:
                step4(Batch(i, 0), Batch(i, 1))
                step4(Batch(i, 1), Batch(i + 1, 0))
            step4(Batch(NG // 2 - 1, 0), Batch(NG // 2 - 1, 1))
            step4(Batch(NG // 2 - 1, 1), None)

        @block.vector
        def _(dve):
            def stats0(n, chunks):
                if chunks:
                    dve.wait_ge(x_in[1], 16 * chunks)
                else:
                    dve.wait_ge(x_in[0], 16)
                passed(dve)
                for t in range(2):
                    ins = dve.bn_stats(stats[:, t, :], xa_all[:, bass.ds(n.b * 2 + t, 1), :].rearrange("p a c -> p (a c)"))
                ins.then_inc(S["bn"], 1)
                dve.wait_ge(S["bn"], n.b + 1)
                passed(dve)
                for t in range(2):
                    ins = dve.bn_aggr(mv[:, t, :], stats[:, t, :])
                ins.then_inc(S["stats_done"], 1)

            def norm(n, prior):
                u = n.half
                if prior:
                    dve.wait_ge(S["xn_kept"], n.b - 1)
                    dve.wait_ge(S["xnT_ps"], n.b - 1)
                dve.wait_ge(S["rstd_done"], n.b + 1)
                dve.wait_ge(S["stats_done"], n.b + 1)
                for t in range(2):
                    ins = dve.tensor_scalar(xn[:, u, t, :], xa_all[:, bass.ds(n.b * 2 + t, 1), :].rearrange("p a c -> p (a c)"),
                                            mv[:, t, 0:1], rstd[:, 1, t:t + 1], ALU.subtract, ALU.mult)
                ins.then_inc(S["xn_done"], 1)

            def kv(n):
                u = n.half
                dve.wait_ge(S["kv_ps"], n.b + 1)
                for e in range(2):
                    r = slice(LP * e, LP * (e + 1))
                    dve.tensor_scalar(kT[r, u, e, :], bankB[r, 0:T], lb[r, 0:1], None, ALU.add)
                values = bankB[:, 256:256 + 2 * LR].rearrange("p (t l) -> p t l", t=2)
                for j, l0, r0, w in PARTS:
                    dve.tensor_copy(vaug[:, u, :, j, r0:r0 + w], values[:, :, l0:l0 + w])
                dve.tensor_copy(lg_all[:, bass.ds(n.b * 2, 2), :],
                                values[:, :, L:LR]).then_inc(S["kv_sb"], 1)

            def red(n, g):
                dve.wait_ge(S["s_ps"], n.b * PAIRS + (g + 1))
                dve.tensor_reduce(mneg[:, n.half, 0, :, g], bankS[:, :, 0:128], AX.X, ALU.max, negate=True)
                dve.tensor_reduce(mneg[:, n.half, 1, :, g], bankS[:, :, 128:384], AX.X, ALU.max,
                                  negate=True).then_inc(S["red_done"], 1)

            def denominators(b, k):
                dens = slice(DEN, DEN + min(3, H - 3 * k))
                dve.wait_ge(S["av_done"], b.b * H + min(3 * k + 3, H))
                dve.reciprocal(rz[dens, k % 2, :], bankY[k % 2][dens, 0:T]).then_inc(S["rz_done"], 1)

            def normalise(b, k):
                dve.wait_ge(S["rz_ps"], b.b * TRIPLES + (k + 1))
                dve.tensor_copy(rzb[0:ROWS, k % 2, :], bankY[k % 2][0:ROWS, T:2 * T]).then_inc(S["rzb_sb"], 1)
                dve.wait_ge(S["rzb_sb"], b.b * TRIPLES + (k + 1))
                dve.tensor_tensor(zT[0:ROWS, b.half, k, :], bankY[k % 2][0:ROWS, 0:T], rzb[0:ROWS, k % 2, :], ALU.mult).then_inc(S["y_sb"], 1)

            def resid(b):
                dve.wait_ge(S["out_ps"], b.b + 1)
                dve.tensor_tensor(xa_all[:, bass.ds(b.b * 2, 2), :], bankB[:, 0:2 * C].rearrange("p (t c) -> p t c", t=2),
                                  xa_all[:, bass.ds(b.b * 2, 2), :], ALU.add).then_inc(S["xa_done"], 1)

            def step(b, n, m):
                for g in range(1, PAIRS + 1):
                    if n and g == 1:
                        kv(n)
                    for r in MAX_BEFORE[g] if n else ():
                        red(n, r)
                    for k in DENS[g]:
                        denominators(b, k)
                    for r in MAX_AFTER[g] if n else ():
                        red(n, r)
                    for k in SPREAD[g]:
                        normalise(b, k)
                    if m and g == 2:
                        stats0(m, XCH)
                    if m and g == 3:
                        norm(m, True)
                resid(b)

            dve.sem_inc(S["xa_done"], 1)
            dve.sem_inc(S["red_done"], 1)
            dve.sem_inc(S["y_sb"], 2)
            dve.wait_ge(S["w_in"], 16 * NW)
            dve.wait_ge(S["consts"], 1)
            first, second = Batch(0, 0), Batch(0, 1)
            stats0(first, 0)
            norm(first, False)
            kv(first)
            stats0(second, 0)
            norm(second, False)
            for g in range(PAIRS):
                red(first, g)
            with dve.Fori(0, LOOP) as i:
                step(Batch(i, 0), Batch(i, 1), Batch(i + 1, 0))
                step(Batch(i, 1), Batch(i + 1, 0), Batch(i + 1, 1))
            step(Batch(LOOP, 0), Batch(LOOP, 1), None)
            step(Batch(LOOP, 1), None, None)

            done = 0

            def link(ins):
                nonlocal done
                done += 1
                ins.then_inc(S["rt"], 1)
                dve.wait_ge(S["rt"], done)

            def cast(v, shape):
                return v.to_broadcast(shape)

            full = [P, NT, E0]
            dve.wait_ge(S["kv_sb"], B)
            link(dve.tensor_copy(iota_f[:, :], iota_i[:, :]))
            link(dve.tensor_reduce(mx0[:, :], lg_all[:, :, :], AX.X, ALU.max))
            link(dve.tensor_tensor(lgs0[:, :, :], lg_all[:, :, :], cast(mx0[:, :].unsqueeze(2), full), ALU.subtract))
            link(dve.tensor_tensor(eq0[:, :, :], lg_all[:, :, :], cast(mx0[:, :].unsqueeze(2), full), ALU.is_equal))
            link(dve.tensor_scalar(pbase[:, :], iota_f[:, 0:E0], -1.0, float(E0), ALU.mult, ALU.add))
            link(dve.tensor_tensor(eq0[:, :, :], eq0[:, :, :], cast(pbase[:, :].unsqueeze(1), full), ALU.mult))
            link(dve.tensor_reduce(mx0[:, :], eq0[:, :, :], AX.X, ALU.max))
            link(dve.tensor_tensor(oh0[:, :, :], eq0[:, :, :], cast(mx0[:, :].unsqueeze(2), full), ALU.is_equal))
            dve.sem_inc(S["te_go"], 1)
            dve.wait_ge(S["ex0"], 1)
            link(dve.tensor_reduce(posf[:, :], lgs0[:, :, :], AX.X, ALU.add))
            link(dve.reciprocal(gate_all[:, :], posf[:, :]))
            dve.wait_ge(S["rk_ps"], 1)
            link(dve.tensor_copy(tot0[:, :, :], bankB[:, :].rearrange("p (n e) -> p n e", e=E0)))
            for e in range(E0):
                ins = dve.tensor_tensor_scan(cs0[:, :, e], cast(iota_f[:, 1:2], [P, NT]), tot0[:, :, e], 0.0, ALU.mult, ALU.add)
            link(ins)
            link(dve.tensor_scalar(cnt_i[:, 0, :], cs0[:, NT - 1, :], float(P - 1), None, ALU.add))
            link(dve.tensor_scalar(cnt_i[:, 1, :], cnt_i[:, 0, :], P.bit_length() - 1, None, ALU.arith_shift_right))
            link(dve.tensor_copy(ptile[:, :], cnt_i[:, 1, :]))
            link(dve.tensor_tensor_scan(pend[:, :], cast(iota_f[:, 1:2], [P, E0]), ptile[:, :], 0.0, ALU.mult, ALU.add))
            link(dve.tensor_tensor(pbase[:, :], pend[:, :], ptile[:, :], ALU.subtract))
            link(dve.tensor_scalar(pbase[:, :], pbase[:, :], float(P), None, ALU.mult))
            link(dve.tensor_tensor(cs0[:, :, :], cs0[:, :, :], tot0[:, :, :], ALU.subtract))
            link(dve.tensor_tensor(cs0[:, :, :], cs0[:, :, :], cast(pbase[:, :].unsqueeze(1), full), ALU.add))
            link(dve.tensor_tensor(cs0[:, :, :], bankA[:, :].rearrange("p (n e) -> p n e", e=E0), cs0[:, :, :], ALU.add))
            link(dve.tensor_tensor(cs0[:, :, :], cs0[:, :, :], oh0[:, :, :], ALU.mult))
            link(dve.tensor_reduce(posf[:, :], cs0[:, :, :], AX.X, ALU.add))
            link(dve.tensor_copy(pos_all[:, :], posf[:, :]))
            tiles = [P, TILES, E0]
            link(dve.tensor_tensor(tsel[:, :, :], cast(pend[:, :].unsqueeze(1), tiles), cast(iota_f[:, :].unsqueeze(2), tiles), ALU.is_le))
            link(dve.tensor_reduce(tef[:, :], tsel[:, :, :], AX.X, ALU.add))
            dve.tensor_scalar(te_i[:, :], tef[:, :], float(E0 - 1), None, ALU.min).then_inc(S["te_done"], 1)
            dve.wait_ge(S["te_done"], 1)

            def expert_tile(i, u, first):
                j = i * 2 + u
                e = dve.value_load(te_i[0:1, bass.ds(j, 1)], min_val=0, max_val=E0 - 1)
                if not first:
                    dve.wait_ge(S["h_dve"], j - 1)
                dve.tensor_copy(w1b[:, u, :], wall[:, bass.ds(e, 1), 0:F0 + KF].rearrange("p a c -> p (a c)")).then_inc(S["w1_sb"], 1)
                dve.wait_ge(S["w1_sb"], j + 1)
                dve.wait_ge(S["h_ps"], j + 1)
                for k in range(KF // 2, KF):
                    ins = dve.tensor_scalar(hT[:, u, k, :], hbank[u][:, 1, (k - KF // 2) * P:(k - KF // 2 + 1) * P],
                                            w1b[:, u, F0 + k:F0 + k + 1], 0.0, ALU.add, ALU.max)
                ins.then_inc(S["h_dve"], 1)
                if not first:
                    dve.wait_ge(S[f"ys_out{u}"], i * 16)
                dve.wait_ge(S["yt_ps"], j + 1)
                dve.tensor_copy(ysb[:, u], bankY[u][:, 0:C]).then_inc(S["yt_sb"], 1)

            for u in range(2):
                expert_tile(0, u, True)
            with dve.Fori(1, TILES // 2) as i:
                for u in range(2):
                    expert_tile(i, u, False)

            dve.sem_inc(S["res_done"], 1)
            dve.sem_inc(S["cnt_sb"], 1)
            for u in range(2):
                dve.sem_inc(S[f"res_out{u}"], 16)
                dve.sem_inc(S[f"tab_out{u}"], 16)
            dve.wait_ge(S["w1_in"], 16 * 14)
            dve.wait_ge(S["l1_consts"], 1)
            dve.wait_ge(S["pads"], 64)
            for k in range(2):
                dve.tensor_scalar(gates[:, k, :], block16[:, :], gcol[:, k:k + 1], None, ALU.mult)
            dve.tensor_scalar(wgqk[:, 1, :], wgqk[:, 1, :], 1.0 / CHUNK, None, ALU.mult)
            dve.tensor_scalar(wgv[:, :], wgv[:, :], 1.0 / CHUNK, None, ALU.mult)
            dve.tensor_scalar(wo1[:, :], wo1[:, :], 0.5, None, ALU.mult)
            dve.tensor_scalar(sdw[:, :, :], sdw[:, :, :], 0.5, None, ALU.mult).then_inc(S["wprep"], 1)

            def norm1(n, prior):
                u = n.half
                dve.wait_ge(S[f"yg{u}"], n.pair * 32 + 32)
                if prior:
                    dve.wait_ge(S["res_done"], n.b)
                for t in range(2):
                    ins = dve.scalar_tensor_tensor(x1[:, u, t, :], yg[:, u, t, :], gate_g[:, u, t:t + 1],
                                                   xa_all[:, bass.ds(n.b * 2 + t, 1), :].rearrange("p a c -> p (a c)"),
                                                   ALU.mult, ALU.add)
                ins.then_inc(S["x1_done"], 1)
                dve.wait_ge(S["x1_done"], n.b + 1)
                passed(dve)
                for t in range(2):
                    ins = dve.bn_stats(stats[:, t, :], x1[:, u, t, :])
                ins.then_inc(S["bn1"], 1)
                dve.wait_ge(S["bn1"], n.b + 1)
                passed(dve)
                for t in range(2):
                    ins = dve.bn_aggr(mv[:, t, :], stats[:, t, :])
                ins.then_inc(S["stats1"], 1)
                dve.wait_ge(S["rstd1"], n.b + 1)
                dve.wait_ge(S["stats1"], n.b + 1)
                dve.wait_ge(S[f"tab_out{u}"], n.pair * 16 + 16)
                for t in range(2):
                    ins = dve.tensor_scalar(tab[:, u, t, 0:C], x1[:, u, t, :], mv[:, t, 0:1], rstd[:, 1, t:t + 1],
                                            ALU.subtract, ALU.mult)
                ins.then_inc(S["xn1_done"], 1)

            def pool_latents(n):
                dve.wait_ge(S["tT_sb"], n.b * 2 + 1)
                dve.tensor_reduce(xp[:, n.half, :], xT1[:, n.half, :].rearrange("p (n k) -> p n k", k=CHUNK), AX.X,
                                  ALU.add).then_inc(S["xp_done"], 1)

            def spread(dst, src):
                return dve.tensor_tensor(dst, src.rearrange("p (n q) -> p n q", q=W).unsqueeze(2).to_broadcast([P, NB, 4, W]),
                                         headcol[:, :].unsqueeze(1).unsqueeze(3).to_broadcast([P, NB, 4, W]), ALU.mult)

            def queries(n):
                dve.wait_ge(S["qk_ps"], n.b + 1)
                spread(qx[:, n.half], bank[1][:, 0:T]).then_inc(S["qx_done"], 1)

            RSTEPS = 4

            def route(n):
                u = n.half
                dve.wait_ge(S["rt_ps"], n.b + 1)
                dve.tensor_copy(lg1[:, :, :], bank[0][:, 256:256 + 2 * (E1 + 1)].rearrange("p (t e) -> p t e", t=2)).then_inc(S["rt_sb"], 1)
                dve.wait_ge(S["rt_sb"], n.b + 1)
                passed(dve)
                for t in range(2):
                    ins = dve.max(mx8[:, t, :], lg1[:, t, 0:E1])
                ins.then_inc(S["rstep"], 1)
                dve.wait_ge(S["rstep"], n.b * RSTEPS + 1)
                passed(dve)
                for t in range(2):
                    ins = dve.match_replace(lgr[:, t, :], mx8[:, t, :], lg1[:, t, 0:E1], NEG)
                dve.tensor_tensor(shl[:, :, :], lg1[:, :, 0:E1], mx8[:, :, 0:1].to_broadcast([P, 2, E1]), ALU.subtract).then_inc(S["ex_in"], 1)
                dve.wait_ge(S["ex_in"], n.b + 1)
                dve.tensor_tensor(mb[:, u], lg1[:, :, 0:E1], lgr[:, :, :], ALU.not_equal).then_inc(S["M_done"], 1)

            def weigh(n):
                u = n.half
                dve.wait_ge(S["ex_done"], n.b + 1)
                dve.wait_ge(S["M_done"], n.b + 1)
                dve.tensor_tensor(exl[:, :, :], exl[:, :, :], mb[:, u], ALU.mult).then_inc(S["rstep"], 1)
                dve.wait_ge(S["rstep"], n.b * RSTEPS + 2)
                dve.tensor_reduce(wsum[:, 0, :], exl[:, :, :], AX.X, ALU.add).then_inc(S["rstep"], 1)
                dve.wait_ge(S["rstep"], n.b * RSTEPS + 3)
                dve.reciprocal(wsum[:, 1, :], wsum[:, 0, :]).then_inc(S["rstep"], 1)
                dve.wait_ge(S["rstep"], n.b * RSTEPS + 4)
                dve.tensor_scalar(sgc[:, u, :], tsg[:, :], 0.5, 0.5, ALU.mult, ALU.add)
                dve.tensor_tensor(tab[:, u, :, C:C + E1], exl[:, :, :], wsum[:, 1, :].unsqueeze(2).to_broadcast([P, 2, E1]),
                                  ALU.mult).then_inc(S["tab_done"], 1)

            def latents(n):
                u = n.half
                dve.wait_ge(S["g_ps"], n.b + 1)
                spread(gqx[:, u], bank[2][:, 0:T])
                dve.tensor_tensor(gvx[:, u], bank[2][:, 320:320 + 2 * DL].rearrange("p (k c) -> p k c", k=2),
                                  quadcol[:, 0:DL].unsqueeze(1).to_broadcast([P, 2, DL]), ALU.mult).then_inc(S["g_sb"], 1)

            def count(n):
                u = n.half
                dve.wait_ge(S["cnt_sb"], n.b + 1)
                dve.wait_ge(S["cnt_ps"], n.b + 1)
                dve.tensor_scalar(carry[:, u, :], bank[3][0:E1, T - 1:T], carry[:, 1 - u, :], None, ALU.add)
                dve.tensor_scalar(cnt_all[:, bass.ds(n.b * T, T)], bank[3][0:E1, 0:T], carry[:, 1 - u, :], None, ALU.add).then_inc(S["cnt_sb"], 1)

            def values(n):
                for k in range(2):
                    dve.wait_ge(S["v_ps"], n.b * 2 + (k + 1))
                    dve.tensor_tensor(vx[:, n.half, 4 * k:4 * k + 4, :], bank[k][:, :].rearrange("p (n c) -> p n c", c=C),
                                      quadcol[:, :].unsqueeze(1).to_broadcast([P, 4, C]), ALU.mult).then_inc(S["v_sb"], 1)

            def shift(b, g):
                k = g % 2
                s = (bankS, bankT)[k][:, :, 0:6 * NL].rearrange("p b (g k) -> p b g k", k=NL)
                dve.wait_ge(S["s2_ps"], b.b * 4 + (g + 1))
                dve.tensor_reduce(mxs[:, k, :].rearrange("p (b g) -> p b g", b=2), s, AX.X, ALU.max).then_inc(S["red2"], 1)
                dve.wait_ge(S["red2"], b.b * 4 + (g + 1))
                if g >= 2:
                    dve.wait_ge(S["tr_done"], b.b * 4 + (g - 1))
                dve.tensor_tensor(pr[:, k, :].rearrange("p (b g k) -> p b g k", b=2, k=NL), s,
                                  mxs[:, k, :].rearrange("p (b g) -> p b g", b=2).unsqueeze(3).to_broadcast([P, 2, 6, NL]),
                                  ALU.subtract).then_inc(S["sub_done"], 1)

            def turn(b, g):
                dve.wait_ge(S["exp2"], b.b * 4 + (g + 1))
                dve.transpose(pt[:, 2 * g:2 * g + 2].rearrange("p b g k q -> p (b g k q)"), pr[:, g % 2, :]).then_inc(S["tr_done"], 1)

            def shared(b):
                dve.wait_ge(S["tanh_sh"], b.b + 1)
                h = shT[:, :, :].rearrange("p k t -> p (k t)")
                dve.scalar_tensor_tensor(h, tsh[:, :], 1.0, bank[0][:, :], ALU.add, ALU.mult).then_inc(S["sh1_done"], 1)
                dve.wait_ge(S["sh1_done"], b.b + 1)
                dve.wait_ge(S["shu_ps"], b.b + 1)
                dve.tensor_tensor(h, h, bank[1][:, :], ALU.mult).then_inc(S["sh_sb"], 1)

            def finish(b):
                u = b.half
                dve.wait_ge(S["av_ps"], b.b + 1)
                dve.reciprocal(rdr[:, :], bank[3][0:DL, T:2 * T]).then_inc(S["rd_done"], 1)
                dve.wait_ge(S["rd_done"], b.b + 1)
                dve.tensor_tensor(remn[:, :], bank[3][0:DL, 0:T], rdr[:, :], ALU.mult).then_inc(S["remn_done"], 1)
                dve.reciprocal(rdl[:, :], bank[2][:, T:2 * T])
                dve.wait_ge(S["gate_sb"], b.b + 1)
                dve.scalar_tensor_tensor(at1[:, :], tg[:, 0, :], 1.0, bank[2][:, 0:T], ALU.add, ALU.mult).then_inc(S["comb"], 1)
                dve.wait_ge(S["comb"], b.b * 3 + 1)
                dve.tensor_tensor(at1[:, :], at1[:, :], rdl[:, :], ALU.mult).then_inc(S["comb"], 1)
                dve.wait_ge(S["rem2_ps"], b.b + 1)
                dve.scalar_tensor_tensor(at2[:, :], tg[:, 1, :], 1.0, bank[3][:, 0:T], ALU.add, ALU.mult).then_inc(S["comb"], 1)
                dve.wait_ge(S["comb"], b.b * 3 + 3)
                dve.tensor_tensor(aT[:, :], at1[:, :], at2[:, :], ALU.add).then_inc(S["aT_done"], 1)
                dve.wait_ge(S["shd_ps"], b.b + 1)
                dve.wait_ge(S[f"res_out{u}"], b.pair * 16 + 16)
                for t in range(2):
                    ins = dve.scalar_tensor_tensor(res[:, u, t, :], bank[1][:, t * C:(t + 1) * C], sgc[:, u, t:t + 1],
                                                   x1[:, u, t, :], ALU.mult, ALU.add)
                ins.then_inc(S["r1_done"], 1)
                dve.wait_ge(S["r1_done"], b.b + 1)
                dve.wait_ge(S["ao_ps"], b.b + 1)
                dve.tensor_tensor(res[:, u], bank[2][:, 0:2 * C].rearrange("p (t c) -> p t c", t=2), res[:, u],
                                  ALU.add).then_inc(S["res_done"], 1)

            def step1(b, n):
                if b:
                    shift(b, 0)
                if n:
                    norm1(n, b is not None)
                if b:
                    shift(b, 1)
                    turn(b, 0)
                if n:
                    pool_latents(n)
                    queries(n)
                    route(n)
                if b:
                    shift(b, 2)
                    turn(b, 1)
                if n:
                    latents(n)
                    count(n)
                    weigh(n)
                if b:
                    shift(b, 3)
                    turn(b, 2)
                if n:
                    values(n)
                if b:
                    turn(b, 3)
                    shared(b)
                    finish(b)

            step1(None, Batch(0, 0))
            with dve.Fori(0, LOOP) as i:
                step1(Batch(i, 0), Batch(i, 1))
                step1(Batch(i, 1), Batch(i + 1, 0))
            step1(Batch(LOOP, 0), Batch(LOOP, 1))
            step1(Batch(LOOP, 1), None)
            steps4 = 0

            def link4(ins):
                nonlocal steps4
                steps4 += 1
                ins.then_inc(S["sel"], 1)
                dve.wait_ge(S["sel"], steps4)

            for u in range(2):
                dve.wait_ge(S[f"res_out{u}"], 16 * (B // 2) + 16)
                dve.wait_ge(S[f"tab_out{u}"], 16 * (B // 2) + 16)
            dve.wait_ge(S["cnt_sb"], B + 1)
            dve.wait_ge(S["slots"], 1)
            dve.tensor_copy(slot_f[:, 0:1], slot_i[:, :])
            link4(dve.tensor_scalar(slot_f[:, 1:2], slot_i[:, :], float(NT), None, ALU.mult))
            link4(dve.tensor_tensor(full_tiles[:, :, :],
                                    cnt_all[:, :].rearrange("e (n p) -> e n p", p=P)[:, :, P - 1].unsqueeze(1).to_broadcast([E1, CAP, NT]),
                                    iota_f[0:E1, 0:CAP].unsqueeze(2).to_broadcast([E1, CAP, NT]), ALU.is_le))
            link4(dve.tensor_reduce(tile_row[:, 0, :], full_tiles[:, :, :], AX.X, ALU.add))
            link4(dve.tensor_scalar(tile_row[:, 0, :], tile_row[:, 0, :], float(NT - 1), None, ALU.min))
            dve.tensor_scalar(tile_row[:, 1, :], tile_row[:, 0, :], slot_f[:, 1:2], None, ALU.add).then_inc(S["tr4"], 1)
            dve.wait_ge(S["tr4"], 2)
            dve.tensor_scalar(tile_at[:, :], bank[0][0:CAP, 0:E1], float(P), None, ALU.mult)
            dve.tensor_copy(row_at[:, :], bank[0][0:CAP, E1:2 * E1]).then_inc(S["f4"], 1)
            dve.wait_ge(S["f4"], 1)

            def slots(g):
                u = g.half
                at = steps4
                dve.wait_ge(S[f"cg_in{u}"], g.pair * (16 * GE) + 16 * GE)
                dve.tensor_scalar(below[:, :, :], cg[:, u], slot_f[:, 0:1], None, ALU.is_le).then_inc(S["sel"], 1)
                dve.wait_ge(S["sel"], g.b * 4 + (at + 1))
                dve.tensor_reduce(tok[:, 0, :], below[:, :, :], AX.X, ALU.add).then_inc(S["sel"], 1)
                dve.wait_ge(S["sel"], g.b * 4 + (at + 2))
                dve.tensor_tensor(tok[:, 1, :], tok[:, 0, :], tile_at[:, bass.ds(g.b * GE, GE)], ALU.add).then_inc(S["sel"], 1)
                dve.wait_ge(S["sel"], g.b * 4 + (at + 3))
                dve.tensor_scalar(dump[:, :], tok[:, 1, :], float(B * T), slot_f[:, 0:1], ALU.is_ge, ALU.mult).then_inc(S["sel"], 1)
                dve.wait_ge(S["sel"], g.b * 4 + (at + 4))
                dve.tensor_tensor(sidx[:, u, :], tok[:, 1, :], dump[:, :], ALU.add).then_inc(S["sidx_done"], 1)

            def experts(g):
                u = g.half
                dve.wait_ge(S[f"xg_in{u}"], g.pair * (16 * GE) + 16 * GE)
                dve.tensor_copy(wblk[:, u, :].rearrange("p (e k) -> p e k", k=GE), xg[:, u, :, bass.ds(g.b * GE + C, GE)]).then_inc(S["wblk_sb"], 1)
                dve.wait_ge(S["the_sb"], g.b + 1)
                dve.scalar_tensor_tensor(ae[:, :], the[:, :], 1.0, bank[2][0:IE, :], ALU.add, ALU.mult).then_inc(S["ae1"], 1)
                dve.wait_ge(S["ae1"], g.b + 1)
                dve.tensor_tensor(ae[:, :], ae[:, :], bank[3][0:IE, :], ALU.mult).then_inc(S["ae_sb"], 1)
                dve.wait_ge(S["oe_ps"], g.b + 1)
                dve.wait_ge(S["wblk_sb"], g.b + 1)
                for k in range(2):
                    diag = wblk[:, u, 4 * k * (GE + 1):4 * k * (GE + 1) + 3 * (GE + 1) + 1:GE + 1]
                    ins = dve.scalar_tensor_tensor(yo[:, u, 4 * k:4 * k + 4, :], bankS[0:CAP, k, :].rearrange("p (e c) -> p e c", c=C), 0.5,
                                                   diag.unsqueeze(2).to_broadcast([CAP, 4, C]), ALU.mult, ALU.mult)
                ins.then_inc(S["yo_sb"], 1)

            def step4(g, n):
                if n:
                    slots(n)
                if g:
                    experts(g)

            step4(None, Batch(0, 0))
            with dve.Fori(0, NG // 2 - 1) as i:
                step4(Batch(i, 0), Batch(i, 1))
                step4(Batch(i, 1), Batch(i + 1, 0))
            step4(Batch(NG // 2 - 1, 0), Batch(NG // 2 - 1, 1))
            step4(Batch(NG // 2 - 1, 1), None)

        @block.scalar
        def _(act):
            def xnt(n):
                act.wait_ge(S["xnT_ps"], n.b + 1)
                act.copy(xnT[:, n.half, :], bankA[:, 0:T]).then_inc(S["xnT_sb"], 1)

            def qevac(n, r):
                act.wait_ge(S["q_ps"], n.b * 4 + (r + 1))
                for k in range(2):
                    j = 2 * r + k
                    act.activation(qT[:, n.half, j, :], bankA[:, k * T:(k + 1) * T], ACT.Identity,
                                   bias=bd[:, j:j + 1]).then_inc(S["q_sb"], 1)

            def mt(n):
                act.wait_ge(S["mT_ps"], n.b + 1)
                act.copy(mT[:, n.half, :], bankA[0:H, 0:T]).then_inc(S["mT_sb"], 1)

            def probs(b, g):
                for e in range(2):
                    h = 2 * g + e
                    act.wait_ge(S["st_ps"], b.b * H + (h + 1))
                    if h >= 4:
                        act.wait_ge(S["av_done"], b.b * H + (h - 3))
                    act.activation(pT[:, h % 4, :], bankT[:, e, 0:384], ACT.Exp, scale=SCALE0).then_inc(S["exp_done"], 1)

            def step(b, n):
                for g in range(PAIRS):
                    probs(b, g)
                    if n and g == 0:
                        xnt(n)
                    if n and 1 <= g <= 4:
                        qevac(n, g - 1)
                if n:
                    mt(n)

            act.wait_ge(S["w_in"], 16 * NW)
            first = Batch(0, 0)
            xnt(first)
            for r in range(4):
                qevac(first, r)
            mt(first)
            with act.Fori(0, LOOP) as i:
                step(Batch(i, 0), Batch(i, 1))
                step(Batch(i, 1), Batch(i + 1, 0))
            step(Batch(LOOP, 0), Batch(LOOP, 1))
            step(Batch(LOOP, 1), None)

            act.wait_ge(S["te_go"], 1)
            act.activation(lgs0[:, :, :], lgs0[:, :, :], ACT.Exp).then_inc(S["ex0"], 1)

            def expert_tile(i, u):
                j = i * 2 + u
                act.wait_ge(S["xsT_ps"], j + 1)
                act.copy(xsT[:, u, :], bank[u][:, 0:P]).then_inc(S["xsT_sb"], 1)
                act.wait_ge(S["h_ps"], j + 1)
                for k in range(KF // 2):
                    ins = act.activation(hT[:, u, k, :], hbank[u][:, 0, k * P:(k + 1) * P], ACT.Relu,
                                         bias=w1b[:, u, F0 + k:F0 + k + 1])
                ins.then_inc(S["h_act"], 1)

            with act.Fori(0, TILES // 2) as i:
                for u in range(2):
                    expert_tile(i, u)

            SCALE1 = float((C // H) ** -0.5)

            def soft(b, g):
                act.wait_ge(S["sub_done"], b.b * 4 + (g + 1))
                act.activation(pr[:, g % 2, :], pr[:, g % 2, :], ACT.Exp, scale=SCALE1).then_inc(S["exp2"], 1)

            def xt1(n):
                act.wait_ge(S["tT_ps"], n.b + 1)
                act.copy(xT1[:, n.half, :], bank[0][:, 0:T]).then_inc(S["tT_sb"], 1)
                act.copy(xr[:, n.half], bank[0][:, 0:T].rearrange("p (n q) -> p n q", q=W).unsqueeze(2).to_broadcast([P, NB, 4, W])).then_inc(S["tT_sb"], 1)
                act.wait_ge(S["xp_done"], n.b + 1)
                act.copy(xpr[:, n.half], xp[:, n.half, :].rearrange("p (n q) -> p n q", q=W).unsqueeze(2).to_broadcast([P, 2, 4, W])).then_inc(S["xpr_sb"], 1)

            def keys(n):
                u = n.half
                act.wait_ge(S["qx_done"], n.b + 1)
                act.copy(qs[:, u, :], bank[1][:, 0:T])
                for g in range(4):
                    q = slice(W * g, W * g + W)
                    ins = act.copy(km[q, u, g, W:W + T], bank[1][q, T:2 * T])
                ins.then_inc(S["kt_sb"], 1)

            def latent_keys(n):
                act.wait_ge(S["g_sb"], n.b + 1)
                for g in range(2):
                    q = slice(W * g, W * g + W)
                    ins = act.copy(gkm[q, n.half, g, :], bank[2][q, 256:256 + NL])
                ins.then_inc(S["gk_sb"], 1)

            def route(n):
                act.wait_ge(S["ex_in"], n.b + 1)
                act.activation(exl[:, :, :], shl[:, :, :], ACT.Exp)
                act.activation(tsg[:, :], lg1[:, :, E1], ACT.Tanh, scale=0.5).then_inc(S["ex_done"], 1)

            def shared(b):
                act.wait_ge(S["shg_ps"], b.b + 1)
                act.activation(tsh[:, :], bank[0][:, :], ACT.Tanh, scale=0.5).then_inc(S["tanh_sh"], 1)

            def gate(b):
                act.wait_ge(S["gate_ps"], b.b + 1)
                act.activation(tg[:, :, :].rearrange("p k t -> p (k t)"), bank[0][:, :], ACT.Tanh, scale=0.5).then_inc(S["gate_sb"], 1)

            def step1(b, n):
                if b:
                    soft(b, 0)
                if n:
                    xt1(n)
                if b:
                    soft(b, 1)
                if n:
                    keys(n)
                    route(n)
                if b:
                    soft(b, 2)
                if n:
                    latent_keys(n)
                if b:
                    soft(b, 3)
                    shared(b)
                    gate(b)

            act.wait_ge(S["wprep"], 1)
            step1(None, Batch(0, 0))
            with act.Fori(0, LOOP) as i:
                step1(Batch(i, 0), Batch(i, 1))
                step1(Batch(i, 1), Batch(i + 1, 0))
            step1(Batch(LOOP, 0), Batch(LOOP, 1))
            step1(Batch(LOOP, 1), None)
            def experts(g):
                u = g.half
                act.wait_ge(S["xgT_ps"], g.b + 1)
                act.copy(xgT[:, u, :], bank[1][:, :]).then_inc(S["xgT_sb"], 1)
                act.wait_ge(S["gu_ps"], g.b + 1)
                act.activation(the[:, :], bank[2][0:IE, :], ACT.Tanh, scale=0.5).then_inc(S["the_sb"], 1)

            with act.Fori(0, NG // 2) as i:
                experts(Batch(i, 0))
                experts(Batch(i, 1))

        @block.tensor
        def _(pe):
            def xnt(n):
                pe.wait_ge(S["xn_done"], n.b + 1)
                for t in range(2):
                    ins = pe.transpose(bankA[:, t * P:(t + 1) * P], xn[:, n.half, t, :], ident[:, :])
                ins.then_inc(S["xnT_ps"], 1)

            def kv(n, prior):
                u = n.half
                pe.wait_ge(S["xnT_sb"], n.b + 1)
                if prior:
                    pe.wait_ge(S["xa_done"], n.b)
                pe.matmul(bankB[:, 0:T], lw[:, :, :].rearrange("p e l -> p (e l)"), xnT[:, u, :], start=True, stop=True)
                for t in range(2):
                    tok = xnT[:, u, t * P:(t + 1) * P]
                    o = bankB[:, 256 + t * LR:256 + (t + 1) * LR]
                    pe.matmul(o, tok, lwr[:, :], start=True, stop=False)
                    ins = pe.matmul(o, ones[:, :], lbrow[:, :], start=False, stop=True)
                ins.then_inc(S["kv_ps"], 1)

            def qproj(n, r):
                if r >= 1:
                    pe.wait_ge(S["q_sb"], n.b * PAIRS + 2 * r)
                for k in range(2):
                    ins = pe.matmul(bankA[:, k * T:(k + 1) * T], wd[:, 2 * r + k, :, :].rearrange("p e l -> p (e l)"),
                                    xnT[:, n.half, :], start=True, stop=True)
                ins.then_inc(S["q_ps"], 1)

            def diagonal(s, mask):
                return pe.matmul(s[:, 0:384].rearrange("p (k t) -> p k t", t=P)[:, 0:3:2, :], identb[:, :],
                          mask[:, :].unsqueeze(1).to_broadcast([P, 2, P]), start=False, stop=True)

            def smax(n, g):
                u = n.half
                pe.wait_ge(S["q_sb"], n.b * PAIRS + (g + 1))
                if g == 0:
                    pe.wait_ge(S["kv_sb"], n.b + 1)
                pe.wait_ge(S["red_done"], n.b * PAIRS + (g + 1))
                for e in range(2):
                    s = bankS[:, e, :]
                    pe.matmul(s[:, 0:128], qT[:, u, g, 0:P], kT[:, u, e, 0:P], start=True, stop=False)
                    pe.matmul(s[:, 128:384], qT[:, u, g, P:T], kT[:, u, e, :], start=False, stop=False)
                    ins = diagonal(s, maskq)
                ins.then_inc(S["s_ps"], 1)

            def mt(n):
                pe.wait_ge(S["red_done"], n.b * PAIRS + (PAIRS + 1))
                pe.wait_ge(S["q_sb"], n.b * PAIRS + PAIRS)
                passed(pe)
                for t in range(2):
                    ins = pe.transpose(bankA[0:H, t * P:(t + 1) * P], mneg[:, n.half, t].rearrange("p e j -> p (e j)"), ident[:, :])
                ins.then_inc(S["mT_ps"], 1)

            def st(b, g):
                u = b.half
                if g == 0:
                    pe.wait_ge(S[f"m_in{u}"], b.pair * 32 + 32)
                for e in range(2):
                    h = 2 * g + e
                    if h >= 2:
                        pe.wait_ge(S["exp_done"], b.b * H + (h - 1))
                    s = bankT[:, e, :]
                    for k, cols in ((0, slice(0, 256)), (1, slice(256, 384))):
                        pe.matmul(s[:, cols], kT[:, u, e, k * P:(k + 1) * P], qT[:, u, g, k * P:T], start=(k == 0), stop=False)
                    ins = diagonal(s, maskk)
                    ins.then_inc(S["st_ps"], 1)

            def av(b, h):
                u, k = b.half, h // 3
                y = bankY[k % 2]
                if h % 3 == 0:
                    pe.wait_ge(S["y_sb"], b.b * TRIPLES + (k + 1))
                pe.wait_ge(S["exp_done"], b.b * H + (h + 1))
                p = pT[:, h % 4, :]
                last = h % 3 == 2 or h == H - 1
                pe.matmul(y[:, 0:T], vaug[:, u, 0, h % 3, :], p[:, 0:256], start=(h % 3 == 0), stop=False)
                pe.matmul(y[:, P:T], vaug[:, u, 1, h % 3, :], p[:, 256:384], start=False, stop=last).then_inc(S["av_done"], 1)

            def spread(b, k):
                dens = slice(DEN, DEN + min(3, H - 3 * k))
                pe.wait_ge(S["rz_done"], b.b * TRIPLES + (k + 1))
                pe.matmul(bankY[k % 2][:, T:2 * T], headsel[dens, :], rz[dens, k % 2, :], start=True, stop=True).then_inc(S["rz_ps"], 1)

            def outp(b):
                for t in range(2):
                    o = bankB[:, t * C:(t + 1) * C]
                    pe.matmul(o, ones[:, :], ob[:, :], start=True, stop=False)
                    for k in range(TRIPLES):
                        if t == 0:
                            if k == TRIPLES - 2:
                                spread(b, k)
                                spread(b, k + 1)
                            pe.wait_ge(S["y_sb"], b.b * TRIPLES + (k + 3))
                        ins = pe.matmul(o, zT[0:ROWS, b.half, k, t * P:(t + 1) * P], ow[0:ROWS, k, :], start=False, stop=(k == TRIPLES - 1))
                ins.then_inc(S["out_ps"], 1)

            def step(b, n):
                for g in range(PAIRS + 1):
                    if 1 <= g < PAIRS:
                        st(b, g)
                    if n and g == 0:
                        xnt(n)
                    if n and g == 1:
                        kv(n, True)
                    for r in MAX_BEFORE[g] if n else ():
                        smax(n, r)
                    if g >= 1:
                        av(b, 2 * g - 2)
                        av(b, 2 * g - 1)
                    if n and 1 <= g <= 4:
                        qproj(n, g - 1)
                    for r in MAX_AFTER[g] if n else ():
                        smax(n, r)
                    if g < PAIRS:
                        for k in SPREAD[g]:
                            spread(b, k)
                if n:
                    mt(n)
                outp(b)
                if n:
                    st(n, 0)

            pe.wait_ge(S["w_in"], 16 * NW)
            pe.wait_ge(S["consts"], 1)
            first = Batch(0, 0)
            xnt(first)
            kv(first, False)
            for r in range(4):
                qproj(first, r)
            for g in range(PAIRS):
                smax(first, g)
            mt(first)
            st(first, 0)
            with pe.Fori(0, LOOP) as i:
                step(Batch(i, 0), Batch(i, 1))
                step(Batch(i, 1), Batch(i + 1, 0))
            step(Batch(LOOP, 0), Batch(LOOP, 1))
            step(Batch(LOOP, 1), None)

            pe.wait_ge(S["te_go"], 1)
            pe.wait_ge(S["xa_done"], B + 1)
            flat = oh0[:, :, :].rearrange("p n e -> p (n e)")
            pe.matmul(bankA[:, :], strict[:, :], flat, start=True, stop=True)
            pe.matmul(bankB[:, :], onesb[:, :], flat, start=True, stop=True).then_inc(S["rk_ps"], 1)
            pe.wait_ge(S["te_done"], 1)

            def expert_tile(i, u, first):
                j = i * 2 + u
                e = pe.value_load(te_i[0:1, bass.ds(j, 1)], min_val=0, max_val=E0 - 1)
                pe.wait_ge(S[f"xs_in{u}"], i * 16 + 16)
                pe.transpose(bank[u][:, 0:P], xsb[:, u, :], ident[:, :]).then_inc(S["xsT_ps"], 1)
                pe.wait_ge(S["w1_sb"], j + 1)
                pe.wait_ge(S["xsT_sb"], j + 1)
                for k in range(KF):
                    c = (k % 2) * P
                    ins = pe.matmul(hbank[u][:, k // 2, c:c + P], w1b[:, u, k * P:(k + 1) * P], xsT[:, u, :], start=True, stop=True)
                ins.then_inc(S["h_ps"], 1)
                pe.wait_ge(S["h_act"], j + 1)
                pe.wait_ge(S["h_dve"], j + 1)
                if not first:
                    pe.wait_ge(S["yt_sb"], j - 1)
                for k in range(KF):
                    pe.matmul(bankY[u][:, 0:C], hT[:, u, k, :],
                              wall[:, bass.ds(e, 1), F0 + KF + k * C:F0 + KF + (k + 1) * C].rearrange("p a c -> p (a c)"),
                              start=(k == 0), stop=False)
                pe.matmul(bankY[u][:, 0:C], ones[:, :], b2row[:, bass.ds(e, 1), :].rearrange("p a c -> p (a c)"),
                          start=False, stop=True).then_inc(S["yt_ps"], 1)

            for u in range(2):
                expert_tile(0, u, True)
            with pe.Fori(1, TILES // 2) as i:
                for u in range(2):
                    expert_tile(i, u, False)

            def scores(b, g):
                u = b.half
                if g == 0:
                    pe.wait_ge(S["kt_sb"], b.b + 1)
                    pe.wait_ge(S["gk_sb"], b.b + 1)
                else:
                    pe.wait_ge(S["s2_ps"], b.b * 4 + g)
                if g >= 2:
                    pe.wait_ge(S["sub_done"], b.b * 4 + (g - 1))
                for k in range(2):
                    n = 2 * g + k
                    s = (bankS, bankT)[g % 2][:, k, :]
                    pe.matmul(s[:, 0:4 * NL], identb[:, :], maskl[:, min(n, 1), :].unsqueeze(1).to_broadcast([P, 4, NL]), start=True, stop=False)
                    for h in range(4):
                        pe.matmul(s[:, h * NL:(h + 1) * NL], qx[:, u, n].rearrange("p h q -> p (h q)"),
                                  km[:, u, h, n * W:n * W + 2 * W], start=False, stop=(h == 3))
                    pe.matmul(s[:, 4 * NL:6 * NL], identb[:, :], maskr[:, n, :].unsqueeze(1).to_broadcast([P, 2, NL]), start=True, stop=False)
                    for h in range(2):
                        ins = pe.matmul(s[:, (4 + h) * NL:(5 + h) * NL], gqx[:, u, n].rearrange("p h q -> p (h q)"),
                                        gkm[:, u, h, :], start=False, stop=(h == 1))
                ins.then_inc(S["s2_ps"], 1)

            def xt1(n):
                pe.wait_ge(S["xn1_done"], n.b + 1)
                for t in range(2):
                    ins = pe.transpose(bank[0][:, t * P:(t + 1) * P], tab[:, n.half, t, 0:C], ident[:, :])
                ins.then_inc(S["tT_ps"], 1)

            def qk(n, prior):
                u = n.half
                pe.wait_ge(S["tT_sb"], n.b * 2 + 2)
                if prior:
                    pe.wait_ge(S["res_done"], n.b)
                for k in range(2):
                    ins = pe.matmul(bank[1][:, k * T:(k + 1) * T], wqk[:, k, :], xT1[:, u, :], start=True, stop=True)
                ins.then_inc(S["qk_ps"], 1)
                for t in range(2):
                    c = 256 + t * (E1 + 1)
                    ins = pe.matmul(bank[0][:, c:c + E1 + 1], xT1[:, u, t * P:(t + 1) * P], gw[:, :], start=True, stop=True)
                ins.then_inc(S["rt_ps"], 1)

            def latents(n):
                u = n.half
                pe.wait_ge(S["xpr_sb"], n.b + 1)
                pe.matmul(bank[2][:, 0:T], wgqk[:, 0, :], xT1[:, u, :], start=True, stop=True)
                pe.matmul(bank[2][:, T:T + NL], wgqk[:, 1, :], xp[:, u, :], start=True, stop=True)
                for k in range(2):
                    ins = pe.matmul(bank[2][:, 320 + k * DL:320 + (k + 1) * DL], xpr[:, u, k].rearrange("p r q -> p (r q)"), wgv[:, :], start=True, stop=True)
                ins.then_inc(S["g_ps"], 1)

            def count(n):
                pe.wait_ge(S["M_done"], n.b + 1)
                pe.matmul(bank[3][0:E1, 0:T], mb[:, n.half, 0, :], upto[:, :, :].rearrange("p k t -> p (k t)"), start=True, stop=False)
                pe.matmul(bank[3][0:E1, P:T], mb[:, n.half, 1, :], upto[:, 0, :], start=False, stop=True).then_inc(S["cnt_ps"], 1)

            def values(n):
                u = n.half
                pe.wait_ge(S["kt_sb"], n.b + 1)
                pe.wait_ge(S["rt_sb"], n.b + 1)
                for k in range(2):
                    for j in range(4):
                        ins = pe.matmul(bank[k][:, j * C:(j + 1) * C], xr[:, u, 4 * k + j].rearrange("p r q -> p (r q)"), wv[:, :], start=True, stop=True)
                    ins.then_inc(S["v_ps"], 1)

            def shared_up(b, last):
                u = b.half
                pe.wait_ge(S["v_sb"], b.b * 2 + (2 if last else 4))
                for k in range(2):
                    for j in range(2):
                        c = (2 * k + j) * P
                        ins = pe.matmul(bank[k][:, j * T:(j + 1) * T], sgu[:, c:c + P], xT1[:, u, :], start=True, stop=True)
                    ins.then_inc(S[("shg_ps", "shu_ps")[k]], 1)

            def attend(b, last):
                u = b.half
                pe.wait_ge(S["tr_done"], b.b * 4 + 4)
                pe.wait_ge(S["gk_sb"], b.b + (1 if last else 2))
                pe.wait_ge(S["cnt_sb"], b.b + (2 if last else 3))
                for h in range(4):
                    q = slice(W * h, W * h + W)
                    if h < 2:
                        for k in range(2):
                            pe.matmul(bank[3][q, 0:T], gvx[:, u, k, q], pt[:, :, 4 + h, k, :], start=(k == 0), stop=(k == 1))
                        for k in range(2):
                            pe.matmul(bank[3][q, T:2 * T], quadcol[:, 0:W], pt[:, :, 4 + h, k, :], start=(k == 0), stop=(k == 1))
                    for n in range(NB):
                        o = bank[2][q, n * W:(n + 1) * W]
                        if n:
                            pe.matmul(o, vx[:, u, n - 1, q], pt[:, n, h, 0, :], start=True, stop=False)
                        pe.matmul(o, vx[:, u, n, q], pt[:, n, h, 1, :], start=(n == 0), stop=True)
                    for k in range(2):
                        ins = pe.matmul(bank[2][q, T:2 * T], quadcol[:, 0:W], pt[:, :, h, k, :], start=(k == 0), stop=(k == 1))
                ins.then_inc(S["av_ps"], 1)

            def finish(b):
                u = b.half
                pe.wait_ge(S["sh1_done"], b.b + 1)
                for k in range(2):
                    ins = pe.matmul(bank[0][:, k * T:(k + 1) * T], gates[:, k, :], qs[:, u, :], start=True, stop=True)
                ins.then_inc(S["gate_ps"], 1)
                pe.wait_ge(S["remn_done"], b.b + 1)
                pe.matmul(bank[3][:, 0:T], wro[:, :], remn[:, :], start=True, stop=True).then_inc(S["rem2_ps"], 1)
                pe.wait_ge(S["sh_sb"], b.b + 1)
                for t in range(2):
                    for k in range(2):
                        ins = pe.matmul(bank[1][:, t * C:(t + 1) * C], shT[:, k, t * P:(t + 1) * P], sdw[:, k, :], start=(k == 0), stop=(k == 1))
                ins.then_inc(S["shd_ps"], 1)
                pe.wait_ge(S["aT_done"], b.b + 1)
                for t in range(2):
                    ins = pe.matmul(bank[2][:, t * C:(t + 1) * C], aT[:, t * P:(t + 1) * P], wo1[:, :], start=True, stop=True)
                ins.then_inc(S["ao_ps"], 1)

            def step1(b, n):
                if b:
                    scores(b, 0)
                if n:
                    xt1(n)
                if b:
                    scores(b, 1)
                if n:
                    qk(n, b is not None)
                if b:
                    scores(b, 2)
                if n:
                    latents(n)
                    count(n)
                if b:
                    scores(b, 3)
                if n:
                    values(n)
                if b:
                    shared_up(b, n is None)
                    attend(b, n is None)
                    finish(b)

            pe.wait_ge(S["wprep"], 1)
            step1(None, Batch(0, 0))
            with pe.Fori(0, LOOP) as i:
                step1(Batch(i, 0), Batch(i, 1))
                step1(Batch(i, 1), Batch(i + 1, 0))
            step1(Batch(LOOP, 0), Batch(LOOP, 1))
            step1(Batch(LOOP, 1), None)
            pe.wait_ge(S["tr4"], 1)
            pe.transpose(bank[0][0:CAP, 0:E1], tile_row[:, 0, :], ident[0:E1, 0:E1])
            pe.transpose(bank[0][0:CAP, E1:2 * E1], tile_row[:, 1, :], ident[0:E1, 0:E1]).then_inc(S["tr4"], 1)

            def experts(g):
                u = g.half
                pe.wait_ge(S[f"xg_in{u}"], g.pair * (16 * GE) + 16 * GE)
                passed(pe)
                for e in range(GE):
                    ins = pe.transpose(bank[1][:, e * CAP:(e + 1) * CAP], xg[:, u, e, 0:C], ident[0:CAP, 0:CAP])
                ins.then_inc(S["xgT_ps"], 1)
                pe.wait_ge(S["xgT_sb"], g.b + 1)
                pe.wait_ge(S[f"we_in{u}"], g.pair * 32 + 32)
                for k in range(2):
                    for e in range(GE):
                        ins = pe.matmul(bank[2 + k][0:IE, e * CAP:(e + 1) * CAP], wge[:, u, e, k * IE:(k + 1) * IE],
                                        xgT[:, u, e * CAP:(e + 1) * CAP], start=True, stop=True)
                ins.then_inc(S["gu_ps"], 1)
                pe.wait_ge(S["ae_sb"], g.b + 1)
                passed(pe)
                for e in range(GE):
                    ins = pe.matmul(bankS[0:CAP, e // 4, (e % 4) * C:(e % 4 + 1) * C], ae[:, e * CAP:(e + 1) * CAP],
                                    wde[:, u, e, :], start=True, stop=True)
                ins.then_inc(S["oe_ps"], 1)

            with pe.Fori(0, NG // 2) as i:
                experts(Batch(i, 0))
                experts(Batch(i, 1))


_INS = ['L0_attn_x', 'L0_attn_latent_w', 'L0_attn_latent_b', 'L0_attn_Wd_w', 'L0_attn_Wd_b', 'L0_attn_out_w',
        'L0_attn_out_b', 'L0_ffn_Wr', 'L0_ffn_br', 'L0_ffn_W1', 'L0_ffn_b1', 'L0_ffn_W2', 'L0_ffn_b2', 'L1_attn_wq',
        'L1_attn_wk', 'L1_attn_wv', 'L1_attn_wgq', 'L1_attn_wgk', 'L1_attn_wgv', 'L1_attn_r_out_w',
        'L1_attn_gate_local_w', 'L1_attn_gate_remote_w', 'L1_attn_w_out', 'L1_ffn_gate_w', 'L1_ffn_shared_gate_w',
        'L1_ffn_shared_gate_up_w', 'L1_ffn_shared_down_w', 'L1_ffn_expert_gate_up_w', 'L1_ffn_expert_down_w']


def kernel(**inputs):
    import numpy as _np
    import concourse.bacc as _bacc
    from concourse import mybir as _mybir
    from concourse.bass_utils import run_bass_kernel_spmd as _run

    nc = _bacc.Bacc("TRN2", target_bir_lowering=False, num_devices=1)
    arrays, aps = {}, {}
    for name in _INS:
        v = _np.ascontiguousarray(inputs[name])
        arrays[f"in_{name}"] = v
        aps[name] = nc.dram_tensor(f"in_{name}", v.shape, _mybir.dt.from_np(v.dtype), kind="ExternalInput").ap()
    shape = inputs["L0_attn_x"].shape
    out = nc.dram_tensor("out_x", shape, _mybir.dt.float32, kind="ExternalOutput").ap()
    program(nc, aps, out)
    r = _run(nc, [arrays], core_ids=[0])
    return r.results[0]["out_x"]
```

```python
from contextlib import ExitStack

import concourse.bass as bass
from concourse import mybir

F32 = mybir.dt.float32
BF16 = mybir.dt.bfloat16
U32 = mybir.dt.uint32
I32 = mybir.dt.int32
ALU = mybir.AluOpType
ACT = mybir.ActivationFunctionType
AX = mybir.AxisListType
P = 128
NEG = -1e30
EPS = 1e-5


class Batch:

    def __init__(self, pair, half):
        self.pair, self.half, self.b = pair, half, pair * 2 + half

    def next(self):
        return Batch(self.pair, 1) if self.half == 0 else Batch(self.pair + 1, 0)


def program(nc, a, out):
    x = a["L0_attn_x"]
    B, T, C = x.shape
    H, _, L = a["L0_attn_Wd_w"].shape
    E0 = a["L0_ffn_Wr"].shape[1]
    NT = B * T // P
    TILES = NT + E0
    E1 = a["L1_ffn_gate_w"].shape[1]
    IS = a["L1_ffn_shared_down_w"].shape[0]
    DL = a["L1_attn_wgq"].shape[1]
    W = 32
    NL = 64
    CHUNK = T // NL
    PAIRS = H // 2
    SCALE0 = float((C // H) ** -0.5)
    LP = 64
    XCH = 4
    TRIPLES = 1 + (H - 1) // 3
    DEN = 96
    THIRD = DEN - 2 * L
    ROWS = 3 * L + 3
    LR = L + E0
    PARTS = ((0, 0, 0, L), (1, 0, L, L), (2, 0, 2 * L, THIRD), (2, THIRD, DEN + 3, L - THIRD))

    ctx = ExitStack()
    with ctx:
        ctx.enter_context(nc.allow_non_contiguous_dma(reason="small weight columns, once"))

        early = ExitStack()
        scope = [ctx]

        def sb(name, shape, dt=F32):
            return scope[0].enter_context(nc.sbuf_tensor(name, shape, dt))

        def sem(name):
            return ctx.enter_context(nc.semaphore(name))

        bank = [ctx.enter_context(nc.psum_tensor(f"bank{i}", [P, 512], F32)) for i in range(4)]
        bankA, bankB = bank[0], bank[1]
        bankY = bank[2:4]
        bankS = ctx.enter_context(nc.psum_tensor("bankS", [P, 2, 512], F32))
        bankT = ctx.enter_context(nc.psum_tensor("bankT", [P, 2, 512], F32))

        ident = sb("ident", [P, P])
        identb = sb("identb", [P, P], BF16)
        ones = sb("ones", [1, P])
        halfneg = sb("halfneg", [P, 2])
        zeros = sb("zeros", [P, C])
        iota_i = sb("iota_i", [P, TILES], I32)
        iota_f = sb("iota_f", [P, TILES])
        gate_all = sb("gate_all", [P, NT])
        pos_all = sb("pos_all", [P, NT], I32)
        mv = sb("mv", [P, 2, 2])
        stats = sb("stats", [P, 2, 6])
        rstd = sb("rstd", [P, 2, 2])
        xa_all = sb("xa_all", [P, NT, C])
        NB = T // W
        wqk = sb("wqk", [P, 2, C])
        wv = sb("wv", [P, C])
        wgqk = sb("wgqk", [P, 2, P])
        wgv = sb("wgv", [P, DL])
        wro = sb("wro", [DL, C])
        wo1 = sb("wo1", [P, C])
        gw = sb("gw", [P, E1 + 1])
        sgu = sb("sgu", [P, 2 * IS])
        sdw = sb("sdw", [P, IS // P, C])
        gcol = sb("gcol", [P, 2])
        gates = sb("gates", [P, 2, P])
        block16 = sb("block16", [P, P])
        maskl = sb("maskl", [P, 2, 2 * W], BF16)
        maskr = sb("maskr", [P, NB, NL], BF16)
        headcol = sb("headcol", [P, 4])
        quadcol = sb("quadcol", [P, P])
        upto = sb("upto", [P, 2, P], BF16)
        scope[0] = early
        xn_all = sb("xn_all", [P, NT, C])
        lg_all = sb("lg_all", [P, NT, E0])

        F0 = a["L0_ffn_W1"].shape[2]
        KF = F0 // P
        TILES = NT + E0
        WC = 2 * F0 + KF
        wall = sb("wall", [P, E0, WC])
        b2row = sb("b2row", [1, E0, C])
        strict = sb("strict", [P, P], BF16)
        onesb = sb("onesb", [P, P], BF16)
        attention = ExitStack()
        scope[0] = attention
        maskq = sb("maskq", [P, P], BF16)
        maskk = sb("maskk", [P, P], BF16)
        wd = sb("wd", [P, PAIRS, 2, LP])
        bd = sb("bd", [P, PAIRS])
        lw = sb("lw", [P, 2, LP])
        lb = sb("lb", [P, 1])
        lbrow = sb("lbrow", [1, LR])
        lwr = sb("lwr", [P, LR])
        ow = sb("ow", [P, TRIPLES, C])
        headsel = sb("headsel", [P, P])
        ob = sb("ob", [1, P])

        xn = sb("xn", [P, 2, 2, C])
        xnT = sb("xnT", [P, 2, T])
        kT = sb("kT", [P, 2, 2, T])
        vaug = sb("vaug", [P, 2, 2, 3, P])
        qT = sb("qT", [P, 2, PAIRS, T])
        kb = sb("kb", [P, 2, T], BF16)
        qb = sb("qb", [P, PAIRS, T], BF16)
        mneg = sb("mneg", [P, 2, 2, 2, PAIRS])
        mT = sb("mT", [H, 2, T])
        pT = sb("pT", [P, 4, 384])
        rz = sb("rz", [P, 2, T])
        rzb = sb("rzb", [P, 2, T])
        zT = sb("zT", [P, 2, TRIPLES, T])
        attention.close()
        scope[0] = early

        mx0 = sb("mx0", [P, NT])
        lgs0 = sb("lgs0", [P, NT, E0])
        eq0 = sb("eq0", [P, NT, E0])
        oh0 = sb("oh0", [P, NT, E0], BF16)
        tot0 = sb("tot0", [P, NT, E0])
        cs0 = sb("cs0", [P, NT, E0])
        cnt_i = sb("cnt_i", [P, 2, E0], I32)
        ptile = sb("ptile", [P, E0])
        pend = sb("pend", [P, E0])
        pbase = sb("pbase", [P, E0])
        posf = sb("posf", [P, NT])
        tsel = sb("tsel", [P, TILES, E0])
        tef = sb("tef", [P, TILES])
        te_i = sb("te_i", [P, TILES], I32)
        SG = 4
        stage_x = sb("stage_x", [P, 2, SG, C])
        stage_p = sb("stage_p", [P, 2, SG], I32)
        xsb = sb("xsb", [P, 2, 2, C])
        xsT = sb("xsT", [P, 2, P])
        w1b = sb("w1b", [P, 2, F0 + KF])
        hT = sb("hT", [P, 2, KF, P])
        ysb = sb("ysb", [P, 2, 2, C])
        xs_d = nc.dram_tensor("xs_sorted", [TILES * P, C], F32).ap()
        ys_d = nc.dram_tensor("ys_sorted", [TILES * P, C], F32).ap()

        early.close()
        scope[0] = ctx
        cnt_all = sb("cnt_all", [E1, B * T])
        mid = ExitStack()
        scope[0] = mid
        yg = sb("yg", [P, 2, 2, C])
        idx_g = sb("idx_g", [P, 2, 2], I32)
        gate_g = sb("gate_g", [P, 2, 2])
        tab = sb("tab", [P, 2, 2, C + E1])
        xT1 = sb("xT1", [P, 2, T])
        xp = sb("xp", [P, 2, NL])
        xr = sb("xr", [P, 2, NB, 4, W])
        xpr = sb("xpr", [P, 2, 2, 4, W])
        qx = sb("qx", [P, 2, NB, 4, W])
        qs = sb("qs", [P, 2, T])
        km = sb("km", [P, 2, 4, W + T])
        gqx = sb("gqx", [P, 2, NB, 4, W])
        gkm = sb("gkm", [P, 2, 2, NL])
        vx = sb("vx", [P, 2, NB, C])
        gvx = sb("gvx", [P, 2, 2, DL])
        lg1 = sb("lg1", [P, 2, E1 + 1])
        mx8 = sb("mx8", [P, 2, 8])
        lgr = sb("lgr", [P, 2, E1])
        mb = sb("mb", [P, 2, 2, E1], BF16)
        shl = sb("shl", [P, 2, E1])
        exl = sb("exl", [P, 2, E1])
        tsg = sb("tsg", [P, 2])
        sgc = sb("sgc", [P, 2, 2])
        wsum = sb("wsum", [P, 2, 2])
        carry = sb("carry", [E1, 2, 1])
        mxs = sb("mxs", [P, 2, 12])
        pr = sb("pr", [P, 2, 12 * NL])
        pt = sb("pt", [P, NB, 6, 2, W])
        tsh = sb("tsh", [P, 2 * T])
        shT = sb("shT", [P, IS // P, T])
        rdr = sb("rdr", [DL, T])
        remn = sb("remn", [DL, T])
        rdl = sb("rdl", [P, T])
        tg = sb("tg", [P, 2, T])
        at1 = sb("at1", [P, T])
        at2 = sb("at2", [P, T])
        aT = sb("aT", [P, T])
        res = sb("res", [P, 2, 2, C])
        mid.close()
        scope[0] = ctx
        CAP = 64
        IE = a["L1_ffn_expert_down_w"].shape[1]
        GE = 8
        GH = GE // 2
        EH = E1 // 2
        SLOTS = (slice(0, CAP), slice(CAP, 2 * CAP))
        NG = E1 // GE
        RW = C + E1
        slot_i = sb("slot_i", [P, 1], I32)
        slot_f = sb("slot_f", [P, 2])
        full_tiles = sb("full_tiles", [E1, CAP, NT])
        tile_row = sb("tile_row", [E1, CAP])
        tile_rows = sb("tile_rows", [E1, 2, 2, CAP])
        tile_at = sb("tile_at", [P, EH])
        row_at = sb("row_at", [P, EH], I32)
        ridx = sb("ridx", [P, 2, GH], I32)
        cg = sb("cg", [P, 2, GH, P])
        below = sb("below", [P, GH, P])
        tok = sb("tok", [P, 2, GH])
        dump = sb("dump", [P, GH])
        sidx = sb("sidx", [P, 2, GH], I32)
        aidx = sb("aidx", [CAP, 2, 2, GH], I32)
        xg = sb("xg", [P, 2, GH, RW])
        xgT = sb("xgT", [P, 2, GE * CAP])
        wge = sb("wge", [P, 2, GE, 2 * IE])
        wde = sb("wde", [IE, 2, GE, C])
        the = sb("the", [IE, GE * CAP])
        ae = sb("ae", [IE, GE * CAP])
        wblk = sb("wblk", [P, 2, GH * GE])
        yo = sb("yo", [P, 2, GH, C])
        cnt_d = nc.dram_tensor("counts", [E1 * NT, P], F32).ap()
        PAD = P
        xtab_d = nc.dram_tensor("xtab", [B * T + PAD, C + E1], F32).ap()
        acc_d = nc.dram_tensor("acc", [B * T + PAD, C], F32).ap()

        names = """consts zeroed zeroed1 w_in x_in0 x_in1 bn stats_done var rstd_done xn_done xn_kept xnT_ps xnT_sb kv_ps kv_sb
        q_ps q_sb s_ps red_done mT_ps mT_sb st_ps exp_done av_done rz_done y_sb zt_ps zt_sb out_ps xa_done cst dumped passed xs_zero rt ex0 rk_ps staged scat0 scat1 te_done xs_in0 xs_in1 w1_sb xsT_ps xsT_sb h_ps h_act h_dve
        yt_ps yt_sb ys_out0 ys_out1 yg_t x1_all te_go w1_in pads
        yg0 yg1 gidx x1_done bn1 stats1 var1 rstd1 xn1_done tT_ps tT_sb xp_done qk_ps rt_ps rt_sb qx_done kt_sb g_ps g_sb gk_sb
        rstep M_done ex_in ex_done tab_done cnt_ps cnt_sb v_ps v_sb s2_ps red2 sub_done exp2 tr_done shg_ps shu_ps tanh_sh
        sh1_done sh_sb shd_ps av_ps rd_done remn_done rem2_ps gate_ps gate_sb comb aT_done ao_ps r1_done res_done
        tab_out0 tab_out1 res_out0 res_out1 l1_consts wprep xpr_sb slots cnt_out f4 cg_in0 cg_in1 sel sidx_done xg_in0 xg_in1 xgT_ps xgT_sb gu_ps
        the_sb ae1 ae_sb oe_ps wblk_sb yo_sb rix added aidx_done we_in0 we_in1 tr4 m_in0 m_in1 kb_sb qb_sb rz_ps rzb_sb""".split()
        S = {n: sem(n) for n in names}
        x_in = [S["x_in0"], S["x_in1"]]
        block = ctx.enter_context(nc.Block())

        def passed(eng):
            eng.sem_inc(S["passed"], 1)

        NW = 16 + 4 + 2 * KF + 1
        hbank = [bankS, bankT]
        xv = x.rearrange("b (t p) c -> p (b t) c", p=P)
        LOOP = B // 2 - 1
        MAX_BEFORE = ((), (), (0,), (1,), (3,), (4,), (6,), (7,), ())
        MAX_AFTER = ((), (), (), (2,), (), (5,), (), (), ())
        DENS = ((), (0,), (1,), (), (2,), (3,), (), (4,), (5,))
        SPREAD = ((), (), (0,), (1,), (), (2,), (3,), (), (4,))

        def heads_of(k):
            return 3 if k else 1

        @block.sync
        def _(sp):
            sp.dma_start(xa_all[:, 0:4, :], xv[:, 0:4, :]).then_inc(x_in[0], 16)
            sp.wait_ge(S["zeroed"], 5)
            for e in range(2):
                sp.dma_start(wd[:, :, e, 0:L], a["L0_attn_Wd_w"].rearrange("(j e) c l -> e c j l", e=2)[e]).then_inc(S["w_in"], 16)
                sp.dma_start(bd[LP * e:LP * e + L, :], a["L0_attn_Wd_b"].rearrange("(j e) l -> e l j", e=2)[e]).then_inc(S["w_in"], 16)
                sp.dma_start(lw[:, e, 0:L], a["L0_attn_latent_w"]).then_inc(S["w_in"], 16)
                sp.dma_start(lb[LP * e:LP * e + L, :], a["L0_attn_latent_b"].rearrange("(l o) -> l o", o=1)).then_inc(S["w_in"], 16)
            sp.dma_start(lwr[:, 0:L], a["L0_attn_latent_w"]).then_inc(S["w_in"], 16)
            sp.dma_start(lbrow[:, 0:L], a["L0_attn_latent_b"].rearrange("(o l) -> o l", o=1)).then_inc(S["w_in"], 16)
            sp.dma_start(lwr[:, L:LR], a["L0_ffn_Wr"]).then_inc(S["w_in"], 16)
            sp.dma_start(lbrow[:, L:LR], a["L0_ffn_br"].rearrange("(o l) -> o l", o=1)).then_inc(S["w_in"], 16)
            oh = a["L0_attn_out_w"].rearrange("(h l) c -> l h c", l=L)
            for j, l0, r0, n in PARTS:
                sp.dma_start(ow[r0:r0 + n, 1:TRIPLES, :], oh[l0:l0 + n, j + 1:H:3, :]).then_inc(S["w_in"], 16)
            sp.dma_start(ow[0:L, 0, :], oh[:, 0, :]).then_inc(S["w_in"], 16)
            sp.dma_start(ob[:, :], a["L0_attn_out_b"].rearrange("(o l) -> o l", o=1)).then_inc(S["w_in"], 16)
            for k in range(XCH):
                lo, hi = (4 if k == 0 else k * NT // XCH), (k + 1) * NT // XCH
                sp.dma_start(xa_all[:, lo:hi, :], xv[:, lo:hi, :]).then_inc(x_in[1], 16)
            for e in range(2):
                lo, hi = e * E0 // 2, (e + 1) * E0 // 2
                sp.dma_start(wall[:, lo:hi, 0:F0], a["L0_ffn_W1"][lo:hi].rearrange("e c f -> c e f")).then_inc(S["w_in"], 16)
            for k in range(KF):
                sp.dma_start(wall[:, :, F0 + KF + k * C:F0 + KF + (k + 1) * C],
                             a["L0_ffn_W2"].rearrange("e (k p) c -> k p e c", p=P)[k]).then_inc(S["w_in"], 16)
                sp.dma_start(wall[:, :, F0 + k:F0 + k + 1], a["L0_ffn_b1"].rearrange("e (k p o) -> k p e o", p=P, o=1)[k]).then_inc(S["w_in"], 16)
            sp.dma_start(b2row[:, :, :], a["L0_ffn_b2"].rearrange("(o e) c -> o e c", o=1)).then_inc(S["w_in"], 16)
            sp.dma_start(xs_d.rearrange("(j p) c -> p j c", p=P), zeros[:, :].unsqueeze(1).to_broadcast([P, TILES, C])).then_inc(S["xs_zero"], 16)
            sp.wait_ge(S["zeroed1"], 1)
            for k, w in enumerate(("wq", "wk")):
                sp.dma_start(wqk[:, k, :], a["L1_attn_" + w]).then_inc(S["w1_in"], 16)
                sp.dma_start(wgqk[:, k, 0:DL], a["L1_attn_" + ("wgq", "wgk")[k]]).then_inc(S["w1_in"], 16)
                sp.dma_start(gcol[:, k:k + 1], a["L1_attn_gate_" + ("local_w", "remote_w")[k]].rearrange("h (d o) -> (h d) o", o=1)).then_inc(S["w1_in"], 16)
            sp.dma_start(wv[:, :], a["L1_attn_wv"]).then_inc(S["w1_in"], 16)
            sp.dma_start(wgv[:, :], a["L1_attn_wgv"]).then_inc(S["w1_in"], 16)
            sp.dma_start(wro[:, :], a["L1_attn_r_out_w"]).then_inc(S["w1_in"], 16)
            sp.dma_start(wo1[:, :], a["L1_attn_w_out"]).then_inc(S["w1_in"], 16)
            sp.dma_start(gw[:, 0:E1], a["L1_ffn_gate_w"]).then_inc(S["w1_in"], 16)
            sp.dma_start(gw[:, E1:E1 + 1], a["L1_ffn_shared_gate_w"]).then_inc(S["w1_in"], 16)
            sp.dma_start(sgu[:, :], a["L1_ffn_shared_gate_up_w"]).then_inc(S["w1_in"], 16)
            sp.dma_start(sdw[:, :, :], a["L1_ffn_shared_down_w"].rearrange("(k p) c -> p k c", p=P)).then_inc(S["w1_in"], 16)
            sp.dma_start(acc_d[B * T:B * T + PAD, :], zeros[:, :]).then_inc(S["pads"], 16)
            sp.dma_start(xtab_d[B * T:B * T + PAD, 0:C], zeros[:, :]).then_inc(S["pads"], 16)
            sp.dma_start(xtab_d[B * T:B * T + PAD, C:C + E1], zeros[:, 0:E1]).then_inc(S["pads"], 16)

            def maxima(n):
                sp.wait_ge(S["mT_sb"], n.b + 1)
                for e in range(2):
                    r = LP * e + L
                    sp.dma_start(qT[r:r + 1, n.half], mT[PAIRS * e:PAIRS * (e + 1), n.half, :]).then_inc(S[f"m_in{n.half}"], 16)

            with sp.Fori(0, B // 2) as i:
                maxima(Batch(i, 0))
                maxima(Batch(i, 1))

            def load(i, u):
                sp.dma_start(xsb[:, u], xs_d[bass.ds((i * 2 + u) * 2 * P, 2 * P), :].rearrange("(t p) c -> p t c", p=P)).then_inc(S[f"xs_in{u}"], 16)

            def store(i, u):
                sp.wait_ge(S["yt_sb"], i * 4 + (2 * u + 4))
                sp.dma_start(ys_d[bass.ds((i * 2 + u) * 2 * P, 2 * P), :].rearrange("(t p) c -> p t c", p=P), ysb[:, u]).then_inc(S[f"ys_out{u}"], 16)

            sp.wait_ge(S["scat0"], 16 * (NT // 2))
            sp.wait_ge(S["scat1"], 16 * (NT // 2))
            load(0, 0)
            load(0, 1)
            with sp.Fori(0, TILES // 4 - 1) as i:
                for u in range(2):
                    sp.wait_ge(S["xsT_ps"], i * 4 + (2 * u + 2))
                    load(i + 1, u)
                    store(i, u)
            for u in range(2):
                store(TILES // 4 - 1, u)
            for u in range(2):
                sp.wait_ge(S[f"ys_out{u}"], 16 * (TILES // 4) + 16)

            def save_table(n):
                sp.wait_ge(S["tab_done"], n.b + 1)
                sp.dma_start(xtab_d[bass.ds(n.b * T, T), :].rearrange("(t p) c -> p t c", p=P), tab[:, n.half]).then_inc(S[f"tab_out{n.half}"], 16)

            def save_stream(b):
                sp.wait_ge(S["res_done"], b.b + 2)
                sp.dma_start(acc_d[bass.ds(b.b * T, T), :].rearrange("(t p) c -> p t c", p=P), res[:, b.half]).then_inc(S[f"res_out{b.half}"], 16)

            save_table(Batch(0, 0))
            with sp.Fori(0, LOOP) as i:
                for b in (Batch(i, 0), Batch(i, 1)):
                    save_table(b.next())
                    save_stream(b)
            save_table(Batch(LOOP, 1))
            save_stream(Batch(LOOP, 0))
            save_stream(Batch(LOOP, 1))
            for u in range(2):
                sp.wait_ge(S[f"res_out{u}"], 16 * (B // 2) + 16)
                sp.wait_ge(S[f"tab_out{u}"], 16 * (B // 2) + 16)
            sp.wait_ge(S["cnt_sb"], B + 1)
            sp.dma_start(cnt_d.rearrange("(e n) p -> e (n p)", e=E1), cnt_all[:, :]).then_inc(S["cnt_out"], 16)

            def weights(g):
                u = g.half
                sp.dma_start(wge[:, u], a["L1_ffn_expert_gate_up_w"][bass.ds(g.b * GE, GE)].rearrange("e h f -> h e f")).then_inc(S[f"we_in{u}"], 16)
                sp.dma_start(wde[:, u], a["L1_ffn_expert_down_w"][bass.ds(g.b * GE, GE)].rearrange("e i h -> i e h")).then_inc(S[f"we_in{u}"], 16)

            weights(Batch(0, 0))
            weights(Batch(0, 1))
            with sp.Fori(0, NG // 2 - 1) as i:
                for g in (Batch(i, 0), Batch(i, 1)):
                    sp.wait_ge(S["oe_ps"], g.b + 1)
                    weights(g.next().next())
            sp.wait_ge(S["added"], 16 * E1)
            sp.dma_start(out.rearrange("b t c -> (b t) c"), acc_d[0:B * T, :]).then_inc(S["dumped"], 16)
            sp.wait_ge(S["dumped"], 16)

        @block.gpsimd
        def _(pool):
            pool.memset(zeros[:, :], 0.0)
            pool.memset(wd[:, :, :, :], 0.0).then_inc(S["zeroed"], 1)
            pool.memset(lw[:, :, :], 0.0).then_inc(S["zeroed"], 1)
            pool.memset(bd[:, :], 0.0).then_inc(S["zeroed"], 1)
            pool.memset(lb[:, :], 0.0).then_inc(S["cst"], 1)
            pool.wait_ge(S["cst"], 1)
            pool.affine_select(out=lb[:, :], in_=lb[:, :], compare_op=ALU.not_equal, fill=1.0, base=-L,
                               pattern=[[0, 1]], channel_multiplier=1).then_inc(S["cst"], 1)
            pool.wait_ge(S["cst"], 2)
            pool.affine_select(out=lb[:, :], in_=lb[:, :], compare_op=ALU.not_equal, fill=1.0, base=-(L + LP),
                               pattern=[[0, 1]], channel_multiplier=1).then_inc(S["zeroed"], 1)
            pool.memset(ones[:, :], 1.0)
            pool.memset(halfneg[:, :], -0.5)
            pool.memset(ow[:, :, :], 0.0).then_inc(S["zeroed"], 1)
            pool.memset(headsel[:, :], 0.0)
            pool.memset(vaug[:, :, :, :, :], 0.0)
            pool.memset(kT[:, :, :, :], 0.0)
            pool.memset(onesb[:, :], 1.0)
            pool.memset(strict[:, :], 1.0)
            pool.iota(iota_i[:, :], pattern=[[1, TILES]], base=0, channel_multiplier=0)
            pool.memset(ident[:, :], 0.0)
            pool.memset(identb[:, :], 0.0)
            pool.memset(maskq[:, :], 0.0)
            pool.memset(maskk[:, :], 0.0).then_inc(S["cst"], 1)
            pool.wait_ge(S["cst"], 3)
            for j in range(3):
                pool.memset(vaug[:, :, :, j, DEN + j:DEN + j + 1], 1.0)
            for j, _, r0, n in PARTS:
                pool.affine_select(out=headsel[:, r0:r0 + n], in_=headsel[:, r0:r0 + n], compare_op=ALU.not_equal, fill=1.0,
                                   base=-(DEN + j), pattern=[[0, n]], channel_multiplier=1)
            for m in (ident, identb):
                pool.affine_select(out=m[:, :], in_=m[:, :], compare_op=ALU.not_equal, fill=1.0, base=0,
                                   pattern=[[-1, P]], channel_multiplier=1)
            pool.affine_select(out=maskq[:, :], in_=maskq[:, :], compare_op=ALU.is_ge, fill=NEG, base=0,
                               pattern=[[-1, P]], channel_multiplier=1)
            pool.affine_select(out=strict[:, :], in_=strict[:, :], compare_op=ALU.is_gt, fill=0.0, base=0,
                               pattern=[[1, P]], channel_multiplier=-1)
            pool.affine_select(out=maskk[:, :], in_=maskk[:, :], compare_op=ALU.is_ge, fill=NEG, base=0,
                               pattern=[[1, P]], channel_multiplier=-1).then_inc(S["consts"], 1)

            made = 3

            def chain(ins):
                nonlocal made
                made += 1
                ins.then_inc(S["cst"], 1)
                pool.wait_ge(S["cst"], made)

            def keep(v, op, fill, base, pattern, step):
                chain(pool.affine_select(out=v, in_=v, compare_op=op, fill=fill, base=base, pattern=pattern, channel_multiplier=step))

            pool.memset(wgqk[:, :, :], 0.0).then_inc(S["zeroed1"], 1)
            pool.memset(maskl[:, :, :], 0.0)
            pool.memset(maskr[:, :, :], 0.0)
            pool.memset(headcol[:, :], 1.0)
            pool.memset(quadcol[:, :], 0.0)
            pool.memset(upto[:, :, :], 1.0)
            chain(pool.memset(block16[:, :], 1.0))
            keep(block16[:, :], ALU.is_ge, 0.0, 0, [[-8, 16], [0, 8]], 1)
            keep(block16[:, :], ALU.is_ge, 0.0, 7, [[8, 16], [0, 8]], -1)
            keep(upto[:, 0, :], ALU.is_ge, 0.0, 0, [[1, P]], -1)
            for g in range(4):
                q = slice(W * g, W * g + W)
                keep(maskl[q], ALU.is_gt, NEG, 0, [[0, 2], [1, 2 * W]], -1)
                keep(maskl[q], ALU.is_ge, NEG, W, [[0, 2], [-1, 2 * W]], 1)
                keep(maskr[q], ALU.is_ge, NEG, 0, [[W, NB], [-CHUNK, NL]], 1)
                keep(headcol[q, :], ALU.is_ge, 0.0, 0, [[-8, 4]], 1)
                keep(headcol[q, :], ALU.is_ge, 0.0, 7, [[8, 4]], -1)
                chain(pool.memset(quadcol[q, :].rearrange("p (a h d) -> p a h d", h=4, d=8)[:, :, g, :], 1.0))
            pool.memset(maskl[:, 0, 0:W], NEG).then_inc(S["l1_consts"], 1)
            pool.wait_ge(S["l1_consts"], 1)

            def deviation0(m):
                pool.wait_ge(S["stats_done"], m.b + 1)
                passed(pool)
                pool.tensor_scalar(rstd[:, 0], mv[:, :, 1], EPS, None, ALU.add).then_inc(S["var"], 1)
                pool.wait_ge(S["var"], m.b + 1)
                pool.tensor_tensor(rstd[:, 1], rstd[:, 0], halfneg[:, :], ALU.pow).then_inc(S["rstd_done"], 1)

            def keep_rows(m):
                pool.wait_ge(S["xn_done"], m.b + 1)
                pool.tensor_copy(xn_all[:, bass.ds(m.b * 2, 2), :], xn[:, m.half]).then_inc(S["xn_kept"], 1)

            def round_keys(n):
                pool.wait_ge(S["kv_sb"], n.b + 1)
                passed(pool)
                pool.tensor_copy(kb[:, :, :], kT[:, n.half, :, :]).then_inc(S["kb_sb"], 1)

            def round_queries(n, r):
                for j in (2 * r, 2 * r + 1):
                    pool.wait_ge(S["q_sb"], n.b * PAIRS + (j + 1))
                    passed(pool)
                    pool.tensor_copy(qb[:, j, :], qT[:, n.half, j, :]).then_inc(S["qb_sb"], 1)

            def stage_a(n, m):
                round_keys(n)
                round_queries(n, 0)
                if m:
                    deviation0(m)
                round_queries(n, 1)
                if m:
                    keep_rows(m)
                round_queries(n, 2)
                round_queries(n, 3)

            first, second = Batch(0, 0), Batch(0, 1)
            deviation0(first)
            keep_rows(first)
            round_keys(first)
            deviation0(second)
            keep_rows(second)
            for r in range(4):
                round_queries(first, r)
            with pool.Fori(0, LOOP) as i:
                stage_a(Batch(i, 1), Batch(i + 1, 0))
                stage_a(Batch(i + 1, 0), Batch(i + 1, 1))
            stage_a(Batch(LOOP, 1), None)

            pool.wait_ge(S["te_done"], 1)
            pool.wait_ge(S["xs_zero"], 16)

            def scatter(i, u):
                pool.wait_ge(S["staged"], i * 2 + (u + 1))
                passed(pool)
                for k in range(SG):
                    pool.indirect_dma_start(out=xs_d, out_offset=bass.IndirectOffsetOnAxis(ap=stage_p[:, u, k:k + 1], axis=0),
                                            in_=stage_x[:, u, k, :], in_offset=None).then_inc(S[f"scat{u}"], 16)

            with pool.Fori(0, NT // (2 * SG)) as i:
                for u in range(2):
                    scatter(i, u)

            for u in range(2):
                pool.wait_ge(S[f"ys_out{u}"], 16 * (TILES // 4) + 16)
                pool.wait_ge(S[f"scat{u}"], 16 * (NT // 2))

            pool.memset(km[:, :, :, :], 0.0)
            pool.memset(gkm[:, :, :, :], 0.0)
            pool.memset(carry[:, :, :], 0.0).then_inc(S["pads"], 16)

            def gather(m):
                u = m.half
                pool.tensor_copy(idx_g[:, u, :], pos_all[:, bass.ds(m.b * 2, 2)])
                pool.tensor_copy(gate_g[:, u, :], gate_all[:, bass.ds(m.b * 2, 2)]).then_inc(S["gidx"], 1)
                pool.wait_ge(S["gidx"], m.b + 1)
                passed(pool)
                for t in range(2):
                    pool.indirect_dma_start(out=yg[:, u, t, :], out_offset=None, in_=ys_d,
                                            in_offset=bass.IndirectOffsetOnAxis(ap=idx_g[:, u, t:t + 1], axis=0)).then_inc(S[f"yg{u}"], 16)

            def deviation(n):
                pool.wait_ge(S["stats1"], n.b + 1)
                passed(pool)
                pool.tensor_scalar(rstd[:, 0], mv[:, :, 1], EPS, None, ALU.add).then_inc(S["var1"], 1)
                pool.wait_ge(S["var1"], n.b + 1)
                pool.tensor_tensor(rstd[:, 1], rstd[:, 0], halfneg[:, :], ALU.pow).then_inc(S["rstd1"], 1)

            gather(Batch(0, 0))
            gather(Batch(0, 1))
            deviation(Batch(0, 0))
            with pool.Fori(0, LOOP) as i:
                for b in (Batch(i, 0), Batch(i, 1)):
                    deviation(b.next())
                    gather(b.next().next())
            deviation(Batch(LOOP, 1))
            pool.iota(slot_i[:, :], pattern=[[0, 1]], base=0, channel_multiplier=1).then_inc(S["slots"], 1)
            for u in range(2):
                pool.wait_ge(S[f"res_out{u}"], 16 * (B // 2) + 16)
                pool.wait_ge(S[f"tab_out{u}"], 16 * (B // 2) + 16)
            pool.wait_ge(S["cnt_out"], 16)
            pool.wait_ge(S["f4"], 1)

            def rows_of(g):
                pool.tensor_copy(ridx[:, g.half, :], row_at[:, bass.ds(g.b * GH, GH)]).then_inc(S["rix"], 1)
                pool.wait_ge(S["rix"], g.b + 1)
                passed(pool)

            def count_rows(g, j):
                u = g.half
                pool.indirect_dma_start(out=cg[:, u, j, :], out_offset=None, in_=cnt_d,
                                        in_offset=bass.IndirectOffsetOnAxis(ap=ridx[:, u, j:j + 1], axis=0)).then_inc(S[f"cg_in{u}"], 16)

            def slots_ready(g):
                pool.wait_ge(S["sidx_done"], g.b + 1)
                passed(pool)

            def token_rows(g, j):
                u = g.half
                pool.indirect_dma_start(out=xg[:, u, j, :], out_offset=None, in_=xtab_d,
                                        in_offset=bass.IndirectOffsetOnAxis(ap=sidx[:, u, j:j + 1], axis=0)).then_inc(S[f"xg_in{u}"], 16)

            def add_rows(g, e):
                u, j, h = g.half, e // 2, e % 2
                pool.indirect_dma_start(out=acc_d, out_offset=bass.IndirectOffsetOnAxis(ap=aidx[:, u, h, j:j + 1], axis=0),
                                        in_=yo[SLOTS[h], u, j, :], in_offset=None, compute_op=ALU.add).then_inc(S["added"], 16)

            def step4(g, n1, n2, n3):
                if n3:
                    rows_of(n3)
                pool.wait_ge(S["yo_sb"], g.b + 1)
                passed(pool)
                pool.wait_ge(S["aidx_done"], g.b + 1)
                passed(pool)
                for e in range(GE):
                    j = e // 2
                    add_rows(g, e)
                    if e % 2 == 0:
                        if n3:
                            count_rows(n3, j)
                    elif j == 0:
                        if n1:
                            token_rows(n1, GH - 1)
                    elif n2:
                        if j == 1:
                            slots_ready(n2)
                        token_rows(n2, j - 1)
                    pool.wait_ge(S["added"], (g.b * GE + (e + 1)) * 16)
                    passed(pool)

            for b in range(3):
                rows_of(Batch(b // 2, b % 2))
                if b:
                    slots_ready(Batch(0, b - 1))
                for j in range(GH):
                    count_rows(Batch(b // 2, b % 2), j)
                    if b == 1 or b == 2 and j < GH - 1:
                        token_rows(Batch(0, b - 1), j)
            with pool.Fori(0, NG // 2 - 2) as i:
                step4(Batch(i, 0), Batch(i, 1), Batch(i + 1, 0), Batch(i + 1, 1))
                step4(Batch(i, 1), Batch(i + 1, 0), Batch(i + 1, 1), Batch(i + 2, 0))
            L4 = NG // 2 - 2
            step4(Batch(L4, 0), Batch(L4, 1), Batch(L4 + 1, 0), Batch(L4 + 1, 1))
            step4(Batch(L4, 1), Batch(L4 + 1, 0), Batch(L4 + 1, 1), None)
            step4(Batch(L4 + 1, 0), Batch(L4 + 1, 1), None, None)
            step4(Batch(L4 + 1, 1), None, None, None)

        @block.vector
        def _(dve):
            def stats0(n, chunks):
                if chunks:
                    dve.wait_ge(x_in[1], 16 * chunks)
                else:
                    dve.wait_ge(x_in[0], 16)
                passed(dve)
                for t in range(2):
                    ins = dve.bn_stats(stats[:, t, :], xa_all[:, bass.ds(n.b * 2 + t, 1), :].rearrange("p a c -> p (a c)"))
                ins.then_inc(S["bn"], 1)
                dve.wait_ge(S["bn"], n.b + 1)
                passed(dve)
                for t in range(2):
                    ins = dve.bn_aggr(mv[:, t, :], stats[:, t, :])
                ins.then_inc(S["stats_done"], 1)

            def norm(n, prior):
                u = n.half
                if prior:
                    dve.wait_ge(S["xn_kept"], n.b - 1)
                    dve.wait_ge(S["xnT_ps"], n.b - 1)
                dve.wait_ge(S["rstd_done"], n.b + 1)
                dve.wait_ge(S["stats_done"], n.b + 1)
                for t in range(2):
                    ins = dve.tensor_scalar(xn[:, u, t, :], xa_all[:, bass.ds(n.b * 2 + t, 1), :].rearrange("p a c -> p (a c)"),
                                            mv[:, t, 0:1], rstd[:, 1, t:t + 1], ALU.subtract, ALU.mult)
                ins.then_inc(S["xn_done"], 1)

            def kv(n):
                u = n.half
                dve.wait_ge(S["kv_ps"], n.b + 1)
                for e in range(2):
                    r = slice(LP * e, LP * (e + 1))
                    dve.tensor_scalar(kT[r, u, e, :], bankB[r, 0:T], lb[r, 0:1], None, ALU.add)
                values = bankB[:, 256:256 + 2 * LR].rearrange("p (t l) -> p t l", t=2)
                for j, l0, r0, w in PARTS:
                    dve.tensor_copy(vaug[:, u, :, j, r0:r0 + w], values[:, :, l0:l0 + w])
                dve.tensor_copy(lg_all[:, bass.ds(n.b * 2, 2), :],
                                values[:, :, L:LR]).then_inc(S["kv_sb"], 1)

            def red(n, g):
                dve.wait_ge(S["s_ps"], n.b * PAIRS + (g + 1))
                dve.tensor_reduce(mneg[:, n.half, 0, :, g], bankS[:, :, 0:128], AX.X, ALU.max, negate=True)
                dve.tensor_reduce(mneg[:, n.half, 1, :, g], bankS[:, :, 128:384], AX.X, ALU.max,
                                  negate=True).then_inc(S["red_done"], 1)

            def denominators(b, k):
                dens = slice(DEN, DEN + heads_of(k))
                dve.wait_ge(S["av_done"], b.b * H + (3 * k + 1))
                dve.reciprocal(rz[dens, k % 2, :], bankY[k % 2][dens, 0:T]).then_inc(S["rz_done"], 1)

            def normalise(b, k):
                dve.wait_ge(S["rz_ps"], b.b * TRIPLES + (k + 1))
                dve.tensor_copy(rzb[0:ROWS, k % 2, :], bankY[k % 2][0:ROWS, T:2 * T]).then_inc(S["rzb_sb"], 1)
                dve.wait_ge(S["rzb_sb"], b.b * TRIPLES + (k + 1))
                dve.tensor_tensor(zT[0:ROWS, b.half, k, :], bankY[k % 2][0:ROWS, 0:T], rzb[0:ROWS, k % 2, :], ALU.mult).then_inc(S["y_sb"], 1)

            def resid(b):
                dve.wait_ge(S["out_ps"], b.b + 1)
                for t in range(2):
                    row = xa_all[:, bass.ds(b.b * 2 + t, 1), :].rearrange("p a c -> p (a c)")
                    ins = dve.tensor_tensor(row, (bankB, bankY[0])[t][:, 0:C], row, ALU.add)
                ins.then_inc(S["xa_done"], 1)

            def step(b, n, m):
                for g in range(1, PAIRS + 1):
                    if n and g == 1:
                        kv(n)
                    for k in SPREAD[g]:
                        normalise(b, k)
                    for r in MAX_BEFORE[g] if n else ():
                        red(n, r)
                    for k in DENS[g]:
                        denominators(b, k)
                    for r in MAX_AFTER[g] if n else ():
                        red(n, r)
                    if m and g == 2:
                        stats0(m, XCH)
                    if m and g == 3:
                        norm(m, True)
                normalise(b, TRIPLES - 1)
                resid(b)

            dve.sem_inc(S["xa_done"], 1)
            dve.sem_inc(S["red_done"], 1)
            dve.sem_inc(S["y_sb"], 2)
            dve.wait_ge(S["w_in"], 16 * NW)
            dve.wait_ge(S["consts"], 1)
            first, second = Batch(0, 0), Batch(0, 1)
            stats0(first, 0)
            norm(first, False)
            kv(first)
            stats0(second, 0)
            norm(second, False)
            for g in range(PAIRS):
                red(first, g)
            with dve.Fori(0, LOOP) as i:
                step(Batch(i, 0), Batch(i, 1), Batch(i + 1, 0))
                step(Batch(i, 1), Batch(i + 1, 0), Batch(i + 1, 1))
            step(Batch(LOOP, 0), Batch(LOOP, 1), None)
            step(Batch(LOOP, 1), None, None)

            done = 0

            def link(ins):
                nonlocal done
                done += 1
                ins.then_inc(S["rt"], 1)
                dve.wait_ge(S["rt"], done)

            def cast(v, shape):
                return v.to_broadcast(shape)

            full = [P, NT, E0]
            dve.wait_ge(S["kv_sb"], B)
            dve.wait_ge(S["xn_kept"], B)
            link(dve.tensor_copy(iota_f[:, :], iota_i[:, :]))
            link(dve.tensor_reduce(mx0[:, :], lg_all[:, :, :], AX.X, ALU.max))
            link(dve.tensor_tensor(lgs0[:, :, :], lg_all[:, :, :], cast(mx0[:, :].unsqueeze(2), full), ALU.subtract))
            link(dve.tensor_tensor(eq0[:, :, :], lg_all[:, :, :], cast(mx0[:, :].unsqueeze(2), full), ALU.is_equal))
            link(dve.tensor_scalar(pbase[:, :], iota_f[:, 0:E0], -1.0, float(E0), ALU.mult, ALU.add))
            link(dve.tensor_tensor(eq0[:, :, :], eq0[:, :, :], cast(pbase[:, :].unsqueeze(1), full), ALU.mult))
            link(dve.tensor_reduce(mx0[:, :], eq0[:, :, :], AX.X, ALU.max))
            link(dve.tensor_tensor(oh0[:, :, :], eq0[:, :, :], cast(mx0[:, :].unsqueeze(2), full), ALU.is_equal))
            dve.sem_inc(S["te_go"], 1)
            dve.wait_ge(S["ex0"], 1)
            link(dve.tensor_reduce(posf[:, :], lgs0[:, :, :], AX.X, ALU.add))
            link(dve.reciprocal(gate_all[:, :], posf[:, :]))
            dve.wait_ge(S["rk_ps"], 1)
            link(dve.tensor_copy(tot0[:, :, :], bankB[:, :].rearrange("p (n e) -> p n e", e=E0)))
            for e in range(E0):
                ins = dve.tensor_tensor_scan(cs0[:, :, e], cast(iota_f[:, 1:2], [P, NT]), tot0[:, :, e], 0.0, ALU.mult, ALU.add)
            link(ins)
            link(dve.tensor_scalar(cnt_i[:, 0, :], cs0[:, NT - 1, :], float(P - 1), None, ALU.add))
            link(dve.tensor_scalar(cnt_i[:, 1, :], cnt_i[:, 0, :], P.bit_length() - 1, None, ALU.arith_shift_right))
            link(dve.tensor_copy(ptile[:, :], cnt_i[:, 1, :]))
            link(dve.tensor_tensor_scan(pend[:, :], cast(iota_f[:, 1:2], [P, E0]), ptile[:, :], 0.0, ALU.mult, ALU.add))
            link(dve.tensor_tensor(pbase[:, :], pend[:, :], ptile[:, :], ALU.subtract))
            link(dve.tensor_scalar(pbase[:, :], pbase[:, :], float(P), None, ALU.mult))
            link(dve.tensor_tensor(cs0[:, :, :], cs0[:, :, :], tot0[:, :, :], ALU.subtract))
            link(dve.tensor_tensor(cs0[:, :, :], cs0[:, :, :], cast(pbase[:, :].unsqueeze(1), full), ALU.add))
            link(dve.tensor_tensor(cs0[:, :, :], bankA[:, :].rearrange("p (n e) -> p n e", e=E0), cs0[:, :, :], ALU.add))
            link(dve.tensor_tensor(cs0[:, :, :], cs0[:, :, :], oh0[:, :, :], ALU.mult))
            link(dve.tensor_reduce(posf[:, :], cs0[:, :, :], AX.X, ALU.add))
            link(dve.tensor_copy(pos_all[:, :], posf[:, :]))
            tiles = [P, TILES, E0]
            link(dve.tensor_tensor(tsel[:, :, :], cast(pend[:, :].unsqueeze(1), tiles), cast(iota_f[:, :].unsqueeze(2), tiles), ALU.is_le))
            link(dve.tensor_reduce(tef[:, :], tsel[:, :, :], AX.X, ALU.add))
            dve.tensor_scalar(te_i[:, :], tef[:, :], float(E0 - 1), None, ALU.min).then_inc(S["te_done"], 1)
            dve.wait_ge(S["te_done"], 1)

            def stage(i, u, first):
                if not first:
                    dve.wait_ge(S[f"scat{u}"], i * (16 * SG))
                n = (i * 2 + u) * SG
                dve.tensor_copy(stage_x[:, u], xn_all[:, bass.ds(n, SG), :])
                dve.tensor_copy(stage_p[:, u, :], pos_all[:, bass.ds(n, SG)]).then_inc(S["staged"], 1)

            dve.wait_ge(S["xn_kept"], B)
            for u in range(2):
                stage(0, u, True)
            with dve.Fori(1, NT // (2 * SG)) as i:
                for u in range(2):
                    stage(i, u, False)

            def first_weights(j, q):
                e = dve.value_load(te_i[0:1, bass.ds(j, 1)], min_val=0, max_val=E0 - 1)
                dve.tensor_copy(w1b[:, q % 2, :], wall[:, bass.ds(e, 1), 0:F0 + KF].rearrange("p a c -> p (a c)")).then_inc(S["w1_sb"], 1)

            def hidden(j, q):
                u = q % 2
                dve.wait_ge(S["w1_sb"], j + 1)
                dve.wait_ge(S["h_ps"], j + 1)
                for k in range(KF // 2, KF):
                    ins = dve.tensor_scalar(hT[:, u, k, :], hbank[u][:, 1, (k - KF // 2) * P:(k - KF // 2 + 1) * P],
                                            w1b[:, u, F0 + k:F0 + k + 1], 0.0, ALU.add, ALU.max)
                ins.then_inc(S["h_dve"], 1)

            def result(i, q):
                j = i * 4 + q
                if q % 2 == 0:
                    dve.wait_ge(S[f"ys_out{q // 2}"], i * 16 + 16)
                dve.wait_ge(S["yt_ps"], j + 1)
                dve.tensor_copy(ysb[:, q // 2, q % 2, :], bankY[q % 2][:, 0:C]).then_inc(S["yt_sb"], 1)

            def tile_step(i, q, left):
                j = i * 4 + q
                if left > 1:
                    hidden(j + 1, q + 1)
                if left > 3:
                    dve.wait_ge(S["h_act"], j + 2)
                    dve.wait_ge(S["h_dve"], j + 2)
                    first_weights(j + 3, q + 3)
                result(i, q)

            dve.sem_inc(S["yt_sb"], 2)
            for u in range(2):
                dve.sem_inc(S[f"ys_out{u}"], 16)
            first_weights(0, 0)
            first_weights(1, 1)
            hidden(0, 0)
            dve.wait_ge(S["h_act"], 1)
            dve.wait_ge(S["h_dve"], 1)
            first_weights(2, 2)
            with dve.Fori(0, TILES // 4 - 1) as i:
                for q in range(4):
                    tile_step(i, q, 8)
            for q in range(4):
                tile_step(TILES // 4 - 1, q, 4 - q)

            dve.sem_inc(S["res_done"], 1)
            dve.sem_inc(S["r1_done"], 1)
            dve.sem_inc(S["cnt_sb"], 1)
            for u in range(2):
                dve.sem_inc(S[f"res_out{u}"], 16)
                dve.sem_inc(S[f"tab_out{u}"], 16)
            dve.wait_ge(S["w1_in"], 16 * 14)
            dve.wait_ge(S["l1_consts"], 1)
            dve.wait_ge(S["pads"], 64)
            for k in range(2):
                dve.tensor_scalar(gates[:, k, :], block16[:, :], gcol[:, k:k + 1], None, ALU.mult)
            dve.tensor_scalar(wgqk[:, 1, :], wgqk[:, 1, :], 1.0 / CHUNK, None, ALU.mult)
            dve.tensor_scalar(wgv[:, :], wgv[:, :], 1.0 / CHUNK, None, ALU.mult)
            dve.tensor_scalar(wo1[:, :], wo1[:, :], 0.5, None, ALU.mult)
            dve.tensor_scalar(sdw[:, :, :], sdw[:, :, :], 0.5, None, ALU.mult).then_inc(S["wprep"], 1)

            def norm1(n, prior):
                u = n.half
                dve.wait_ge(S[f"yg{u}"], n.pair * 32 + 32)
                for t in range(2):
                    row = xa_all[:, bass.ds(n.b * 2 + t, 1), :].rearrange("p a c -> p (a c)")
                    ins = dve.scalar_tensor_tensor(row, yg[:, u, t, :], gate_g[:, u, t:t + 1], row, ALU.mult, ALU.add)
                ins.then_inc(S["x1_done"], 1)
                dve.wait_ge(S["x1_done"], n.b + 1)
                passed(dve)
                for t in range(2):
                    ins = dve.bn_stats(stats[:, t, :], xa_all[:, bass.ds(n.b * 2 + t, 1), :].rearrange("p a c -> p (a c)"))
                ins.then_inc(S["bn1"], 1)
                dve.wait_ge(S["bn1"], n.b + 1)
                passed(dve)
                for t in range(2):
                    ins = dve.bn_aggr(mv[:, t, :], stats[:, t, :])
                ins.then_inc(S["stats1"], 1)

            def norm1_end(n):
                u = n.half
                dve.wait_ge(S["rstd1"], n.b + 1)
                dve.wait_ge(S["stats1"], n.b + 1)
                dve.wait_ge(S[f"tab_out{u}"], n.pair * 16 + 16)
                for t in range(2):
                    ins = dve.tensor_scalar(tab[:, u, t, 0:C], xa_all[:, bass.ds(n.b * 2 + t, 1), :].rearrange("p a c -> p (a c)"),
                                            mv[:, t, 0:1], rstd[:, 1, t:t + 1], ALU.subtract, ALU.mult)
                ins.then_inc(S["xn1_done"], 1)

            def pool_latents(n):
                dve.wait_ge(S["tT_sb"], n.b * 2 + 1)
                dve.tensor_reduce(xp[:, n.half, :], xT1[:, n.half, :].rearrange("p (n k) -> p n k", k=CHUNK), AX.X,
                                  ALU.add).then_inc(S["xp_done"], 1)

            RSTEPS = 4

            def route(n):
                u = n.half
                dve.wait_ge(S["rt_ps"], n.b + 1)
                dve.tensor_copy(lg1[:, :, :], bank[0][:, 256:256 + 2 * (E1 + 1)].rearrange("p (t e) -> p t e", t=2)).then_inc(S["rt_sb"], 1)
                dve.wait_ge(S["rt_sb"], n.b + 1)
                passed(dve)
                for t in range(2):
                    ins = dve.max(mx8[:, t, :], lg1[:, t, 0:E1])
                ins.then_inc(S["rstep"], 1)
                dve.wait_ge(S["rstep"], n.b * RSTEPS + 1)
                passed(dve)
                for t in range(2):
                    ins = dve.match_replace(lgr[:, t, :], mx8[:, t, :], lg1[:, t, 0:E1], NEG)
                dve.tensor_tensor(shl[:, :, :], lg1[:, :, 0:E1], mx8[:, :, 0:1].to_broadcast([P, 2, E1]), ALU.subtract).then_inc(S["ex_in"], 1)
                dve.wait_ge(S["ex_in"], n.b + 1)
                dve.tensor_tensor(mb[:, u], lg1[:, :, 0:E1], lgr[:, :, :], ALU.not_equal).then_inc(S["M_done"], 1)

            def weigh(n):
                u = n.half
                dve.wait_ge(S["ex_done"], n.b + 1)
                dve.wait_ge(S["M_done"], n.b + 1)
                dve.tensor_tensor(exl[:, :, :], exl[:, :, :], mb[:, u], ALU.mult).then_inc(S["rstep"], 1)
                dve.wait_ge(S["rstep"], n.b * RSTEPS + 2)
                dve.tensor_reduce(wsum[:, 0, :], exl[:, :, :], AX.X, ALU.add).then_inc(S["rstep"], 1)
                dve.wait_ge(S["rstep"], n.b * RSTEPS + 3)
                dve.reciprocal(wsum[:, 1, :], wsum[:, 0, :]).then_inc(S["rstep"], 1)
                dve.wait_ge(S["rstep"], n.b * RSTEPS + 4)
                dve.tensor_scalar(sgc[:, u, :], tsg[:, :], 0.5, 0.5, ALU.mult, ALU.add)
                dve.tensor_tensor(tab[:, u, :, C:C + E1], exl[:, :, :], wsum[:, 1, :].unsqueeze(2).to_broadcast([P, 2, E1]),
                                  ALU.mult).then_inc(S["tab_done"], 1)

            def latents(n):
                u = n.half
                dve.wait_ge(S["g_ps"], n.b + 1)
                dve.tensor_tensor(gvx[:, u], bank[2][:, 320:320 + 2 * DL].rearrange("p (k c) -> p k c", k=2),
                                  quadcol[:, 0:DL].unsqueeze(1).to_broadcast([P, 2, DL]), ALU.mult).then_inc(S["g_sb"], 1)

            def values(n):
                for k in range(2):
                    dve.wait_ge(S["v_ps"], n.b * 2 + (k + 1))
                    dve.tensor_tensor(vx[:, n.half, 4 * k:4 * k + 4, :], bank[k][:, :].rearrange("p (n c) -> p n c", c=C),
                                      quadcol[:, :].unsqueeze(1).to_broadcast([P, 4, C]), ALU.mult).then_inc(S["v_sb"], 1)

            def shift(b, g):
                k = g % 2
                s = (bankS, bankT)[k][:, :, 0:6 * NL].rearrange("p b (g k) -> p b g k", k=NL)
                dve.wait_ge(S["s2_ps"], b.b * 4 + (g + 1))
                dve.tensor_reduce(mxs[:, k, :].rearrange("p (b g) -> p b g", b=2), s, AX.X, ALU.max).then_inc(S["red2"], 1)
                dve.wait_ge(S["red2"], b.b * 4 + (g + 1))
                if g >= 2:
                    dve.wait_ge(S["tr_done"], b.b * 4 + (g - 1))
                dve.tensor_tensor(pr[:, k, :].rearrange("p (b g k) -> p b g k", b=2, k=NL), s,
                                  mxs[:, k, :].rearrange("p (b g) -> p b g", b=2).unsqueeze(3).to_broadcast([P, 2, 6, NL]),
                                  ALU.subtract).then_inc(S["sub_done"], 1)

            def turn(b, g):
                dve.wait_ge(S["exp2"], b.b * 4 + (g + 1))
                dve.transpose(pt[:, 2 * g:2 * g + 2].rearrange("p b g k q -> p (b g k q)"), pr[:, g % 2, :]).then_inc(S["tr_done"], 1)

            def shared(b):
                dve.wait_ge(S["tanh_sh"], b.b + 1)
                h = shT[:, :, :].rearrange("p k t -> p (k t)")
                dve.scalar_tensor_tensor(h, tsh[:, :], 1.0, bank[0][:, :], ALU.add, ALU.mult).then_inc(S["sh1_done"], 1)
                dve.wait_ge(S["sh1_done"], b.b + 1)
                dve.wait_ge(S["shu_ps"], b.b + 1)
                dve.tensor_tensor(h, h, bank[1][:, :], ALU.mult).then_inc(S["sh_sb"], 1)

            def finish_remote(b):
                dve.wait_ge(S["av_ps"], b.b + 1)
                dve.reciprocal(rdr[:, :], bank[3][0:DL, T:2 * T]).then_inc(S["rd_done"], 1)
                dve.wait_ge(S["rd_done"], b.b + 1)
                dve.tensor_tensor(remn[:, :], bank[3][0:DL, 0:T], rdr[:, :], ALU.mult).then_inc(S["remn_done"], 1)
                dve.reciprocal(rdl[:, :], bank[2][:, T:2 * T])

            def combine(b):
                dve.wait_ge(S["gate_sb"], b.b + 2)
                dve.scalar_tensor_tensor(at1[:, :], tg[:, 0, :], 1.0, bank[2][:, 0:T], ALU.add, ALU.mult).then_inc(S["comb"], 1)
                dve.wait_ge(S["comb"], b.b * 3 + 1)
                dve.tensor_tensor(at1[:, :], at1[:, :], rdl[:, :], ALU.mult).then_inc(S["comb"], 1)
                dve.wait_ge(S["rem2_ps"], b.b + 1)
                dve.scalar_tensor_tensor(at2[:, :], tg[:, 1, :], 1.0, bank[3][:, 0:T], ALU.add, ALU.mult).then_inc(S["comb"], 1)
                dve.wait_ge(S["comb"], b.b * 3 + 3)
                dve.tensor_tensor(aT[:, :], at1[:, :], at2[:, :], ALU.add).then_inc(S["aT_done"], 1)

            def finish(b):
                u = b.half
                dve.wait_ge(S["shd_ps"], b.b + 1)
                dve.wait_ge(S[f"res_out{u}"], b.pair * 16 + 16)
                for t in range(2):
                    ins = dve.scalar_tensor_tensor(res[:, u, t, :], bank[1][:, t * C:(t + 1) * C], sgc[:, u, t:t + 1],
                                                   xa_all[:, bass.ds(b.b * 2 + t, 1), :].rearrange("p a c -> p (a c)"), ALU.mult, ALU.add)
                ins.then_inc(S["r1_done"], 1)
                dve.wait_ge(S["r1_done"], b.b + 2)
                dve.wait_ge(S["ao_ps"], b.b + 1)
                dve.tensor_tensor(res[:, u], bank[2][:, 0:2 * C].rearrange("p (t c) -> p t c", t=2), res[:, u],
                                  ALU.add).then_inc(S["res_done"], 1)

            def step1(b, n, m):
                if b:
                    shift(b, 0)
                    shift(b, 1)
                    turn(b, 0)
                if n:
                    pool_latents(n)
                if b:
                    shift(b, 2)
                    turn(b, 1)
                if n:
                    route(n)
                    latents(n)
                    values(n)
                if b:
                    shift(b, 3)
                    turn(b, 2)
                if n:
                    weigh(n)
                if b:
                    turn(b, 3)
                    shared(b)
                if m:
                    norm1(m, True)
                if b:
                    finish_remote(b)
                if m:
                    norm1_end(m)
                if b:
                    combine(b)
                    finish(b)

            norm1(Batch(0, 0), False)
            norm1_end(Batch(0, 0))
            step1(None, Batch(0, 0), Batch(0, 1))
            with dve.Fori(0, LOOP) as i:
                step1(Batch(i, 0), Batch(i, 1), Batch(i + 1, 0))
                step1(Batch(i, 1), Batch(i + 1, 0), Batch(i + 1, 1))
            step1(Batch(LOOP, 0), Batch(LOOP, 1), None)
            step1(Batch(LOOP, 1), None, None)
            steps4 = 0

            def link4(ins):
                nonlocal steps4
                steps4 += 1
                ins.then_inc(S["sel"], 1)
                dve.wait_ge(S["sel"], steps4)

            for u in range(2):
                dve.wait_ge(S[f"res_out{u}"], 16 * (B // 2) + 16)
                dve.wait_ge(S[f"tab_out{u}"], 16 * (B // 2) + 16)
            dve.wait_ge(S["cnt_sb"], B + 1)
            dve.wait_ge(S["slots"], 1)
            for h in range(2):
                dve.tensor_scalar(slot_f[SLOTS[h], 0:1], slot_i[SLOTS[h], :], float(-CAP * h), None, ALU.add)
            link4(dve.tensor_scalar(slot_f[:, 1:2], slot_i[:, :], float(NT), None, ALU.mult))
            link4(dve.tensor_tensor(full_tiles[:, :, :],
                                    cnt_all[:, :].rearrange("e (n p) -> e n p", p=P)[:, :, P - 1].unsqueeze(1).to_broadcast([E1, CAP, NT]),
                                    iota_f[0:E1, 0:CAP].unsqueeze(2).to_broadcast([E1, CAP, NT]), ALU.is_le))
            link4(dve.tensor_reduce(tile_row[:, :], full_tiles[:, :, :], AX.X, ALU.add))
            link4(dve.tensor_scalar(tile_row[:, :], tile_row[:, :], float(NT - 1), None, ALU.min))
            twice = tile_row[:, :].unsqueeze(1).to_broadcast([E1, 2, CAP])
            dve.tensor_copy(tile_rows[:, 0], twice)
            dve.tensor_scalar(tile_rows[:, 1], twice, slot_f[0:E1, 1:2], None, ALU.add).then_inc(S["tr4"], 1)
            dve.wait_ge(S["tr4"], 2)
            for h in range(2):
                dve.tensor_scalar(tile_at[SLOTS[h], :], bank[0][SLOTS[h], h:E1:2], float(P), None, ALU.mult)
                ins = dve.tensor_copy(row_at[SLOTS[h], :], bank[0][SLOTS[h], E1 + h:2 * E1:2])
            ins.then_inc(S["f4"], 1)
            dve.wait_ge(S["f4"], 1)

            def keep_slots(g):
                for h in range(2):
                    ins = dve.tensor_copy(aidx[:, g.half, h, :], sidx[SLOTS[h], g.half, :])
                ins.then_inc(S["aidx_done"], 1)

            def slots(g, prior):
                u = g.half
                at = steps4
                if prior:
                    dve.wait_ge(S["aidx_done"], g.b - 1)
                dve.wait_ge(S[f"cg_in{u}"], g.pair * (16 * GH) + 16 * GH)
                dve.tensor_scalar(below[:, :, :], cg[:, u], slot_f[:, 0:1], None, ALU.is_le).then_inc(S["sel"], 1)
                dve.wait_ge(S["sel"], g.b * 4 + (at + 1))
                dve.tensor_reduce(tok[:, 0, :], below[:, :, :], AX.X, ALU.add).then_inc(S["sel"], 1)
                dve.wait_ge(S["sel"], g.b * 4 + (at + 2))
                dve.tensor_tensor(tok[:, 1, :], tok[:, 0, :], tile_at[:, bass.ds(g.b * GH, GH)], ALU.add).then_inc(S["sel"], 1)
                dve.wait_ge(S["sel"], g.b * 4 + (at + 3))
                dve.tensor_scalar(dump[:, :], tok[:, 1, :], float(B * T), slot_f[:, 0:1], ALU.is_ge, ALU.mult).then_inc(S["sel"], 1)
                dve.wait_ge(S["sel"], g.b * 4 + (at + 4))
                dve.tensor_tensor(sidx[:, u, :], tok[:, 1, :], dump[:, :], ALU.add).then_inc(S["sidx_done"], 1)

            def experts(g, prior):
                u = g.half
                if prior:
                    dve.wait_ge(S["added"], (g.b - 1) * (16 * GE))
                dve.wait_ge(S[f"xg_in{u}"], g.pair * (16 * GH) + 16 * GH)
                dve.tensor_copy(wblk[:, u, :].rearrange("p (e k) -> p e k", k=GE), xg[:, u, :, bass.ds(g.b * GE + C, GE)]).then_inc(S["wblk_sb"], 1)
                dve.wait_ge(S["the_sb"], g.b + 1)
                dve.scalar_tensor_tensor(ae[:, :], the[:, :], 1.0, bank[2][0:IE, :], ALU.add, ALU.mult).then_inc(S["ae1"], 1)
                dve.wait_ge(S["ae1"], g.b + 1)
                dve.tensor_tensor(ae[:, :], ae[:, :], bank[3][0:IE, :], ALU.mult).then_inc(S["ae_sb"], 1)
                dve.wait_ge(S["oe_ps"], g.b + 1)
                dve.wait_ge(S["wblk_sb"], g.b + 1)
                for h in range(2):
                    diag = wblk[SLOTS[h], u, h:h + (GH - 1) * (GE + 2) + 1:GE + 2]
                    ins = dve.scalar_tensor_tensor(yo[SLOTS[h], u], bankS[SLOTS[h], 0, :].rearrange("p (j c) -> p j c", c=C), 0.5,
                                                   diag.unsqueeze(2).to_broadcast([CAP, GH, C]), ALU.mult, ALU.mult)
                ins.then_inc(S["yo_sb"], 1)

            def step4(n1, n3, prior=True):
                experts(n1, prior)
                keep_slots(n1)
                if n3:
                    slots(n3, True)

            slots(Batch(0, 0), False)
            slots(Batch(0, 1), False)
            step4(Batch(0, 0), Batch(1, 0), False)
            step4(Batch(0, 1), Batch(1, 1), False)
            with dve.Fori(0, NG // 2 - 2) as i:
                step4(Batch(i + 1, 0), Batch(i + 2, 0))
                step4(Batch(i + 1, 1), Batch(i + 2, 1))
            step4(Batch(NG // 2 - 1, 0), None)
            step4(Batch(NG // 2 - 1, 1), None)

        @block.scalar
        def _(act):
            def xnt(n):
                act.wait_ge(S["xnT_ps"], n.b + 1)
                act.copy(xnT[:, n.half, :], bankA[:, 0:T]).then_inc(S["xnT_sb"], 1)

            def qevac(n, r):
                act.wait_ge(S["q_ps"], n.b * 4 + (r + 1))
                for k in range(2):
                    j = 2 * r + k
                    act.activation(qT[:, n.half, j, :], bankA[:, k * T:(k + 1) * T], ACT.Identity,
                                   bias=bd[:, j:j + 1]).then_inc(S["q_sb"], 1)

            def mt(n):
                act.wait_ge(S["mT_ps"], n.b + 1)
                act.copy(mT[:, n.half, :], bankA[0:H, 0:T]).then_inc(S["mT_sb"], 1)

            def probs(b, g):
                for e in range(2):
                    h = 2 * g + e
                    act.wait_ge(S["st_ps"], b.b * H + (h + 1))
                    if h >= 4:
                        act.wait_ge(S["av_done"], b.b * H + (h - 3))
                    act.activation(pT[:, h % 4, :], bankT[:, e, 0:384], ACT.Exp, scale=SCALE0).then_inc(S["exp_done"], 1)

            def step(b, n):
                for g in range(PAIRS):
                    probs(b, g)
                    if n and g == 0:
                        xnt(n)
                    if n and 1 <= g <= 4:
                        qevac(n, g - 1)
                if n:
                    mt(n)

            act.wait_ge(S["w_in"], 16 * NW)
            first = Batch(0, 0)
            xnt(first)
            for r in range(4):
                qevac(first, r)
            mt(first)
            with act.Fori(0, LOOP) as i:
                step(Batch(i, 0), Batch(i, 1))
                step(Batch(i, 1), Batch(i + 1, 0))
            step(Batch(LOOP, 0), Batch(LOOP, 1))
            step(Batch(LOOP, 1), None)

            act.wait_ge(S["te_go"], 1)
            act.activation(lgs0[:, :, :], lgs0[:, :, :], ACT.Exp).then_inc(S["ex0"], 1)

            def turned(j, q):
                act.wait_ge(S["xsT_ps"], j + 1)
                act.copy(xsT[:, q % 2, :], bank[q % 2][:, 0:P]).then_inc(S["xsT_sb"], 1)

            def hidden(j, q):
                u = q % 2
                act.wait_ge(S["h_ps"], j + 1)
                for k in range(KF // 2):
                    ins = act.activation(hT[:, u, k, :], hbank[u][:, 0, k * P:(k + 1) * P], ACT.Relu,
                                         bias=w1b[:, u, F0 + k:F0 + k + 1])
                ins.then_inc(S["h_act"], 1)

            def tile_step(j, q, left):
                if left > 2:
                    turned(j + 2, q + 2)
                if left > 1:
                    hidden(j + 1, q + 1)

            turned(0, 0)
            turned(1, 1)
            hidden(0, 0)
            with act.Fori(0, TILES // 4 - 1) as i:
                for q in range(4):
                    tile_step(i * 4 + q, q, 8)
            for q in range(4):
                tile_step(TILES - 4 + q, q, 4 - q)

            SCALE1 = float((C // H) ** -0.5)

            def soft(b, g):
                act.wait_ge(S["sub_done"], b.b * 4 + (g + 1))
                act.activation(pr[:, g % 2, :], pr[:, g % 2, :], ACT.Exp, scale=SCALE1).then_inc(S["exp2"], 1)

            def xt1(n):
                act.wait_ge(S["tT_ps"], n.b + 1)
                act.copy(xT1[:, n.half, :], bank[0][:, 0:T]).then_inc(S["tT_sb"], 1)
                act.copy(xr[:, n.half], bank[0][:, 0:T].rearrange("p (n q) -> p n q", q=W).unsqueeze(2).to_broadcast([P, NB, 4, W])).then_inc(S["tT_sb"], 1)

            def xp1(n):
                act.wait_ge(S["xp_done"], n.b + 1)
                act.copy(xpr[:, n.half], xp[:, n.half, :].rearrange("p (n q) -> p n q", q=W).unsqueeze(2).to_broadcast([P, 2, 4, W])).then_inc(S["xpr_sb"], 1)

            def spread(dst, src):
                for h in range(4):
                    act.activation(dst[:, :, h, :], src.rearrange("p (n q) -> p n q", q=W), ACT.Copy, scale=headcol[:, h:h + 1])

            def keys(n):
                u = n.half
                act.wait_ge(S["qk_ps"], n.b + 1)
                act.copy(qs[:, u, :], bank[1][:, 0:T])
                spread(qx[:, u], bank[1][:, 0:T])
                for g in range(4):
                    q = slice(W * g, W * g + W)
                    ins = act.copy(km[q, u, g, W:W + T], bank[1][q, T:2 * T])
                ins.then_inc(S["kt_sb"], 1)

            def count(n):
                u = n.half
                act.wait_ge(S["cnt_sb"], n.b + 1)
                act.wait_ge(S["cnt_ps"], n.b + 1)
                act.activation(carry[:, u, :], bank[3][0:E1, T - 1:T], ACT.Identity, bias=carry[:, 1 - u, :])
                act.activation(cnt_all[:, bass.ds(n.b * T, T)], bank[3][0:E1, 0:T], ACT.Identity, bias=carry[:, 1 - u, :]).then_inc(S["cnt_sb"], 1)

            def latent_keys(n):
                act.wait_ge(S["g_sb"], n.b + 1)
                spread(gqx[:, n.half], bank[2][:, 0:T])
                for g in range(2):
                    q = slice(W * g, W * g + W)
                    ins = act.copy(gkm[q, n.half, g, :], bank[2][q, 256:256 + NL])
                ins.then_inc(S["gk_sb"], 1)

            def route(n):
                act.wait_ge(S["ex_in"], n.b + 1)
                act.activation(exl[:, :, :], shl[:, :, :], ACT.Exp)
                act.activation(tsg[:, :], lg1[:, :, E1], ACT.Tanh, scale=0.5).then_inc(S["ex_done"], 1)

            def shared(b):
                act.wait_ge(S["shg_ps"], b.b + 1)
                act.activation(tsh[:, :], bank[0][:, :], ACT.Tanh, scale=0.5).then_inc(S["tanh_sh"], 1)

            def gate(b):
                act.wait_ge(S["gate_ps"], b.b + 1)
                act.activation(tg[:, :, :].rearrange("p k t -> p (k t)"), bankS[:, 0, :], ACT.Tanh, scale=0.5).then_inc(S["gate_sb"], 1)

            def step1(b, n, m):
                if b:
                    soft(b, 0)
                if n:
                    keys(n)
                    xp1(n)
                if b:
                    soft(b, 1)
                    soft(b, 2)
                if n:
                    route(n)
                    latent_keys(n)
                    count(n)
                if b:
                    gate(b)
                    soft(b, 3)
                    shared(b)
                if m:
                    xt1(m)

            act.sem_inc(S["gate_sb"], 1)
            act.wait_ge(S["wprep"], 1)
            xt1(Batch(0, 0))
            step1(None, Batch(0, 0), Batch(0, 1))
            with act.Fori(0, LOOP) as i:
                step1(Batch(i, 0), Batch(i, 1), Batch(i + 1, 0))
                step1(Batch(i, 1), Batch(i + 1, 0), Batch(i + 1, 1))
            step1(Batch(LOOP, 0), Batch(LOOP, 1), None)
            step1(Batch(LOOP, 1), None, None)
            def experts(g):
                u = g.half
                act.wait_ge(S["xgT_ps"], g.b + 1)
                act.copy(xgT[:, u, :], bank[1][:, :]).then_inc(S["xgT_sb"], 1)
                act.wait_ge(S["gu_ps"], g.b + 1)
                act.activation(the[:, :], bank[2][0:IE, :], ACT.Tanh, scale=0.5).then_inc(S["the_sb"], 1)

            with act.Fori(0, NG // 2) as i:
                experts(Batch(i, 0))
                experts(Batch(i, 1))

        @block.tensor
        def _(pe):
            def xnt(n):
                pe.wait_ge(S["xn_done"], n.b + 1)
                for t in range(2):
                    ins = pe.transpose(bankA[:, t * P:(t + 1) * P], xn[:, n.half, t, :], ident[:, :])
                ins.then_inc(S["xnT_ps"], 1)

            def kv(n, prior):
                u = n.half
                pe.wait_ge(S["xnT_sb"], n.b + 1)
                if prior:
                    pe.wait_ge(S["xa_done"], n.b)
                pe.matmul(bankB[:, 0:T], lw[:, :, :].rearrange("p e l -> p (e l)"), xnT[:, u, :], start=True, stop=True)
                for t in range(2):
                    tok = xnT[:, u, t * P:(t + 1) * P]
                    o = bankB[:, 256 + t * LR:256 + (t + 1) * LR]
                    pe.matmul(o, tok, lwr[:, :], start=True, stop=False)
                    ins = pe.matmul(o, ones[:, :], lbrow[:, :], start=False, stop=True)
                ins.then_inc(S["kv_ps"], 1)

            def qproj(n, r):
                if r >= 1:
                    pe.wait_ge(S["q_sb"], n.b * PAIRS + 2 * r)
                for k in range(2):
                    ins = pe.matmul(bankA[:, k * T:(k + 1) * T], wd[:, 2 * r + k, :, :].rearrange("p e l -> p (e l)"),
                                    xnT[:, n.half, :], start=True, stop=True)
                ins.then_inc(S["q_ps"], 1)

            def diagonal(s, mask):
                return pe.matmul(s[:, 0:384].rearrange("p (k t) -> p k t", t=P)[:, 0:3:2, :], identb[:, :],
                          mask[:, :].unsqueeze(1).to_broadcast([P, 2, P]), start=False, stop=True)

            def smax(n, g):
                u = n.half
                pe.wait_ge(S["q_sb"], n.b * PAIRS + (g + 1))
                pe.wait_ge(S["qb_sb"], n.b * PAIRS + (g + 1))
                if g == 0:
                    pe.wait_ge(S["kb_sb"], n.b + 1)
                pe.wait_ge(S["red_done"], n.b * PAIRS + (g + 1))
                for e in range(2):
                    s = bankS[:, e, :]
                    pe.matmul(s[:, 0:128], qb[:, g, 0:P], kb[:, e, 0:P], start=True, stop=False)
                    pe.matmul(s[:, 128:384], qb[:, g, P:T], kb[:, e, :], start=False, stop=False)
                    ins = diagonal(s, maskq)
                ins.then_inc(S["s_ps"], 1)

            def mt(n):
                pe.wait_ge(S["red_done"], n.b * PAIRS + (PAIRS + 1))
                pe.wait_ge(S["q_sb"], n.b * PAIRS + PAIRS)
                passed(pe)
                for t in range(2):
                    ins = pe.transpose(bankA[0:H, t * P:(t + 1) * P], mneg[:, n.half, t].rearrange("p e j -> p (e j)"), ident[:, :])
                ins.then_inc(S["mT_ps"], 1)

            def st(b, g):
                u = b.half
                if g == 0:
                    pe.wait_ge(S[f"m_in{u}"], b.pair * 32 + 32)
                for e in range(2):
                    h = 2 * g + e
                    if h >= 2:
                        pe.wait_ge(S["exp_done"], b.b * H + (h - 1))
                    s = bankT[:, e, :]
                    for k, cols in ((0, slice(0, 256)), (1, slice(256, 384))):
                        pe.matmul(s[:, cols], kT[:, u, e, k * P:(k + 1) * P], qT[:, u, g, k * P:T], start=(k == 0), stop=False)
                    ins = diagonal(s, maskk)
                    ins.then_inc(S["st_ps"], 1)

            def av(b, h):
                u, k, j = b.half, (h + 2) // 3, (h - 1) % 3 if h else 0
                y = bankY[k % 2]
                if h == 0:
                    pe.wait_ge(S["xa_done"], b.b + 1)
                if j == 0:
                    pe.wait_ge(S["y_sb"], b.b * TRIPLES + (k + 1))
                pe.wait_ge(S["exp_done"], b.b * H + (h + 1))
                p = pT[:, h % 4, :]
                pe.matmul(y[:, 0:T], vaug[:, u, 0, j, :], p[:, 0:256], start=(j == 0), stop=False)
                pe.matmul(y[:, P:T], vaug[:, u, 1, j, :], p[:, 256:384], start=False, stop=(j == 2 or h == 0)).then_inc(S["av_done"], 1)

            def spread(b, k):
                dens = slice(DEN, DEN + heads_of(k))
                pe.wait_ge(S["rz_done"], b.b * TRIPLES + (k + 1))
                pe.matmul(bankY[k % 2][:, T:2 * T], headsel[dens, :], rz[dens, k % 2, :], start=True, stop=True).then_inc(S["rz_ps"], 1)

            def outp(b, ks):
                for t in range(2):
                    o = (bankB, bankY[0])[t][:, 0:C]
                    for k in ks:
                        if k == 0:
                            pe.matmul(o, ones[:, :], ob[:, :], start=True, stop=False)
                        if t == 0:
                            pe.wait_ge(S["y_sb"], b.b * TRIPLES + (k + 3))
                        elif k == 0:
                            pe.wait_ge(S["y_sb"], b.b * TRIPLES + (TRIPLES + 1))
                        ins = pe.matmul(o, zT[0:ROWS, b.half, k, t * P:(t + 1) * P], ow[0:ROWS, k, :], start=False, stop=(k == TRIPLES - 1))
                if ks[-1] == TRIPLES - 1:
                    ins.then_inc(S["out_ps"], 1)

            def step(b, n):
                for g in range(PAIRS + 1):
                    if 1 <= g < PAIRS:
                        st(b, g)
                    if n and g == 0:
                        xnt(n)
                    if n and g == 1:
                        kv(n, True)
                    for k in SPREAD[g] if g < PAIRS else ():
                        spread(b, k)
                    for r in MAX_BEFORE[g] if n else ():
                        smax(n, r)
                    if g >= 1:
                        av(b, 2 * g - 2)
                        av(b, 2 * g - 1)
                    for k in SPREAD[g] if g == PAIRS else ():
                        spread(b, k)
                    if n and 1 <= g <= 4:
                        qproj(n, g - 1)
                    for r in MAX_AFTER[g] if n else ():
                        smax(n, r)
                if n:
                    mt(n)
                outp(b, range(TRIPLES - 1))
                spread(b, TRIPLES - 1)
                if n:
                    st(n, 0)
                outp(b, (TRIPLES - 1,))

            pe.wait_ge(S["w_in"], 16 * NW)
            pe.wait_ge(S["consts"], 1)
            first = Batch(0, 0)
            xnt(first)
            kv(first, False)
            for r in range(4):
                qproj(first, r)
            for g in range(PAIRS):
                smax(first, g)
            mt(first)
            st(first, 0)
            with pe.Fori(0, LOOP) as i:
                step(Batch(i, 0), Batch(i, 1))
                step(Batch(i, 1), Batch(i + 1, 0))
            step(Batch(LOOP, 0), Batch(LOOP, 1))
            step(Batch(LOOP, 1), None)

            pe.wait_ge(S["te_go"], 1)
            pe.wait_ge(S["xa_done"], B + 1)
            flat = oh0[:, :, :].rearrange("p n e -> p (n e)")
            pe.matmul(bankA[:, :], strict[:, :], flat, start=True, stop=True)
            pe.matmul(bankB[:, :], onesb[:, :], flat, start=True, stop=True).then_inc(S["rk_ps"], 1)
            pe.wait_ge(S["te_done"], 1)

            def turn_in(i, q):
                i, q = i + q // 4, q % 4
                if q % 2 == 0:
                    pe.wait_ge(S[f"xs_in{q // 2}"], i * 16 + 16)
                passed(pe)
                pe.transpose(bank[q % 2][:, 0:P], xsb[:, q // 2, q % 2, :], ident[:, :]).then_inc(S["xsT_ps"], 1)

            def hidden(j, q):
                u = q % 2
                pe.wait_ge(S["w1_sb"], j + 1)
                pe.wait_ge(S["xsT_sb"], j + 1)
                for k in range(KF):
                    c = (k % 2) * P
                    ins = pe.matmul(hbank[u][:, k // 2, c:c + P], w1b[:, u, k * P:(k + 1) * P], xsT[:, u, :], start=True, stop=True)
                ins.then_inc(S["h_ps"], 1)

            def result(j, q):
                u = q % 2
                e = pe.value_load(te_i[0:1, bass.ds(j, 1)], min_val=0, max_val=E0 - 1)
                pe.wait_ge(S["h_act"], j + 1)
                pe.wait_ge(S["h_dve"], j + 1)
                pe.wait_ge(S["yt_sb"], j + 1)
                for k in range(KF):
                    pe.matmul(bankY[u][:, 0:C], hT[:, u, k, :],
                              wall[:, bass.ds(e, 1), F0 + KF + k * C:F0 + KF + (k + 1) * C].rearrange("p a c -> p (a c)"),
                              start=(k == 0), stop=False)
                pe.matmul(bankY[u][:, 0:C], ones[:, :], b2row[:, bass.ds(e, 1), :].rearrange("p a c -> p (a c)"),
                          start=False, stop=True).then_inc(S["yt_ps"], 1)

            def tile_step(i, q, left):
                j = i * 4 + q
                if left > 2:
                    turn_in(i, q + 2)
                if left > 1:
                    hidden(j + 1, q + 1)
                result(j, q)

            turn_in(0, 0)
            turn_in(0, 1)
            hidden(0, 0)
            with pe.Fori(0, TILES // 4 - 1) as i:
                for q in range(4):
                    tile_step(i, q, 8)
            for q in range(4):
                tile_step(TILES // 4 - 1, q, 4 - q)

            def scores(b, g):
                u = b.half
                if g == 0:
                    pe.wait_ge(S["kt_sb"], b.b + 1)
                    pe.wait_ge(S["gk_sb"], b.b + 1)
                else:
                    pe.wait_ge(S["s2_ps"], b.b * 4 + g)
                if g >= 2:
                    pe.wait_ge(S["sub_done"], b.b * 4 + (g - 1))
                for k in range(2):
                    n = 2 * g + k
                    s = (bankS, bankT)[g % 2][:, k, :]
                    pe.matmul(s[:, 0:4 * NL], identb[:, :], maskl[:, min(n, 1), :].unsqueeze(1).to_broadcast([P, 4, NL]), start=True, stop=False)
                    pe.matmul(s[:, 0:4 * NL], qx[:, u, n].rearrange("p h q -> p (h q)"), km[:, u, :, n * W:n * W + 2 * W], start=False, stop=True)
                    pe.matmul(s[:, 4 * NL:6 * NL], identb[:, :], maskr[:, n, :].unsqueeze(1).to_broadcast([P, 2, NL]), start=True, stop=False)
                    ins = pe.matmul(s[:, 4 * NL:6 * NL], gqx[:, u, n].rearrange("p h q -> p (h q)"), gkm[:, u, :, :], start=False, stop=True)
                ins.then_inc(S["s2_ps"], 1)

            def xt1(n, prior):
                pe.wait_ge(S["xn1_done"], n.b + 1)
                if prior:
                    pe.wait_ge(S["sh1_done"], n.b - 1)
                passed(pe)
                for t in range(2):
                    ins = pe.transpose(bank[0][:, t * P:(t + 1) * P], tab[:, n.half, t, 0:C], ident[:, :])
                ins.then_inc(S["tT_ps"], 1)

            def qk(n, prior):
                u = n.half
                pe.wait_ge(S["tT_sb"], n.b * 2 + 2)
                if prior:
                    pe.wait_ge(S["r1_done"], n.b)
                for k in range(2):
                    ins = pe.matmul(bank[1][:, k * T:(k + 1) * T], wqk[:, k, :], xT1[:, u, :], start=True, stop=True)
                ins.then_inc(S["qk_ps"], 1)
                for t in range(2):
                    c = 256 + t * (E1 + 1)
                    ins = pe.matmul(bank[0][:, c:c + E1 + 1], xT1[:, u, t * P:(t + 1) * P], gw[:, :], start=True, stop=True)
                ins.then_inc(S["rt_ps"], 1)

            def latents(n, prior):
                u = n.half
                if prior:
                    pe.wait_ge(S["res_done"], n.b)
                pe.wait_ge(S["xpr_sb"], n.b + 1)
                pe.matmul(bank[2][:, 0:T], wgqk[:, 0, :], xT1[:, u, :], start=True, stop=True)
                pe.matmul(bank[2][:, T:T + NL], wgqk[:, 1, :], xp[:, u, :], start=True, stop=True)
                for k in range(2):
                    ins = pe.matmul(bank[2][:, 320 + k * DL:320 + (k + 1) * DL], xpr[:, u, k].rearrange("p r q -> p (r q)"), wgv[:, :], start=True, stop=True)
                ins.then_inc(S["g_ps"], 1)

            def count(n):
                pe.wait_ge(S["M_done"], n.b + 1)
                pe.matmul(bank[3][0:E1, 0:T], mb[:, n.half, 0, :], upto[:, :, :].rearrange("p k t -> p (k t)"), start=True, stop=False)
                pe.matmul(bank[3][0:E1, P:T], mb[:, n.half, 1, :], upto[:, 0, :], start=False, stop=True).then_inc(S["cnt_ps"], 1)

            def values(n):
                u = n.half
                pe.wait_ge(S["kt_sb"], n.b + 1)
                pe.wait_ge(S["rt_sb"], n.b + 1)
                for k in range(2):
                    for j in range(4):
                        ins = pe.matmul(bank[k][:, j * C:(j + 1) * C], xr[:, u, 4 * k + j].rearrange("p r q -> p (r q)"), wv[:, :], start=True, stop=True)
                    ins.then_inc(S["v_ps"], 1)

            def shared_up(b, last):
                u = b.half
                pe.wait_ge(S["v_sb"], b.b * 2 + (2 if last else 4))
                for k in range(2):
                    for j in range(2):
                        c = (2 * k + j) * P
                        ins = pe.matmul(bank[k][:, j * T:(j + 1) * T], sgu[:, c:c + P], xT1[:, u, :], start=True, stop=True)
                    ins.then_inc(S[("shg_ps", "shu_ps")[k]], 1)

            def attend(b, g, last):
                u = b.half
                if g == 0:
                    pe.wait_ge(S["gk_sb"], b.b + (1 if last else 2))
                    pe.wait_ge(S["cnt_sb"], b.b + (2 if last else 3))
                pe.wait_ge(S["tr_done"], b.b * 4 + (g + 1))
                cols, dens = slice(2 * W * g, 2 * W * (g + 1)), slice(T + 2 * W * g, T + 2 * W * (g + 1))
                for h in range(4):
                    q = slice(W * h, W * h + W)
                    if h < 2:
                        for k in range(2):
                            pe.matmul(bank[3][q, cols], gvx[:, u, k, q], pt[:, 2 * g:2 * g + 2, 4 + h, k, :], start=(k == 0), stop=(k == 1))
                        for k in range(2):
                            pe.matmul(bank[3][q, dens], quadcol[:, 0:W], pt[:, 2 * g:2 * g + 2, 4 + h, k, :], start=(k == 0), stop=(k == 1))
                    for n in range(2 * g, 2 * g + 2):
                        o = bank[2][q, n * W:(n + 1) * W]
                        if n:
                            pe.matmul(o, vx[:, u, n - 1, q], pt[:, n, h, 0, :], start=True, stop=False)
                        pe.matmul(o, vx[:, u, n, q], pt[:, n, h, 1, :], start=(n == 0), stop=True)
                    for k in range(2):
                        ins = pe.matmul(bank[2][q, dens], quadcol[:, 0:W], pt[:, 2 * g:2 * g + 2, h, k, :], start=(k == 0), stop=(k == 1))
                if g == 3:
                    ins.then_inc(S["av_ps"], 1)

            def gate(b):
                u = b.half
                pe.wait_ge(S["sub_done"], b.b * 4 + 3)
                for k in range(2):
                    ins = pe.matmul(bankS[:, 0, k * T:(k + 1) * T], gates[:, k, :], qs[:, u, :], start=True, stop=True)
                ins.then_inc(S["gate_ps"], 1)

            def finish(b):
                pe.wait_ge(S["remn_done"], b.b + 1)
                pe.matmul(bank[3][:, 0:T], wro[:, :], remn[:, :], start=True, stop=True).then_inc(S["rem2_ps"], 1)
                pe.wait_ge(S["sh_sb"], b.b + 1)
                for t in range(2):
                    for k in range(2):
                        ins = pe.matmul(bank[1][:, t * C:(t + 1) * C], shT[:, k, t * P:(t + 1) * P], sdw[:, k, :], start=(k == 0), stop=(k == 1))
                ins.then_inc(S["shd_ps"], 1)

            def project(b):
                pe.wait_ge(S["aT_done"], b.b + 1)
                for t in range(2):
                    ins = pe.matmul(bank[2][:, t * C:(t + 1) * C], aT[:, t * P:(t + 1) * P], wo1[:, :], start=True, stop=True)
                ins.then_inc(S["ao_ps"], 1)

            def step1(b, n, m):
                if n:
                    qk(n, b is not None)
                if b:
                    scores(b, 2)
                if n:
                    latents(n, b is not None)
                if b:
                    scores(b, 3)
                if n:
                    values(n)
                    count(n)
                if b:
                    gate(b)
                    attend(b, 0, n is None)
                    attend(b, 1, n is None)
                    shared_up(b, n is None)
                    attend(b, 2, n is None)
                    attend(b, 3, n is None)
                if n:
                    if b:
                        pe.wait_ge(S["gate_sb"], n.b + 1)
                    scores(n, 0)
                    scores(n, 1)
                if b:
                    finish(b)
                if m:
                    if not b:
                        pe.wait_ge(S["v_sb"], 2)
                    xt1(m, b is not None)
                if b:
                    project(b)

            pe.wait_ge(S["wprep"], 1)
            xt1(Batch(0, 0), False)
            step1(None, Batch(0, 0), Batch(0, 1))
            with pe.Fori(0, LOOP) as i:
                step1(Batch(i, 0), Batch(i, 1), Batch(i + 1, 0))
                step1(Batch(i, 1), Batch(i + 1, 0), Batch(i + 1, 1))
            step1(Batch(LOOP, 0), Batch(LOOP, 1), None)
            step1(Batch(LOOP, 1), None, None)
            pe.wait_ge(S["tr4"], 1)
            for k in range(2):
                ins = pe.transpose(bank[0][:, k * E1:(k + 1) * E1], tile_rows[:, k].rearrange("e h c -> e (h c)"), ident[0:E1, 0:E1])
            ins.then_inc(S["tr4"], 1)

            def experts(g):
                u = g.half
                pe.wait_ge(S[f"xg_in{u}"], g.pair * (16 * GH) + 16 * GH)
                passed(pe)
                for j in range(GH):
                    ins = pe.transpose(bank[1][:, j * P:(j + 1) * P], xg[:, u, j, 0:C], ident[:, :])
                ins.then_inc(S["xgT_ps"], 1)
                pe.wait_ge(S["xgT_sb"], g.b + 1)
                pe.wait_ge(S[f"we_in{u}"], g.pair * 32 + 32)
                for k in range(2):
                    for e in range(GE):
                        ins = pe.matmul(bank[2 + k][0:IE, e * CAP:(e + 1) * CAP], wge[:, u, e, k * IE:(k + 1) * IE],
                                        xgT[:, u, e * CAP:(e + 1) * CAP], start=True, stop=True)
                ins.then_inc(S["gu_ps"], 1)
                pe.wait_ge(S["ae_sb"], g.b + 1)
                passed(pe)
                for e in range(GE):
                    ins = pe.matmul(bankS[SLOTS[e % 2], 0, (e // 2) * C:(e // 2 + 1) * C], ae[:, e * CAP:(e + 1) * CAP],
                                    wde[:, u, e, :], start=True, stop=True)
                ins.then_inc(S["oe_ps"], 1)

            with pe.Fori(0, NG // 2) as i:
                experts(Batch(i, 0))
                experts(Batch(i, 1))


_INS = ['L0_attn_x', 'L0_attn_latent_w', 'L0_attn_latent_b', 'L0_attn_Wd_w', 'L0_attn_Wd_b', 'L0_attn_out_w',
        'L0_attn_out_b', 'L0_ffn_Wr', 'L0_ffn_br', 'L0_ffn_W1', 'L0_ffn_b1', 'L0_ffn_W2', 'L0_ffn_b2', 'L1_attn_wq',
        'L1_attn_wk', 'L1_attn_wv', 'L1_attn_wgq', 'L1_attn_wgk', 'L1_attn_wgv', 'L1_attn_r_out_w',
        'L1_attn_gate_local_w', 'L1_attn_gate_remote_w', 'L1_attn_w_out', 'L1_ffn_gate_w', 'L1_ffn_shared_gate_w',
        'L1_ffn_shared_gate_up_w', 'L1_ffn_shared_down_w', 'L1_ffn_expert_gate_up_w', 'L1_ffn_expert_down_w']


def kernel(**inputs):
    import numpy as _np
    import concourse.bacc as _bacc
    from concourse import mybir as _mybir
    from concourse.bass_utils import run_bass_kernel_spmd as _run

    nc = _bacc.Bacc("TRN2", target_bir_lowering=False, num_devices=1)
    arrays, aps = {}, {}
    for name in _INS:
        v = _np.ascontiguousarray(inputs[name])
        arrays[f"in_{name}"] = v
        aps[name] = nc.dram_tensor(f"in_{name}", v.shape, _mybir.dt.from_np(v.dtype), kind="ExternalInput").ap()
    shape = inputs["L0_attn_x"].shape
    out = nc.dram_tensor("out_x", shape, _mybir.dt.float32, kind="ExternalOutput").ap()
    program(nc, aps, out)
    r = _run(nc, [arrays], core_ids=[0])
    return r.results[0]["out_x"]
```
